# Optimizing a Trainium2 kernel written in Bass

```python
import numpy as np
import jax
import jax.numpy as jnp

def _softmax(x, axis=-1):
    return jax.nn.softmax(x, axis=axis)

def _gelu(x):
    return jax.nn.gelu(x, approximate=True)

def _silu(x):
    return jax.nn.silu(x)

def _sigmoid(x):
    return jax.nn.sigmoid(x)

def _layernorm(x, axis=-1, eps=1e-05):
    m = jnp.mean(x, axis=axis, keepdims=True)
    v = jnp.var(x, axis=axis, keepdims=True)
    return (x - m) / jnp.sqrt(v + eps)

def _scatter_add(tgt, idx, src, axis=0):
    return tgt.at[idx].add(src)

def _segment_sum(src, seg, n):
    return jax.ops.segment_sum(src, seg, n)
kernel_name = 'mk_adj_preln_d4_adj_r2_ff6ac5'

def setup_inputs(seed: int=0):
    np.random.seed(seed)
    _w = jnp.asarray

    def _rec_inputs():
        import jax
        import jax.numpy as jnp
        _gk = jax.random.key(seed)
        x = -0.0005207 + 1.001 * jax.random.normal(jax.random.fold_in(_gk, 1), (8, 1024, 128), jnp.float32)
        _a = jax.random.bernoulli(jax.random.fold_in(_gk, 2), 0.00390625, (1024, 1024))
        _a = jnp.logical_or(_a, jnp.swapaxes(_a, -1, -2))
        _a = jnp.logical_or(_a, jnp.eye(1024, dtype=bool))
        adj = _a.astype(jnp.int32)
        return (x, adj)
    x, adj = _rec_inputs()

    def _L0_gnn_setup():
        import jax, jax.numpy as jnp
        import numpy as np
        import math
        CHUNK = 128
        NUM_HEADS = 4
        EPS = 1e-05
        key = jax.random.key(seed)
        ks = jax.random.split(key, 12)
        B, N, F = (4, 1024, 128)
        x = jax.random.normal(ks[0], (B, N, F), dtype=jnp.float32)
        adj_matrix = jax.random.randint(ks[1], (N, N), 0, 2, dtype=jnp.int32)
        s = 1.0 / math.sqrt(F)
        Wq = jax.random.normal(ks[2], (F, F), dtype=jnp.float32) * s
        bq = jnp.zeros((F,), dtype=jnp.float32)
        Wk = jax.random.normal(ks[3], (F, F), dtype=jnp.float32) * s
        bk = jnp.zeros((F,), dtype=jnp.float32)
        Wv = jax.random.normal(ks[4], (F, F), dtype=jnp.float32) * s
        bv = jnp.zeros((F,), dtype=jnp.float32)
        Wo = jax.random.normal(ks[5], (F, F), dtype=jnp.float32) * s
        bo = jnp.zeros((F,), dtype=jnp.float32)
        gamma = jnp.ones((F,), dtype=jnp.float32)
        beta = jnp.zeros((F,), dtype=jnp.float32)
        return {'x': x, 'adj_matrix': adj_matrix, 'Wq': Wq, 'bq': bq, 'Wk': Wk, 'bk': bk, 'Wv': Wv, 'bv': bv, 'Wo': Wo, 'bo': bo, 'gamma': gamma, 'beta': beta}
    _L0_gnn_all = _L0_gnn_setup()
    _L0_gnn_in = {k: v for k, v in _L0_gnn_all.items() if k in ('Wq', 'bq', 'Wk', 'bk', 'Wv', 'bv', 'Wo', 'bo', 'gamma', 'beta')}
    del _L0_gnn_all

    def _L1_gnn_setup():
        import jax, jax.numpy as jnp
        import numpy as np
        ALPHA = 0.2
        key = jax.random.key(seed)
        k1, k2, k3, k4 = jax.random.split(key, 4)
        B, N, Din, Dout = (8, 1024, 128, 128)
        h = jax.random.normal(k1, (B, N, Din), dtype=jnp.float32)
        adj = jax.random.randint(k2, (N, N), 0, 2, dtype=jnp.int32)
        w_bound = float(np.sqrt(6.0 / (Din + Dout)))
        a_bound = float(np.sqrt(6.0 / (2 * Dout + 1)))
        W = jax.random.uniform(k3, (Din, Dout), dtype=jnp.float32, minval=-w_bound, maxval=w_bound)
        a = jax.random.uniform(k4, (2 * Dout, 1), dtype=jnp.float32, minval=-a_bound, maxval=a_bound)
        return {'h': h, 'adj': adj, 'W': W, 'a': a}
    _L1_gnn_all = _L1_gnn_setup()
    _L1_gnn_in = {k: v for k, v in _L1_gnn_all.items() if k in ('W', 'a')}
    del _L1_gnn_all

    def _L2_gnn_setup():
        import jax, jax.numpy as jnp
        import numpy as np
        B, N, F_IN, F_OUT = (8, 1024, 128, 128)
        key = jax.random.key(seed)
        k1, k2, k3, k4 = jax.random.split(key, 4)
        x = jax.random.normal(k1, (B, N, F_IN), dtype=jnp.float32)
        W = jax.random.normal(k2, (F_IN, F_OUT), dtype=jnp.float32) * (1.0 / np.sqrt(F_IN))
        a = jax.random.normal(k3, (2 * F_OUT, 1), dtype=jnp.float32) * (1.0 / np.sqrt(2 * F_OUT))
        adj = jax.random.randint(k4, (N, N), 0, 2, dtype=jnp.int32)
        return {'x': x, 'W': W, 'a': a, 'adj': adj}
    _L2_gnn_all = _L2_gnn_setup()
    _L2_gnn_in = {k: v for k, v in _L2_gnn_all.items() if k in ('W', 'a')}
    del _L2_gnn_all

    def _L3_gnn_setup():
        import jax, jax.numpy as jnp
        import numpy as np
        ALPHA = 0.2
        NEG_INF = -9000000000000000.0

        def _gat(inp, adj_mask, W, a):
            h = jnp.matmul(inp, W)
            F_ = h.shape[-1]
            f1 = jnp.matmul(h, a[:F_, 0])
            f2 = jnp.matmul(h, a[F_:, 0])
            e = jax.nn.leaky_relu(f1[:, :, None] + f2[:, None, :], ALPHA)
            if adj_mask is not None:
                e = jnp.where(adj_mask[None, :, :] > 0, e, NEG_INF)
            att = jax.nn.softmax(e, axis=2)
            h_prime = jnp.einsum('bij,bjf->bif', att, h)
            return jax.nn.elu(h_prime)
        key = jax.random.key(seed)
        ks = jax.random.split(key, 10)
        B, N, Fin, H, O = (16, 512, 128, 256, 128)

        def xavier(k, shape):
            fan_in, fan_out = (shape[0], shape[-1])
            bound = 1.414 * np.sqrt(6.0 / (fan_in + fan_out))
            return jax.random.uniform(k, shape, jnp.float32, -bound, bound)
        return {'x': jax.random.normal(ks[0], (B, N, Fin), jnp.float32), 'adj': jax.random.randint(ks[1], (N, N), 0, 2, jnp.int32), 'mlp1_w': xavier(ks[2], (Fin, H)), 'mlp1_b': jnp.zeros((H,), jnp.float32), 'mlp2_w': xavier(ks[3], (H, O)), 'mlp2_b': jnp.zeros((O,), jnp.float32), 'W_fc': xavier(ks[4], (H, H)), 'a_fc': xavier(ks[5], (2 * H, 1)), 'W_hand': xavier(ks[6], (O, O)), 'a_hand': xavier(ks[7], (2 * O, 1))}
    _L3_gnn_all = _L3_gnn_setup()
    _L3_gnn_in = {k: v for k, v in _L3_gnn_all.items() if k in ('mlp1_w', 'mlp1_b', 'mlp2_w', 'mlp2_b', 'W_fc', 'a_fc', 'W_hand', 'a_hand')}
    del _L3_gnn_all
    return {'x': x, 'adj': adj, 'L0_gnn_Wq': _L0_gnn_in['Wq'], 'L0_gnn_bq': _L0_gnn_in['bq'], 'L0_gnn_Wk': _L0_gnn_in['Wk'], 'L0_gnn_bk': _L0_gnn_in['bk'], 'L0_gnn_Wv': _L0_gnn_in['Wv'], 'L0_gnn_bv': _L0_gnn_in['bv'], 'L0_gnn_Wo': _L0_gnn_in['Wo'], 'L0_gnn_bo': _L0_gnn_in['bo'], 'L0_gnn_gamma': _L0_gnn_in['gamma'], 'L0_gnn_beta': _L0_gnn_in['beta'], 'L1_gnn_W': _L1_gnn_in['W'], 'L1_gnn_a': _L1_gnn_in['a'], 'L2_gnn_W': _L2_gnn_in['W'], 'L2_gnn_a': _L2_gnn_in['a'], 'L3_gnn_mlp1_w': _L3_gnn_in['mlp1_w'], 'L3_gnn_mlp1_b': _L3_gnn_in['mlp1_b'], 'L3_gnn_mlp2_w': _L3_gnn_in['mlp2_w'], 'L3_gnn_mlp2_b': _L3_gnn_in['mlp2_b'], 'L3_gnn_W_fc': _L3_gnn_in['W_fc'], 'L3_gnn_a_fc': _L3_gnn_in['a_fc'], 'L3_gnn_W_hand': _L3_gnn_in['W_hand'], 'L3_gnn_a_hand': _L3_gnn_in['a_hand']}

def reference(x, adj, L0_gnn_Wq, L0_gnn_bq, L0_gnn_Wk, L0_gnn_bk, L0_gnn_Wv, L0_gnn_bv, L0_gnn_Wo, L0_gnn_bo, L0_gnn_gamma, L0_gnn_beta, L1_gnn_W, L1_gnn_a, L2_gnn_W, L2_gnn_a, L3_gnn_mlp1_w, L3_gnn_mlp1_b, L3_gnn_mlp2_w, L3_gnn_mlp2_b, L3_gnn_W_fc, L3_gnn_a_fc, L3_gnn_W_hand, L3_gnn_a_hand):
    import jax
    import jax.numpy as jnp

    def _L0_gnn_ref(x, adj_matrix, Wq, bq, Wk, bk, Wv, bv, Wo, bo, gamma, beta):
        import jax, jax.numpy as jnp
        import numpy as np
        import math
        CHUNK = 128
        NUM_HEADS = 4
        EPS = 1e-05
        B, N, Fin = x.shape
        H = NUM_HEADS
        Dout = Wq.shape[0]
        Dh = Dout // H
        Nc = N // CHUNK
        q = (x @ Wq.T + bq).reshape(B, N, H, Dh).transpose(0, 2, 1, 3)
        k = (x @ Wk.T + bk).reshape(B, N, H, Dh).transpose(0, 2, 1, 3)
        v = (x @ Wv.T + bv).reshape(B, N, H, Dh).transpose(0, 2, 1, 3)
        kc = k.reshape(B, H, Nc, CHUNK, Dh)
        vc = v.reshape(B, H, Nc, CHUNK, Dh)
        scores = jnp.einsum('bhnd,bhjcd->bhnjc', q, kc) / jnp.sqrt(jnp.asarray(Dh, dtype=q.dtype))
        scores = jnp.clip(scores, -10.0, 10.0)
        mask = adj_matrix.reshape(N, Nc, CHUNK)[None, None]
        scores = jnp.where(mask == 0, jnp.asarray(-10.0, scores.dtype), scores)
        attn = jax.nn.softmax(scores, axis=-1)
        ctx = jnp.einsum('bhnjc,bhjcd->bhnd', attn, vc)
        ctx = ctx.transpose(0, 2, 1, 3).reshape(B, N, Dout)
        out = ctx @ Wo.T + bo
        out = out + x
        mu = jnp.mean(out, axis=-1, keepdims=True)
        var = jnp.mean(jnp.square(out - mu), axis=-1, keepdims=True)
        out = (out - mu) * jax.lax.rsqrt(var + EPS) * gamma + beta
        return out

    def _L1_gnn_ref(h, adj, W, a):
        import jax, jax.numpy as jnp
        import numpy as np
        ALPHA = 0.2
        Wh = jnp.matmul(h, W)
        D = W.shape[1]
        e_src = jnp.matmul(Wh, a[:D])
        e_dst = jnp.matmul(Wh, a[D:])
        e = e_src + jnp.swapaxes(e_dst, 1, 2)
        e = jnp.where(e > 0, e, ALPHA * e)
        mask = (adj > 0)[None, :, :]
        e = jnp.where(mask, e, -jnp.inf)
        alpha_w = jax.nn.softmax(e, axis=-1)
        h_prime = jnp.matmul(alpha_w, Wh)
        return jax.nn.elu(h_prime)

    def _L2_gnn_ref(x, W, a, adj):
        import jax, jax.numpy as jnp
        import numpy as np
        B, N, F_IN, F_OUT = (8, 1024, 128, 128)
        h = jnp.einsum('bnf,fo->bno', x, W)
        F = W.shape[1]
        a1 = a[:F, 0]
        a2 = a[F:, 0]
        s1 = jnp.einsum('bno,o->bn', h, a1)
        s2 = jnp.einsum('bno,o->bn', h, a2)
        e = jax.nn.leaky_relu(s1[:, :, None] + s2[:, None, :], negative_slope=0.2)
        mask = adj.astype(h.dtype)[None, :, :]
        e = e + (1.0 - mask) * -1000000000.0
        attention = jax.nn.softmax(e, axis=-1)
        out = jnp.einsum('bnm,bmo->bno', attention, h)
        return out

    def _L3_gnn_ref(x, adj, mlp1_w, mlp1_b, mlp2_w, mlp2_b, W_fc, a_fc, W_hand, a_hand):
        import jax, jax.numpy as jnp
        import numpy as np
        ALPHA = 0.2
        NEG_INF = -9000000000000000.0

        def _gat(inp, adj_mask, W, a):
            h = jnp.matmul(inp, W)
            F_ = h.shape[-1]
            f1 = jnp.matmul(h, a[:F_, 0])
            f2 = jnp.matmul(h, a[F_:, 0])
            e = jax.nn.leaky_relu(f1[:, :, None] + f2[:, None, :], ALPHA)
            if adj_mask is not None:
                e = jnp.where(adj_mask[None, :, :] > 0, e, NEG_INF)
            att = jax.nn.softmax(e, axis=2)
            h_prime = jnp.einsum('bij,bjf->bif', att, h)
            return jax.nn.elu(h_prime)
        out = jax.nn.relu(jnp.matmul(x, mlp1_w) + mlp1_b)
        residual = out
        out = _gat(jax.nn.relu(out), None, W_fc, a_fc)
        out = jax.nn.elu(out) + residual
        out = jax.nn.relu(jnp.matmul(out, mlp2_w) + mlp2_b)
        residual = out
        out = _gat(jax.nn.relu(out), adj, W_hand, a_hand)
        out = jax.nn.elu(out) + residual
        return jax.nn.relu(out)
    h = jnp.maximum(_layernorm(x, axis=-1), 0.0)
    x = x + _L0_gnn_ref(h, adj, L0_gnn_Wq, L0_gnn_bq, L0_gnn_Wk, L0_gnn_bk, L0_gnn_Wv, L0_gnn_bv, L0_gnn_Wo, L0_gnn_bo, L0_gnn_gamma, L0_gnn_beta)
    h = jnp.maximum(_layernorm(x, axis=-1), 0.0)
    x = x + _L1_gnn_ref(h, adj, L1_gnn_W, L1_gnn_a)
    h = jnp.maximum(_layernorm(x, axis=-1), 0.0)
    x = x + _L2_gnn_ref(h, L2_gnn_W, L2_gnn_a, adj)
    h = jnp.maximum(_layernorm(x, axis=-1), 0.0)
    x = x + _L3_gnn_ref(h, adj, L3_gnn_mlp1_w, L3_gnn_mlp1_b, L3_gnn_mlp2_w, L3_gnn_mlp2_b, L3_gnn_W_fc, L3_gnn_a_fc, L3_gnn_W_hand, L3_gnn_a_hand)
    return x

_drawn_inputs = setup_inputs


def setup_inputs(seed=0):
    import zlib

    import numpy as np

    out = dict(_drawn_inputs(seed))
    spreads = {'L0_gnn_bq': (0.0, 2.0),
     'L0_gnn_bk': (0.0, 2.0),
     'L0_gnn_bv': (0.0, 0.1),
     'L0_gnn_bo': (0.0, 0.46),
     'L0_gnn_gamma': (1.0, 0.2),
     'L0_gnn_beta': (0.0, 0.1),
     'L3_gnn_mlp1_b': (0.0, 0.1),
     'L3_gnn_mlp2_b': (0.0, 0.1)}
    factors = {'L3_gnn_a_hand': 8.0, 'L3_gnn_a_fc': 2.704}
    for name, (base, spread) in spreads.items():
        noise = np.random.default_rng([zlib.crc32(name.encode()), seed]).standard_normal(out[name].shape)
        drawn = base * np.exp(spread * noise) if base else spread * noise
        out[name] = jnp.asarray(drawn.astype(out[name].dtype))
    for name, factor in factors.items():
        out[name] = (out[name] * factor).astype(out[name].dtype)
    return out
```

```python
import math
from contextlib import ExitStack

import concourse.bass as bass
from concourse import mybir

F32 = mybir.dt.float32
F32R = mybir.dt.float32r
BF16 = mybir.dt.bfloat16
I32 = mybir.dt.int32
ALU = mybir.AluOpType
ACT = mybir.ActivationFunctionType
AX_X = mybir.AxisListType.X

P = 128
LN_EPS = 1e-5
SLOPE = 0.2
FAR = -1.0e30
CLIP_LO, CLIP_HI = math.exp(-10.0), math.exp(10.0)


def nth(b, per, k):
    return b * per + k


class Phase:

    def __init__(self, nc, ctx, tag):
        self.nc, self.ctx, self.tag = nc, ctx, tag
        self.sems = []
        self.passed = self.sem("passed")
        ctx.callback(self.clear)

    def clear(self):
        self.nc.clear_and_free_semaphores(self.sems)
        self.nc.all_engine_barrier()

    def wait_apart(self, eng, sem, value):
        eng.wait_ge(sem, value)
        eng.sem_inc(self.passed, 1)

    def sb(self, name, shape, dt=F32):
        return self.ctx.enter_context(self.nc.sbuf_tensor(f"{self.tag}_{name}", shape, dt))

    def ps(self, name, shape, dt=F32):
        return self.ctx.enter_context(self.nc.psum_tensor(f"{self.tag}_{name}", shape, dt))

    def sem(self, name):
        self.sems.append(self.nc.alloc_semaphore(f"{self.tag}_{name}"))
        return self.sems[-1]


def pipelined(eng, batches, step, lead):
    looped = batches - lead
    assert looped % 2 == 0 and looped >= 2
    with eng.Fori(0, looped // 2) as pair:
        for s in (0, 1):
            step(pair * 2 + s, s, pair, lead)
    for b in range(looped, batches):
        step(b, b % 2, b // 2, batches - 1 - b)




def masks_phase(nc, adj, clip_high, edge_bias, ident, NT, N):
    with ExitStack() as ctx:
        ph = Phase(nc, ctx, "high" if clip_high is not None else "bias")
        adj_in = ph.sb("adj_in", [P, NT, N], I32)
        adj_here = ph.sem("adj_here")
        bias_made = ph.sem("bias_made")
        if clip_high is not None:
            edge = ph.sb("edge", [P, NT, N], BF16)
            identb = ph.sb("identb", [P, P], BF16)
            turned = ph.ps("turned", [P, 2, 2 * N], BF16)
            zeroed = ph.sem("zeroed")
            ident_made = ph.sem("ident_made")
            edge_made = ph.sem("edge_made")
            turn_done = ph.sem("turn_done")
            high_made = ph.sem("high_made")
        block = ctx.enter_context(nc.Block())

        @block.sync
        def _(sp):
            for t in range(NT):
                sp.dma_start(adj_in[:, t, :], adj[t * P:(t + 1) * P, :]).then_inc(adj_here, 16)

        if clip_high is not None:
            @block.gpsimd
            def _(pool):
                pool.memset(ident[:], 0.0).then_inc(zeroed, 1)
                pool.memset(identb[:], 0.0).then_inc(zeroed, 1)
                pool.wait_ge(zeroed, 2)
                for m in (ident, identb):
                    pool.affine_select(out=m[:], in_=m[:], compare_op=ALU.not_equal, fill=1.0, base=0,
                                       pattern=[[-1, P]], channel_multiplier=1).then_inc(ident_made, 1)

            @block.tensor
            def _(pe):
                pe.wait_ge(ident_made, 2)
                pe.wait_ge(edge_made, NT)
                for c in range(NT):
                    if c >= 2:
                        pe.wait_ge(high_made, c - 1)
                    for t in range(NT):
                        last = pe.transpose(turned[:, c % 2, t * P:(t + 1) * P],
                                            edge[:, t, c * P:(c + 1) * P], identb[:])
                    last.then_inc(turn_done, 1)

        @block.vector
        def _(dve):
            dve.wait_ge(adj_here, 16 * NT)
            for t in range(NT):
                if clip_high is None:
                    dve.tensor_scalar(edge_bias[:, t, :], adj_in[:, t, :], 0, FAR, ALU.is_le,
                                      ALU.mult).then_inc(bias_made, 1)
                else:
                    dve.tensor_scalar(edge[:, t, :], adj_in[:, t, :], 0, None, ALU.is_gt).then_inc(edge_made, 1)
            if clip_high is not None:
                for c in range(NT):
                    dve.wait_ge(turn_done, c + 1)
                    dve.tensor_scalar(clip_high[:, c, :], turned[:, c % 2, 0:N], CLIP_HI - CLIP_LO, CLIP_LO, ALU.mult,
                                      ALU.add).then_inc(high_made, 1)






class Norm:

    def __init__(self, ph, NT, F, buffers=2):
        self.ph, self.NT, self.F = ph, NT, F
        self.x = ph.sb("ln_x", [P, buffers, NT, F])
        self.stats = ph.sb("ln_stats", [P, NT, 6])
        self.mv = ph.sb("ln_mean_var", [P, NT, 2])
        self.var_eps = ph.sb("ln_var_eps", [P, NT])
        self.rstd = ph.sb("ln_rstd", [P, NT])
        self.minus_half = ph.sb("ln_minus_half", [P, NT])
        self.y = ph.sb("ln_y", [P, NT, F])
        self.x_here = [ph.sem(f"x_here{i}") for i in range(buffers)]
        self.stats_made = ph.sem("ln_stats_made")
        self.mv_made = ph.sem("ln_mv_made")
        self.eps_added = ph.sem("ln_eps_added")
        self.rstd_made = ph.sem("ln_rstd_made")
        self.const_made = ph.sem("ln_const_made")
        self.y_made = ph.sem("ln_y_made")

    def vector(self, dve, b, s, turn):
        self.statistics(dve, b, s, turn)
        self.scale(dve, b, s)

    def statistics(self, dve, b, s, turn):
        NT = self.NT
        dve.wait_ge(self.x_here[s], nth(turn, 16, 16))
        for t in range(NT):
            dve.bn_stats(self.stats[:, t, :], self.x[:, s, t, :]).then_inc(self.stats_made, 1)
        self.ph.wait_apart(dve, self.stats_made, nth(b, NT, NT))
        for t in range(NT):
            dve.bn_aggr(self.mv[:, t, :], self.stats[:, t, :]).then_inc(self.mv_made, 1)
        dve.wait_ge(self.mv_made, nth(b, NT, NT))
        dve.tensor_scalar(self.var_eps[:], self.mv[:, :, 1], LN_EPS, None, ALU.add).then_inc(self.eps_added, 1)

    def scale(self, dve, b, s):
        NT = self.NT
        dve.wait_ge(self.rstd_made, nth(b, 1, 1))
        for t in range(NT):
            dve.tensor_scalar(self.y[:, t, :], self.x[:, s, t, :], self.mv[:, t, 0:1], self.rstd[:, t:t + 1],
                              ALU.subtract, ALU.mult).then_inc(self.y_made, 1)

    def gpsimd_consts(self, pool):
        pool.memset(self.minus_half[:], -0.5).then_inc(self.const_made, 1)
        pool.wait_ge(self.const_made, 1)

    def gpsimd(self, pool, b):
        pool.wait_ge(self.eps_added, nth(b, 1, 1))
        pool.tensor_tensor(self.rstd[:], self.var_eps[:], self.minus_half[:], ALU.pow).then_inc(self.rstd_made, 1)




def gat_phase(nc, tag, B, N, F, edge_bias, ident, W, a, x_in, x_out, kind, resid=None, hT_in=None):
    NT = N // P
    HB = NT // 2
    FE = F + 1
    normed = kind != "hand"
    TB = NT
    with ExitStack() as ctx:
        ph = Phase(nc, ctx, tag)
        wa = ph.sb("wa", [P, FE + P])
        w_in = ph.sb("w_in", [P, F])
        wT = ph.sb("wT", [P, F])
        a_in = ph.sb("a_in", [F, 2])
        wa2 = ph.sb("wa2", [P, 1])
        ln = Norm(ph, NT, F, buffers=1)
        x = ph.sb("x", [P, 2, NT, F])
        x_here = [ph.sem("x_again0"), ph.sem("x_again1")]
        if not normed:
            rs = ph.sb("rs", [P, 2, NT, F])
            rs_here = [ph.sem("rs_here0"), ph.sem("rs_here1")]
            hT_here = ph.sem("hT_here")
        hT = ph.sb("hT", [P, N])
        H = ph.sb("H", [P, 2, NT, FE])
        s2row = ph.sb("s2row", [P, N])
        s2row4 = ph.sb("s2row4", [P, N])
        y = ph.sb("y", [P, NT, N])
        u = ph.sb("u", [P, NT])
        s1m4 = ph.sb("s1m4", [P, NT])
        z = ph.sb("z", [P, NT])
        mx = ph.sb("mx", [P, NT])
        shift = ph.sb("shift", [P, NT])
        t_buf = ph.sb("t_buf", [P, TB, N])
        pr = ph.sb("pr", [P, NT, N])
        den = ph.sb("den", [P, 2, NT])
        rden = ph.sb("rden", [P, NT])
        prT = ph.sb("prT", [P, 2, NT, P])
        v = ph.sb("v", [P, 2, HB, F])
        vneg = ph.sb("vneg", [P, 2, HB, F])
        vexp = ph.sb("vexp", [P, 2, HB, F])
        res = ph.sb("res", [P, 2, HB, F])
        minus1 = ph.sb("minus1", [P, 1])
        minus1_made = ph.sem("minus1_made")
        work = ph.ps("work", [P, 2, 512])
        turned = ph.ps("turned", [P, 2, N])
        acc = ph.ps("acc", [P, 2, HB, F])

        w_here = ph.sem("w_here")
        w_turned = ph.sem("w_turned")
        wT_made = ph.sem("wT_made")
        wa_done = ph.sem("wa_done")
        wa_copied = ph.sem("wa_copied")
        wext_made = ph.sem("wext_made")
        work_full = ph.sem("work_full")
        hT_made = ph.sem("hT_made")
        s2_made = ph.sem("s2_made")
        H_made = ph.sem("H_made")
        y_max = ph.sem("y_max")
        s1m4_made = ph.sem("s1m4_made")
        z_made = ph.sem("z_made")
        mx_made = ph.sem("mx_made")
        shift_made = ph.sem("shift_made")
        t_made = ph.sem("t_made")
        pr_made = ph.sem("pr_made")
        turn_done = ph.sem("turn_done")
        prT_made = ph.sem("prT_made")
        weighed = ph.sem("weighed")
        rden_made = ph.sem("rden_made")
        v_made = ph.sem("v_made")
        vneg_made = ph.sem("vneg_made")
        vexp_made = ph.sem("vexp_made")
        vexp2_made = ph.sem("vexp2_made")
        sum_made = ph.sem("sum_made")
        sum2_made = ph.sem("sum2_made")
        res_made = ph.sem("res_made")
        stored = [ph.sem("stored0"), ph.sem("stored1")]
        block = ctx.enter_context(nc.Block())
        JOBS = 5 if normed else 4
        H_JOBS = [(0, 3), (3, 3), (6, 2)]
        NPOST = {"plain": 0, "elu": 1, "hand": 1}[kind]

        def rows(dram, b):
            return dram[b].rearrange("(t p) f -> p t f", p=P)

        ORDER = "e2 x0 x1 e3 h x2 e4 s x3 v0 e5 x4 x5 e6 x6 e7 x7 H n0 n1 v1"

        @block.sync
        def _(sp):
            sp.dma_start(w_in[:], W).then_inc(w_here, 16)
            for k in range(2):
                sp.dma_start(a_in[:, k:k + 1], a[k * F:(k + 1) * F, :]).then_inc(w_here, 16)

            def load(b, s):
                sp.dma_start(x[:, s, :, :], rows(x_in, b)).then_inc(x_here[s], 16)
                if not normed:
                    sp.dma_start(rs[:, s, :, :], rows(resid, b)).then_inc(rs_here[s], 16)

            def load_input(b):
                first = isinstance(b, int) and b == 0
                if normed:
                    if not first:
                        ph.wait_apart(sp, ln.y_made, nth(b, NT, 0))
                    sp.dma_start(ln.x[:, 0, :, :], rows(x_in, b)).then_inc(ln.x_here[0], 16)
                else:
                    if not first:
                        ph.wait_apart(sp, work_full, nth(b, JOBS, 0))
                    sp.dma_start(hT[:], hT_in[b]).then_inc(hT_here, 16)

            load_input(0)
            load(0, 0)
            load_input(1)
            load(1, 1)
            load_input(2)

            def step(b, s, pair, left):
                for k in range(2):
                    ph.wait_apart(sp, res_made, nth(b, 2, k + 1))
                    sp.dma_start(rows(x_out, b)[:, k * HB:(k + 1) * HB, :], res[:, k, :, :]).then_inc(stored[k], 16)
                    if k == 0 and left >= 3:
                        load_input(b + 3)
                if left >= 2:
                    load(b + 2, s)

            pipelined(sp, B, step, 4)
            for k in range(2):
                sp.wait_ge(stored[k], 16 * B + 16)

        @block.gpsimd
        def _(pool):
            pool.sem_inc(weighed, 2)
            pool.sem_inc(prT_made, 2)
            pool.sem_inc(v_made, NT)
            pool.sem_inc(rden_made, 1)
            for k in range(2):
                pool.sem_inc(stored[k], 16)
            if kind == "hand":
                pool.memset(minus1[:], -1.0).then_inc(minus1_made, 1)
            if normed:
                ln.gpsimd_consts(pool)
                ln.gpsimd(pool, 0)
                ln.gpsimd(pool, 1)

                def step(b, s, pair, left):
                    if left >= 2:
                        ln.gpsimd(pool, b + 2)

                pipelined(pool, B, step, 2)

        @block.vector
        def _(dve):
            dve.wait_ge(w_here, 48)
            dve.wait_ge(w_turned, 1)
            dve.tensor_copy(wT[:], work[:, 0, 0:F]).then_inc(wT_made, 1)
            dve.tensor_copy(wa[:, 0:F], w_in[:]).then_inc(wext_made, 1)
            dve.wait_ge(wa_done, 1)
            dve.tensor_copy(wa2[:], work[:, 1, 1:2]).then_inc(wa_copied, 1)
            dve.tensor_copy(wa[:, F:FE], work[:, 1, 0:1]).then_inc(wext_made, 1)
            dve.wait_ge(wa_copied, 1)
            dve.tensor_copy(wa[:, FE:FE + P], wa2[:].broadcast_to([P, P])).then_inc(wext_made, 1)

            def maxima(b, t0, t1):
                if t0 == 0 and (not isinstance(b, int) or b > 0):
                    dve.wait_ge(t_made, nth(b, NT, 0))
                if t0 == 0:
                    ph.wait_apart(dve, s2_made, nth(b, 2, 2))
                for t in range(t0, t1):
                    dve.tensor_tensor_reduce(y[:, t, :], s2row[:], edge_bias[:, t, :], 1.0, -3.0e38, ALU.add,
                                             ALU.max, u[:, t:t + 1]).then_inc(y_max, 1)

            def shifts(b, s):
                dve.wait_ge(H_made, nth(b, 3, 3))
                if not isinstance(b, int) or b > 0:
                    dve.wait_ge(t_made, nth(b, NT, 0))
                s1 = H[:, s, :, F]
                dve.tensor_scalar(s1m4[:], s1, -4.0, None, ALU.mult).then_inc(s1m4_made, 1)
                dve.wait_ge(y_max, nth(b, NT, NT))
                dve.tensor_tensor(z[:], s1, u[:], ALU.add).then_inc(z_made, 1)
                dve.wait_ge(z_made, nth(b, 1, 1))
                dve.scalar_tensor_tensor(out=mx[:], in0=z[:], scalar=SLOPE, in1=z[:], op0=ALU.mult,
                                         op1=ALU.max).then_inc(mx_made, 1)
                dve.wait_ge(mx_made, nth(b, 1, 1))
                if not isinstance(b, int) or b > 0:
                    dve.wait_ge(pr_made, nth(b, NT, 0))
                dve.tensor_tensor(shift[:], s1, mx[:], ALU.subtract).then_inc(shift_made, 1)
                dve.wait_ge(s1m4_made, nth(b, 1, 1))

            def t_tile(b, t):
                if not isinstance(b, int) or b > 0 or t >= TB:
                    dve.wait_ge(pr_made, nth(b, NT, t + 1 - TB))
                dve.scalar_tensor_tensor(out=t_buf[:, t % TB, :], in0=s2row4[:], scalar=s1m4[:, t:t + 1],
                                         in1=y[:, t, :], op0=ALU.max, op1=ALU.add).then_inc(t_made, 1)

            def divide(b, s, k):
                if k == 0:
                    dve.wait_ge(pr_made, nth(b, NT, NT))
                    dve.reciprocal(rden[:], den[:, s, :]).then_inc(rden_made, 1)
                    dve.wait_ge(rden_made, nth(b, 1, 1) + 1)
                dve.wait_ge(weighed, nth(b, NT, (k + 1) * HB) + 2)
                dve.wait_ge(stored[k], nth(b, 16, 16))
                for q in range(HB):
                    t = k * HB + q
                    dve.tensor_scalar(v[:, k, q, :], acc[:, k, q, :], rden[:, t:t + 1], None,
                                      ALU.mult).then_inc(v_made, 1)
                dve.wait_ge(v_made, nth(b, NT, (k + 1) * HB) + NT)
                if kind != "plain":
                    dve.tensor_scalar(vneg[:, k, :, :], v[:, k, :, :], 0.0, None, ALU.min).then_inc(vneg_made, 1)

            def post(b, s, half, k):
                xs = x[:, s, k * HB:(k + 1) * HB, :]
                if k == 0:
                    dve.wait_ge(x_here[s], nth(half, 16, 16))
                if kind == "plain":
                    dve.tensor_tensor(res[:, k, :, :], v[:, k, :, :], xs, ALU.add).then_inc(res_made, 1)
                    return
                dve.wait_ge(vexp_made, nth(b, 2, k + 1))
                dve.scalar_tensor_tensor(out=v[:, k, :, :], in0=v[:, k, :, :], scalar=0.0, in1=vexp[:, k, :, :],
                                         op0=ALU.max, op1=ALU.add).then_inc(sum_made, 1)
                dve.wait_ge(sum_made, nth(b, 2, k + 1))
                if kind == "elu":
                    dve.scalar_tensor_tensor(out=res[:, k, :, :], in0=v[:, k, :, :], scalar=-1.0, in1=xs,
                                             op0=ALU.add, op1=ALU.add).then_inc(res_made, 1)
                    return
                if k == 0:
                    dve.wait_ge(rs_here[s], nth(half, 16, 16))
                dve.scalar_tensor_tensor(out=vneg[:, k, :, :], in0=v[:, k, :, :], scalar=-1.0,
                                         in1=rs[:, s, k * HB:(k + 1) * HB, :], op0=ALU.add,
                                         op1=ALU.add).then_inc(sum2_made, 1)
                dve.wait_ge(sum2_made, nth(b, 2, k + 1))
                dve.scalar_tensor_tensor(out=res[:, k, :, :], in0=vneg[:, k, :, :], scalar=0.0, in1=xs,
                                         op0=ALU.max, op1=ALU.add).then_inc(res_made, 1)

            def norm(b):
                if not isinstance(b, int) or b > 0:
                    dve.wait_ge(work_full, nth(b, JOBS, 1 - JOBS))
                ln.scale(dve, b, 0)

            if normed:
                ln.statistics(dve, 0, 0, 0)
                norm(0)
                ln.statistics(dve, 1, 0, 1)
                norm(1)
            maxima(0, 0, NT)
            shifts(0, 0)
            for t in range(NT):
                t_tile(0, t)
            maxima(1, 0, NT)
            shifts(1, 1)
            t_tile(1, 0)

            def step(b, s, pair, left):
                if left >= 2 and normed:
                    ln.statistics(dve, b + 2, 0, b + 2)
                if left >= 1:
                    for t in range(1, 3):
                        t_tile(b + 1, t)
                if left >= 2 and normed:
                    norm(b + 2)
                if left >= 1:
                    for t in range(3, NT):
                        t_tile(b + 1, t)
                divide(b, s, 0)
                if left >= 2:
                    maxima(b + 2, 0, 3)
                post(b, s, pair, 0)
                if left >= 2:
                    maxima(b + 2, 3, NT)
                    shifts(b + 2, s)
                    t_tile(b + 2, 0)
                divide(b, s, 1)
                post(b, s, pair, 1)

            pipelined(dve, B, step, 2)

        @block.scalar
        def _(act):
            whole = work[:].rearrange("p a n -> p (a n)")

            def take_hT(b):
                if normed:
                    act.wait_ge(work_full, nth(b, JOBS, 1))
                    act.activation(hT[:], whole, ACT.Relu).then_inc(hT_made, 1)

            def take_s2(b):
                act.wait_ge(work_full, nth(b, JOBS, JOBS - 3))
                if not isinstance(b, int) or b > 0:
                    act.wait_ge(t_made, nth(b, NT, 0))
                act.activation(s2row[:], whole, ACT.Copy).then_inc(s2_made, 1)
                act.activation(s2row4[:], whole, ACT.Copy, scale=4.0).then_inc(s2_made, 1)

            def take_H(b, s):
                for i, (t0, n) in enumerate(H_JOBS):
                    act.wait_ge(work_full, nth(b, JOBS, JOBS - 2 + i))
                    act.activation(H[:, s, t0:t0 + n, :],
                                   work[:, i % 2, 0:n * FE].rearrange("p (t f) -> p t f", t=n),
                                   ACT.Copy).then_inc(H_made, 1)

            def exps(b, s, t):
                act.wait_ge(t_made, nth(b, NT, t + 1))
                if t == 0:
                    act.wait_ge(shift_made, nth(b, 1, 1))
                    if not isinstance(b, int) or b > 0:
                        act.wait_ge(rden_made, nth(b, 1, 0))
                if not isinstance(b, int) or b > 0:
                    act.wait_ge(turn_done, nth(b, NT, t + 1 - NT))
                act.activation(pr[:, t, :], t_buf[:, t % TB, :], ACT.Exp, bias=shift[:, t:t + 1], scale=SLOPE,
                               accum_out=den[:, s, t:t + 1]).then_inc(pr_made, 1)

            def evac(b, t):
                act.wait_ge(turn_done, nth(b, NT, t + 1))
                act.wait_ge(weighed, nth(b, NT, t + 1))
                act.activation(prT[:, t % 2, :, :].rearrange("p a n -> p (a n)"), turned[:, t % 2, :],
                               ACT.Copy).then_inc(prT_made, 1)

            def vexp_half(b, k):
                if kind == "plain":
                    return
                act.wait_ge(vneg_made, nth(b, 2, k + 1))
                act.activation(vexp[:, k, :, :], vneg[:, k, :, :], ACT.Exp).then_inc(
                    vexp_made if kind == "elu" else vexp2_made, 1)
                if kind == "hand":
                    act.wait_ge(vexp2_made, nth(b, 2, k + 1))
                    act.activation(vexp[:, k, :, :], vexp[:, k, :, :], ACT.Exp, bias=minus1[:]).then_inc(vexp_made, 1)

            act.wait_ge(wext_made, 3)
            if kind == "hand":
                act.wait_ge(minus1_made, 1)
            take_hT(0)
            take_s2(0)
            take_H(0, 0)
            for t in range(NT):
                exps(0, 0, t)
            take_hT(1)
            take_s2(1)
            take_H(1, 1)
            evac(0, 0)
            evac(0, 1)

            def step(b, s, pair, left):
                for what in ORDER.split():
                    n = int(what[1:] or 0)
                    if what[0] == "e":
                        evac(b, n)
                    elif what[0] == "n" and left >= 1:
                        evac(b + 1, n)
                    elif what[0] == "v":
                        vexp_half(b, n)
                    elif what[0] == "x" and left >= 1:
                        exps(b + 1, 1 - s, n)
                    elif what == "h" and left >= 2:
                        take_hT(b + 2)
                    elif what == "s" and left >= 2:
                        take_s2(b + 2)
                    elif what == "H" and left >= 2:
                        take_H(b + 2, s)

            pipelined(act, B, step, 2)

        @block.tensor
        def _(pe):
            pe.wait_ge(w_here, 48)
            pe.transpose(work[:, 0, 0:P], w_in[:], ident[:]).then_inc(w_turned, 1)
            pe.wait_ge(wT_made, 1)
            pe.matmul(work[:, 1, 0:2], wT[:], a_in[:], start=True, stop=True).then_inc(wa_done, 1)
            pe.wait_ge(wext_made, 3)

            def turn_y(b):
                if normed:
                    pe.wait_ge(ln.y_made, nth(b, NT, NT))
                    if not isinstance(b, int) or b > 0:
                        pe.wait_ge(H_made, nth(b, 3, 0))
                    for t in range(NT):
                        last = pe.transpose(work[:, t // 4, (t % 4) * P:(t % 4 + 1) * P], ln.y[:, t, :], ident[:])
                    last.then_inc(work_full, 1)

            def s2_product(b):
                if normed:
                    pe.wait_ge(hT_made, nth(b, 1, 1))
                else:
                    pe.wait_ge(hT_here, nth(b, 16, 16))
                    if not isinstance(b, int) or b > 0:
                        pe.wait_ge(H_made, nth(b, 3, 0))
                for k in range(2):
                    last = pe.matmul(work[:, k, :], wa[:, FE:FE + P], hT[:, k * 512:(k + 1) * 512], start=True,
                                     stop=True)
                last.then_inc(work_full, 1)

            def H_products(b):
                for i, (t0, n) in enumerate(H_JOBS):
                    if i == 0:
                        pe.wait_ge(s2_made, nth(b, 2, 2))
                    if i == 2:
                        pe.wait_ge(H_made, nth(b, 3, 1))
                    for t in range(t0, t0 + n):
                        last = pe.matmul(work[:, i % 2, (t - t0) * FE:(t - t0 + 1) * FE], hT[:, t * P:(t + 1) * P],
                                         wa[:, 0:FE], start=True, stop=True)
                    last.then_inc(work_full, 1)

            def turn(b, t):
                pe.wait_ge(pr_made, nth(b, NT, t + 1))
                pe.wait_ge(prT_made, nth(b, NT, t + 1))
                for j in range(NT):
                    last = pe.transpose(turned[:, t % 2, j * P:(j + 1) * P], pr[:, t, j * P:(j + 1) * P], ident[:])
                last.then_inc(turn_done, 1)

            def weigh(b, s, t):
                k, q = t // HB, t % HB
                pe.wait_ge(prT_made, nth(b, NT, t + 1) + 2)
                if q == 0:
                    pe.wait_ge(v_made, nth(b, NT, (k + 1) * HB))
                for j in range(NT):
                    last = pe.matmul(acc[:, k, q, :], prT[:, t % 2, j, :], H[:, s, j, 0:F], start=(j == 0),
                                     stop=(j == NT - 1))
                last.then_inc(weighed, 1)

            for b in range(2):
                turn_y(b)
                s2_product(b)
                H_products(b)

            def step(b, s, pair, left):
                turn(b, 0)
                for t in range(NT):
                    if t + 1 < NT:
                        turn(b, t + 1)
                    if left >= 2 and t == 3:
                        turn_y(b + 2)
                    if left >= 2 and t == 4:
                        s2_product(b + 2)
                    weigh(b, s, t)
                if left >= 2:
                    H_products(b + 2)

            pipelined(pe, B, step, 2)




def fc_phase(nc, tag, B, N, F, ident, mlp1_w, mlp1_b, W, a, mlp2_w, mlp2_b, x_in, hT_out, h_out):
    NT = N // P
    HB = NT // 2
    W2 = 2 * F
    with ExitStack() as ctx:
        ph = Phase(nc, ctx, tag)
        ln = Norm(ph, NT, F)
        w1 = ph.sb("w1", [P, W2])
        b1 = ph.sb("b1", [P, 2])
        w_in = ph.sb("w_in", [P, 2, W2])
        wT = ph.sb("wT", [P, 2, W2])
        a_in = ph.sb("a_in", [P, 2, 2])
        wx = ph.sb("wx", [P, 2, W2 + 1])
        wa1 = ph.sb("wa1", [P, 2, 1])
        wa1_wide = ph.sb("wa1_wide", [P, 2, P])
        w2 = ph.sb("w2", [P, 2, F])
        b2 = ph.sb("b2", [P, 1])
        minus1 = ph.sb("minus1", [P, 1])
        hT = ph.sb("hT", [P, N])
        o1T = ph.sb("o1T", [P, 2, 2, N])
        H = ph.sb("H", [P, 2, NT, W2 + 2])
        f2max = ph.sb("f2max", [P, 1])
        G = ph.sb("G", [P, 1])
        mG8 = ph.sb("mG8", [P, 1])
        mG2 = ph.sb("mG2", [P, 1])
        E = ph.sb("E", [P, NT])
        D = ph.sb("D", [P, NT])
        F_raw = ph.sb("F_raw", [P, N])
        F_row = ph.sb("F_row", [P, N])
        prT = ph.sb("prT", [P, 2, NT, N])
        rden = ph.sb("rden", [P, NT])
        v = ph.sb("v", [P, 2, HB, W2])
        vexp = ph.sb("vexp", [P, 2, HB, W2])
        g = ph.sb("g", [P, 2, HB, W2])
        g2T = ph.sb("g2T", [P, 2, N])
        o2T = ph.sb("o2T", [P, 2, 512])
        o2 = ph.sb("o2", [P, 2, HB, F])
        work = ph.ps("work", [P, 2, 512])
        acc = ph.ps("acc", [P, 2, 512])
        gT_ps = ph.ps("gT_ps", [P, 2, 512])
        m2_ps = ph.ps("m2_ps", [P, 512])
        nat_ps = ph.ps("nat_ps", [P, HB, F])

        w_here = ph.sem("w_here")
        w_turned = ph.sem("w_turned")
        wT_made = ph.sem("wT_made")
        wa_done = ph.sem("wa_done")
        wa_copied = ph.sem("wa_copied")
        wext_made = ph.sem("wext_made")
        ones_made = ph.sem("ones_made")
        work_full = ph.sem("work_full")
        hT_made = ph.sem("hT_made")
        o1_made = ph.sem("o1_made")
        H_made = ph.sem("H_made")
        f2max_made = ph.sem("f2max_made")
        G_made = ph.sem("G_made")
        mG_made = ph.sem("mG_made")
        ED_made = ph.sem("ED_made")
        F_made = ph.sem("F_made")
        F_cut = ph.sem("F_cut")
        prT_made = ph.sem("prT_made")
        acc_done = ph.sem("acc_done")
        rden_made = ph.sem("rden_made")
        v_made = ph.sem("v_made")
        vneg_made = ph.sem("vneg_made")
        exp1_made = ph.sem("exp1_made")
        exp2_made = ph.sem("exp2_made")
        g_made = ph.sem("g_made")
        gT_done = ph.sem("gT_done")
        g2T_made = ph.sem("g2T_made")
        m2_done = ph.sem("m2_done")
        o2T_made = ph.sem("o2T_made")
        nat_done = ph.sem("nat_done")
        o2_made = ph.sem("o2_made")
        o2T_stored = [ph.sem("o2T_stored0"), ph.sem("o2T_stored1")]
        o2_stored = [ph.sem("o2_stored0"), ph.sem("o2_stored1")]
        block = ctx.enter_context(nc.Block())
        JOBS = 8

        def rows(dram, b):
            return dram[b].rearrange("(t p) f -> p t f", p=P)

        @block.sync
        def _(sp):
            def load(b, s):
                sp.dma_start(ln.x[:, s, :, :], rows(x_in, b)).then_inc(ln.x_here[s], 16)

            load(0, 0)
            sp.dma_start(w_in[:], W.rearrange("(c p) n -> p c n", p=P)).then_inc(w_here, 16)
            for k in range(2):
                for c in range(2):
                    sp.dma_start(a_in[:, c, k:k + 1], a[k * W2 + c * P:k * W2 + (c + 1) * P, :]).then_inc(w_here, 16)
            sp.dma_start(w1[:], mlp1_w).then_inc(w_here, 16)
            for c in range(2):
                sp.dma_start(b1[:, c:c + 1], mlp1_b[c * P:(c + 1) * P].rearrange("(p o) -> p o", o=1)).then_inc(w_here, 16)
            sp.dma_start(w2[:], mlp2_w.rearrange("(c p) n -> p c n", p=P)).then_inc(w_here, 16)
            sp.dma_start(b2[:], mlp2_b.rearrange("(p o) -> p o", o=1)).then_inc(w_here, 16)
            load(1, 1)

            def step(b, s, pair, left):
                if left >= 2:
                    ph.wait_apart(sp, ln.y_made, nth(b, NT, NT))
                    load(b + 2, s)
                for k in range(2):
                    ph.wait_apart(sp, o2T_made, nth(b, 2, k + 1) + 1)
                    sp.dma_start(hT_out[b][:, k * 512:(k + 1) * 512], o2T[:, k, :]).then_inc(o2T_stored[k], 16)
                    ph.wait_apart(sp, o2_made, nth(b, 2, k + 1) + 1)
                    sp.dma_start(rows(h_out, b)[:, k * HB:(k + 1) * HB, :], o2[:, k, :, :]).then_inc(o2_stored[k], 16)

            pipelined(sp, B, step, 2)
            for k in range(2):
                sp.wait_ge(o2T_stored[k], 16 * B + 16)
                sp.wait_ge(o2_stored[k], 16 * B + 16)

        @block.gpsimd
        def _(pool):
            for s_, n in ((g2T_made, 2), (v_made, 2), (gT_done, 2), (m2_done, 2), (o2T_made, 1), (nat_done, 2),
                          (o2_made, 1), (o2T_stored[0], 16), (o2T_stored[1], 16), (o2_stored[0], 16),
                          (o2_stored[1], 16)):
                pool.sem_inc(s_, n)
            pool.memset(minus1[:], -1.0).then_inc(ones_made, 1)
            for s_ in range(2):
                pool.memset(H[:, s_, :, W2 + 1:W2 + 2], 1.0).then_inc(ones_made, 1)
            ln.gpsimd_consts(pool)

            def reduce_G(b):
                ph.wait_apart(pool, f2max_made, nth(b, 1, 1))
                pool.partition_all_reduce(G[:], f2max[:], P, bass.bass_isa.ReduceOp.max).then_inc(G_made, 1)

            ln.gpsimd(pool, 0)
            ln.gpsimd(pool, 1)
            reduce_G(0)

            def step(b, s, pair, left):
                if left >= 1:
                    reduce_G(b + 1)
                if left >= 2:
                    ln.gpsimd(pool, b + 2)

            pipelined(pool, B, step, 2)

        @block.vector
        def _(dve):
            dve.wait_ge(w_here, 16 * 10)
            dve.wait_ge(w_turned, 1)
            dve.tensor_copy(wT[:].rearrange("p c (e m) -> p c e m", e=2),
                            work[:, 0, :].rearrange("p (c e m) -> p c e m", c=2, e=2)).then_inc(wT_made, 1)
            dve.tensor_copy(wx[:, :, 1:W2 + 1], w_in[:]).then_inc(wext_made, 1)
            dve.wait_ge(wa_done, 1)
            for c in range(2):
                dve.tensor_copy(wa1[:, c, :], work[:, 1, 2 * c:2 * c + 1]).then_inc(wa_copied, 1)
                dve.tensor_copy(wx[:, c, 0:1], work[:, 1, 2 * c + 1:2 * c + 2]).then_inc(wext_made, 1)
            dve.wait_ge(wa_copied, 2)
            for c in range(2):
                dve.tensor_copy(wa1_wide[:, c, :], wa1[:, c, :].broadcast_to([P, P])).then_inc(wext_made, 1)

            def norm(b, s, half):
                if not isinstance(b, int) or b > 0:
                    dve.wait_ge(work_full, nth(b, JOBS, 1 - JOBS))
                ln.vector(dve, b, s, half)

            def top_f2(b, s):
                dve.wait_ge(H_made, nth(b, 4, 4))
                if not isinstance(b, int) or b > 0:
                    dve.wait_ge(G_made, nth(b, 1, 0))
                dve.tensor_reduce(f2max[:], H[:, s, :, 0], AX_X, ALU.max).then_inc(f2max_made, 1)

            def minus_G(b):
                dve.wait_ge(G_made, nth(b, 1, 1))
                if not isinstance(b, int) or b > 0:
                    dve.wait_ge(F_made, nth(b, 1, 0))
                dve.tensor_scalar(mG8[:], G[:], -(1.0 - SLOPE), None, ALU.mult).then_inc(mG_made, 1)
                dve.tensor_scalar(mG2[:], G[:], -SLOPE, None, ALU.mult).then_inc(mG_made, 1)

            def cut_F(b):
                dve.wait_ge(F_made, nth(b, 1, 1))
                if not isinstance(b, int) or b > 0:
                    dve.wait_ge(prT_made, nth(b, NT, 0))
                dve.tensor_scalar(F_row[:], F_raw[:], 1.0, None, ALU.min).then_inc(F_cut, 1)
                dve.wait_ge(F_cut, nth(b, 1, 1))
                dve.wait_ge(ED_made, nth(b, 2, 2))

            def probs(b, s, j0, j1):
                for j in range(j0, j1):
                    dve.tensor_scalar(prT[:, s, j, :], F_row[:], E[:, j:j + 1], D[:, j:j + 1], ALU.max,
                                      ALU.mult).then_inc(prT_made, 1)

            def divide(b, t):
                dve.wait_ge(acc_done, nth(b, NT, t + 1))
                dve.reciprocal(rden[:, t:t + 1], acc[:, t % 2, W2:W2 + 1]).then_inc(rden_made, 1)
                dve.wait_ge(rden_made, nth(b, NT, t + 1))
                dve.tensor_scalar(v[:, t // HB, t % HB, :], acc[:, t % 2, 0:W2], rden[:, t:t + 1], None,
                                  ALU.mult).then_inc(v_made, 1)

            def negative(b, k):
                dve.wait_ge(v_made, nth(b, NT, (k + 1) * HB) + 2)
                dve.tensor_scalar(vexp[:, k, :, :], v[:, k, :, :], 0.0, None, ALU.min).then_inc(vneg_made, 1)

            def positive(b, k):
                dve.wait_ge(exp2_made, nth(b, 2, k + 1))
                dve.wait_ge(gT_done, nth(b, 2, k + 1))
                dve.scalar_tensor_tensor(out=g[:, k, :, :], in0=v[:, k, :, :], scalar=0.0, in1=vexp[:, k, :, :],
                                         op0=ALU.max, op1=ALU.add).then_inc(g_made, 1)

            def add_o1(b, s, k):
                dve.wait_ge(gT_done, nth(b, 2, k + 1) + 2)
                dve.wait_ge(m2_done, nth(b, 2, k + 1))
                dve.scalar_tensor_tensor(out=g2T[:, :, k * 512:(k + 1) * 512], in0=gT_ps[:], scalar=-1.0,
                                         in1=o1T[:, s, :, k * 512:(k + 1) * 512], op0=ALU.add,
                                         op1=ALU.add).then_inc(g2T_made, 1)

            norm(0, 0, 0)
            norm(1, 1, 0)
            top_f2(0, 0)
            minus_G(0)
            cut_F(0)
            probs(0, 0, 0, NT)

            def step(b, s, pair, left):
                more = left >= 1
                for t in range(HB):
                    divide(b, t)
                negative(b, 0)
                divide(b, 4)
                positive(b, 0)
                divide(b, 5)
                if more:
                    top_f2(b + 1, 1 - s)
                divide(b, 6)
                add_o1(b, s, 0)
                if more:
                    minus_G(b + 1)
                divide(b, 7)
                negative(b, 1)
                if more:
                    cut_F(b + 1)
                    probs(b + 1, 1 - s, 0, HB)
                positive(b, 1)
                if more:
                    probs(b + 1, 1 - s, HB, NT)
                add_o1(b, s, 1)
                if left >= 2:
                    norm(b + 2, s, pair + 1)

            pipelined(dve, B, step, 2)

        @block.scalar
        def _(act):
            two = lambda ap: ap.rearrange("p a n -> p (a n)")

            def take_hT(b):
                act.wait_ge(work_full, nth(b, JOBS, 1))
                act.activation(hT[:], two(work[:]), ACT.Relu).then_inc(hT_made, 1)

            def take_o1(b, s, c):
                act.wait_ge(work_full, nth(b, JOBS, 2 + c))
                if c == 0 and (not isinstance(b, int) or b > 0):
                    act.wait_ge(g2T_made, nth(b, 2, 0))
                act.activation(o1T[:, s, c, :], two(work[:]), ACT.Relu, bias=b1[:, c:c + 1]).then_inc(o1_made, 1)

            def take_H(b, s, i):
                act.wait_ge(work_full, nth(b, JOBS, 4 + i))
                act.activation(H[:, s, 2 * i:2 * i + 2, 0:W2 + 1], work[:, :, 0:W2 + 1], ACT.Copy).then_inc(H_made, 1)

            def exp_f2(b, s):
                act.wait_ge(mG_made, nth(b, 2, 2))
                if not isinstance(b, int) or b > 0:
                    act.wait_ge(prT_made, nth(b, NT, 0))
                act.activation(E[:], H[:, s, :, 0], ACT.Exp, bias=mG8[:], scale=1.0 - SLOPE).then_inc(ED_made, 1)
                act.activation(D[:], H[:, s, :, 0], ACT.Exp, bias=mG2[:], scale=SLOPE).then_inc(ED_made, 1)

            def exp_f1(b):
                act.wait_ge(work_full, nth(b, JOBS, 8))
                if not isinstance(b, int) or b > 0:
                    act.wait_ge(F_cut, nth(b, 1, 0))
                act.activation(F_raw[:], two(work[:]), ACT.Exp, bias=mG8[:], scale=-(1.0 - SLOPE)).then_inc(F_made, 1)

            def elu_exps(b, k):
                act.wait_ge(vneg_made, nth(b, 2, k + 1))
                act.activation(vexp[:, k, :, :], vexp[:, k, :, :], ACT.Exp).then_inc(exp1_made, 1)
                act.wait_ge(exp1_made, nth(b, 2, k + 1))
                act.activation(vexp[:, k, :, :], vexp[:, k, :, :], ACT.Exp, bias=minus1[:]).then_inc(exp2_made, 1)

            def take_o2T(b, k):
                act.wait_ge(m2_done, nth(b, 2, k + 1) + 2)
                act.wait_ge(o2T_stored[k], nth(b, 16, 16))
                act.wait_ge(nat_done, nth(b, 2, k + 1))
                act.activation(o2T[:, k, :], m2_ps[:], ACT.Relu, bias=b2[:]).then_inc(o2T_made, 1)

            def take_o2(b, k):
                act.wait_ge(nat_done, nth(b, 2, k + 1) + 2)
                act.wait_ge(o2_stored[k], nth(b, 16, 16))
                act.activation(o2[:, k, :, :], nat_ps[:], ACT.Copy).then_inc(o2_made, 1)

            act.wait_ge(w_here, 16 * 10)
            act.wait_ge(ones_made, 3)
            take_hT(0)
            take_o1(0, 0, 0)
            take_o1(0, 0, 1)
            for i in range(4):
                take_H(0, 0, i)
            exp_f2(0, 0)
            exp_f1(0)

            def step(b, s, pair, left):
                more, n, o = left >= 1, b + 1, 1 - s
                if more:
                    take_hT(n)
                    take_o1(n, o, 0)
                    take_o1(n, o, 1)
                    take_H(n, o, 0)
                    take_H(n, o, 1)
                elu_exps(b, 0)
                if more:
                    take_H(n, o, 2)
                    take_H(n, o, 3)
                    exp_f2(n, o)
                take_o2T(b, 0)
                if more:
                    exp_f1(n)
                take_o2(b, 0)
                elu_exps(b, 1)
                take_o2T(b, 1)
                take_o2(b, 1)

            pipelined(act, B, step, 2)

        @block.tensor
        def _(pe):
            pe.wait_ge(w_here, 16 * 10)
            for e in range(2):
                for c in range(2):
                    last = pe.transpose(work[:, 0, (2 * e + c) * P:(2 * e + c + 1) * P], w_in[:, c, e * P:(e + 1) * P],
                                        ident[:])
            last.then_inc(w_turned, 1)
            pe.wait_ge(wT_made, 1)
            for c in range(2):
                for e in range(2):
                    last = pe.matmul(work[:, 1, 2 * c:2 * c + 2], wT[:, e, c * P:(c + 1) * P], a_in[:, e, :],
                                     start=(e == 0), stop=(e == 1))
            last.then_inc(wa_done, 1)
            pe.wait_ge(wext_made, 5)
            pe.wait_ge(ones_made, 3)

            def job(b, s, n):
                if n == 0:
                    pe.wait_ge(ln.y_made, nth(b, NT, NT))
                    if not isinstance(b, int) or b > 0:
                        pe.wait_ge(F_made, nth(b, 1, 0))
                    for t in range(NT):
                        last = pe.transpose(work[:, t // 4, (t % 4) * P:(t % 4 + 1) * P], ln.y[:, t, :], ident[:])
                elif n in (1, 2):
                    pe.wait_ge(hT_made, nth(b, 1, 1))
                    if n == 2:
                        pe.wait_ge(o1_made, nth(b, 2, 1))
                    c = n - 1
                    for k in range(2):
                        last = pe.matmul(work[:, k, :], w1[:, c * P:(c + 1) * P], hT[:, k * 512:(k + 1) * 512],
                                         start=True, stop=True)
                elif n < 7:
                    i = n - 3
                    if i == 0:
                        pe.wait_ge(o1_made, nth(b, 2, 2))
                    else:
                        pe.wait_ge(H_made, nth(b, 4, i))
                    for q in range(2):
                        t = 2 * i + q
                        for c in range(2):
                            last = pe.matmul(work[:, q, 0:W2 + 1], o1T[:, s, c, t * P:(t + 1) * P], wx[:, c, :],
                                             start=(c == 0), stop=(c == 1))
                else:
                    pe.wait_ge(H_made, nth(b, 4, 4))
                    for k in range(2):
                        for c in range(2):
                            last = pe.matmul(work[:, k, :], wa1_wide[:, c, :], o1T[:, s, c, k * 512:(k + 1) * 512],
                                             start=(c == 0), stop=(c == 1))
                last.then_inc(work_full, 1)

            def weigh(b, s, t):
                if t == 0:
                    pe.wait_ge(prT_made, nth(b, NT, NT))
                pe.wait_ge(v_made, nth(b, NT, t + 1))
                for j in range(NT):
                    last = pe.matmul(acc[:, t % 2, 0:W2 + 1], prT[:, s, j, t * P:(t + 1) * P],
                                     H[:, s, j, 1:W2 + 2], start=(j == 0), stop=(j == NT - 1))
                last.then_inc(acc_done, 1)

            def turn_g(b, k):
                pe.wait_ge(g_made, nth(b, 2, k + 1))
                pe.wait_ge(g2T_made, nth(b, 2, k) + 2)
                for q in range(HB):
                    for c in range(2):
                        last = pe.transpose(gT_ps[:, c, q * P:(q + 1) * P], g[:, k, q, c * P:(c + 1) * P], ident[:])
                last.then_inc(gT_done, 1)

            def mlp2(b, k):
                pe.wait_ge(g2T_made, nth(b, 2, k + 1) + 2)
                pe.wait_ge(o2T_made, nth(b, 2, k) + 1)
                for c in range(2):
                    last = pe.matmul(m2_ps[:], w2[:, c, :], g2T[:, c, k * 512:(k + 1) * 512], start=(c == 0),
                                     stop=(c == 1))
                last.then_inc(m2_done, 1)

            def turn_o2(b, k):
                pe.wait_ge(o2T_made, nth(b, 2, k + 1) + 1)
                pe.wait_ge(o2_made, nth(b, 2, k) + 1)
                for q in range(HB):
                    last = pe.transpose(nat_ps[:, q, :], o2T[:, k, q * P:(q + 1) * P], ident[:])
                last.then_inc(nat_done, 1)

            for n in range(JOBS):
                job(0, 0, n)

            def step(b, s, pair, left):
                more = left >= 1
                if more:
                    job(b + 1, 1 - s, 0)
                for t in range(NT):
                    weigh(b, s, t)
                    if more and t + 1 < JOBS:
                        job(b + 1, 1 - s, t + 1)
                    if t == 5:
                        turn_g(b, 0)
                    if t == 6:
                        mlp2(b, 0)
                turn_o2(b, 0)
                turn_g(b, 1)
                mlp2(b, 1)
                turn_o2(b, 1)

            pipelined(pe, B, step, 2)




class Jobs:

    PREP = {3: [("turn", 0)], 4: [("turn", 1)], 5: [("q", 0)], 6: [("q", 1)], 7: [("v", 0)], 8: [("v", 1)],
            9: [("k", 0)], 10: [("k", 1)]}
    FINISH = {1: [("R", 0), ("R", 1)], 2: [("R", 2), ("R", 3)], 15: [("O", 0), ("O", 1)],
              **{u: [("R", u + 1)] for u in range(3, 15)}}

    def __init__(self, B):
        self.B = B
        self.per = len(self.order(True, True))
        self.first = len(self.order(True, False))

    def at(self, u, prep, finish):
        return (self.PREP.get(u, []) if prep else []) + (self.FINISH.get(u, []) if finish else [])

    def order(self, prep, finish):
        return [j for u in range(16) for j in self.at(u, prep, finish)]

    def base(self, b):
        if isinstance(b, int) and b < 0:
            return 0
        if isinstance(b, int) and b == 0:
            return self.first
        if isinstance(b, int) and b == self.B:
            return self.base(self.B - 1) + len(self.order(False, True))
        return (b - 1) * self.per + 2 * self.first

    def number(self, b, job, prep, finish):
        return self.base(b) + self.order(prep, finish).index(job) + 1


def attention_phase(nc, tag, B, N, F, heads, clip_high, ident, Wq, bq, Wk, bk, Wv, bv, Wo, bo, gamma, beta, x_in,
                    h_scratch, x_out):
    NT = N // P
    D = F // heads
    HALF = 512
    UN = 2 * NT
    SCALE = 1.0 / math.sqrt(D)
    jobs = Jobs(B)
    with ExitStack() as ctx:
        ph = Phase(nc, ctx, tag)
        ln = Norm(ph, NT, F, buffers=1)
        wT = ph.sb("wT", [P, 4, F])
        bias_q = ph.sb("bias_q", [P, 1])
        bias_k = ph.sb("bias_k", [P, 1])
        rows_in = ph.sb("rows_in", [P, 4, F])
        hot = ph.sb("hot", [P, UN, D])
        pick = ph.sb("pick", [P, UN, P], F32R)
        hT = ph.sb("hT", [P, N])
        hi = ph.sb("hi", [P, N], F32R)
        lo = ph.sb("lo", [P, N], F32R)
        qs = ph.sb("qs", [P, 2, heads, N], F32R)
        ks = ph.sb("ks", [P, 2, heads, N], F32R)
        vn = ph.sb("vn", [P, 2, NT, F])
        wt = ph.sb("wt", [P, 2, heads, HALF])
        ctxu = ph.sb("ctxu", [P, UN, HALF])
        rec_hi = ph.sb("rec_hi", [P, HALF], F32R)
        rec_lo = ph.sb("rec_lo", [P, HALF], F32R)
        part = ph.sb("part", [P, 2, HALF])
        rec = part[:, 1, :]
        total = ph.sb("total", [P, 2, HALF])
        z = ph.sb("z", [P, NT, F])
        w_in = z[:, 0:4, :]
        z_stats = ph.sb("z_stats", [P, NT, 6])
        z_mv = ph.sb("z_mv", [P, NT, 2])
        z_eps = ph.sb("z_eps", [P, NT])
        z_rstd = ph.sb("z_rstd", [P, NT])
        xe = ph.sb("xe", [P, NT, F])
        scores = ph.ps("scores", [P, heads, HALF])
        ctx_ps = ph.ps("ctx_ps", [P, 2, HALF])
        sums = ph.ps("sums", [P, HALF])
        work = ph.ps("work", [P, HALF])

        w_here = ph.sem("w_here")
        w_turned = ph.sem("w_turned")
        wT_made = ph.sem("wT_made")
        consts_zeroed = ph.sem("consts_zeroed")
        hot_made = ph.sem("hot_made")
        pick_made = ph.sem("pick_made")
        pick_rounded = ph.sem("pick_rounded")
        h_made = ph.sem("h_made")
        h_stored = ph.sem("h_stored")
        work_full = ph.sem("work_full")
        work_used = ph.sem("work_used")
        hi_made = ph.sem("hi_made")
        q_stacked = ph.sem("q_stacked")
        k_stacked = ph.sem("k_stacked")
        qk_done = ph.sem("qk_done")
        exp_made = ph.sem("exp_made")
        wt_made = ph.sem("wt_made")
        pv_done = ph.sem("pv_done")
        ctx_out = ph.sem("ctx_out")
        rec_made = ph.sem("rec_made")
        rec_hi_made = ph.sem("rec_hi_made")
        rec_split = ph.sem("rec_split")
        added = ph.sem("added")
        z_here = ph.sem("z_here")
        xe_here = ph.sem("xe_here")
        z_biased = ph.sem("z_biased")
        xe_biased = ph.sem("xe_biased")
        z_stats_made = ph.sem("z_stats_made")
        z_mv_made = ph.sem("z_mv_made")
        z_eps_added = ph.sem("z_eps_added")
        z_rstd_made = ph.sem("z_rstd_made")
        z_normed = ph.sem("z_normed")
        z_scaled = ph.sem("z_scaled")
        out_made = ph.sem("out_made")
        stored = ph.sem("stored")
        block = ctx.enter_context(nc.Block())
        WEIGHT_DMAS = 10

        def rows(dram, b):
            return dram[b].rearrange("(t p) f -> p t f", p=P)

        def slots(eng, slot):
            slot(0, 0, True, False, True)
            with eng.Fori(0, (B - 2) // 2) as pair:
                slot(pair * 2 + 1, 1, True, True, True)
                slot(pair * 2 + 2, 0, True, True, True)
            slot(B - 1, (B - 1) % 2, False, True, True)
            slot(B, B % 2, False, True, False)

        @block.sync
        def _(sp):
            def load(b):
                if not isinstance(b, int) or b > 0:
                    ph.wait_apart(sp, ln.y_made, nth(b, NT, 0))
                sp.dma_start(ln.x[:, 0, :, :], rows(x_in, b)).then_inc(ln.x_here[0], 16)

            def store_h(b):
                ph.wait_apart(sp, h_made, nth(b, 1, 1))
                sp.dma_start(rows(h_scratch, b), ln.y[:]).then_inc(h_stored, 16)

            def stack(b, s, what, dst, sem, groups, number):
                sp.wait_ge(work_used, number)
                for g, src in enumerate(groups):
                    for h in range(heads):
                        sp.dma_start(dst[g * D:(g + 1) * D, s, h, :].bitcast(F32),
                                     src[h * D:(h + 1) * D, :].bitcast(F32)).then_inc(sem, 16)

            def stacks(b, s, slot_b, prep, finish):
                stack(b, s, "q", qs, q_stacked, (hi, lo, hi, lo), jobs.number(slot_b, ("q", 1), prep, finish))
                stack(b, s, "k", ks, k_stacked, (hi, hi, lo, lo), jobs.number(slot_b, ("k", 1), prep, finish))

            load(0)
            for i, w in enumerate((Wq, Wk, Wv, Wo)):
                sp.dma_start(w_in[:, i, :], w).then_inc(w_here, 16)
            for t, w in ((bias_q, bq), (bias_k, bk)):
                sp.dma_start(t[:], w.rearrange("(p o) -> p o", o=1)).then_inc(w_here, 16)
            for i, w in enumerate((bv, bo, gamma, beta)):
                sp.dma_start(rows_in[:, i, :], w.rearrange("(o f) -> o f", o=1).broadcast_to([P, F])).then_inc(w_here, 16)
            store_h(0)
            stacks(0, 0, -1, True, False)

            def slot(b, s, prep, finish, attend):
                if prep:
                    load(b + 1)
                if finish:
                    ph.wait_apart(sp, out_made, nth(b, 1, 0))
                    ph.wait_apart(sp, stored, nth(b, 16, 0))
                    ph.wait_apart(sp, h_stored, nth(b, 16, 0))
                    sp.dma_start(z[:], rows(h_scratch, b - 1)).then_inc(z_here, 16)
                    sp.dma_start(xe[:], rows(x_in, b - 1)).then_inc(xe_here, 16)
                if prep:
                    store_h(b + 1)
                    stacks(b + 1, 1 - s, b, prep, finish)
                if finish:
                    ph.wait_apart(sp, out_made, nth(b, 1, 0) + 1)
                    sp.dma_start(rows(x_out, b - 1), xe[:]).then_inc(stored, 16)

            slots(sp, slot)
            sp.wait_ge(stored, 16 * B + 16)

        @block.gpsimd
        def _(pool):
            pool.sem_inc(out_made, 1)
            pool.sem_inc(stored, 16)
            pool.memset(hot[:], 0.0).then_inc(consts_zeroed, 1)
            pick_f = ctxu[:, 0:UN * P // HALF, :].rearrange("p a (b m) -> p (a b) m", m=P)
            pool.memset(ctxu[:, 0:UN * P // HALF, :], 0.0).then_inc(consts_zeroed, 1)
            pool.wait_ge(consts_zeroed, 2)
            for u in range(UN):
                pool.memset(hot[:, u, u:u + UN + 1:UN], 1.0).then_inc(hot_made, 1)
            sel = pick_f.rearrange("p u (h d) -> p u h d", h=heads)
            pool.affine_select(out=sel, in_=sel, compare_op=ALU.not_equal, fill=1.0, base=0,
                               pattern=[[-1, UN], [-D, heads], [0, D]], channel_multiplier=1).then_inc(pick_made, 1)
            ln.gpsimd_consts(pool)
            ln.gpsimd(pool, 0)

            def finish_graph(b, number):
                pool.wait_ge(z_here, nth(b, 16, 16))
                pool.wait_ge(w_here, 16 * WEIGHT_DMAS)
                pool.tensor_tensor(z[:], z[:], rows_in[:, 1:2, :].broadcast_to([P, NT, F]), ALU.add).then_inc(z_biased, 1)
                pool.wait_ge(xe_here, nth(b, 16, 16))
                pool.tensor_tensor(xe[:], xe[:], rows_in[:, 3:4, :].broadcast_to([P, NT, F]), ALU.add).then_inc(xe_biased, 1)
                for u in range(2, UN):
                    pool.wait_ge(work_used, number(u))
                    if u >= 4:
                        pool.wait_ge(added, nth(b, UN - 2, u - 3))
                    pool.tensor_tensor(total[:, u % 2, :], total[:, u % 2, :], part[:, u % 2, :],
                                       ALU.add).then_inc(added, 1)
                pool.wait_ge(z_eps_added, nth(b, 1, 1))
                pool.tensor_tensor(z_rstd[:], z_eps[:], ln.minus_half[:], ALU.pow).then_inc(z_rstd_made, 1)

            def slot(b, s, prep, finish, attend):
                if prep:
                    ln.gpsimd(pool, b + 1)
                if finish:
                    finish_graph(b - 1, lambda u: jobs.number(b, ("R", u), prep, True))

            slots(pool, slot)

        @block.vector
        def _(dve):
            dve.wait_ge(pick_made, 1)
            pick_f = ctxu[:, 0:UN * P // HALF, :].rearrange("p a (b m) -> p (a b) m", m=P)
            dve.tensor_copy(pick[:], pick_f).then_inc(pick_rounded, 1)
            dve.wait_ge(w_turned, 1)
            dve.tensor_copy(wT[:], work[:].rearrange("p (i f) -> p i f", i=4)).then_inc(wT_made, 1)

            def norm(b, turned_number):
                if turned_number is not None:
                    dve.wait_ge(work_full, turned_number)
                    dve.wait_ge(h_stored, nth(b, 16, 0))
                ln.vector(dve, b, 0, b)
                dve.wait_ge(ln.y_made, nth(b, NT, NT))
                dve.tensor_scalar(ln.y[:], ln.y[:], 0.0, None, ALU.max).then_inc(h_made, 1)

            def clip(b, u, p):
                dve.wait_ge(exp_made, nth(b, 2 * UN, 2 * u + p + 1))
                c, k = u // 2, u % 2
                w = wt[:, u % 2, 2 * p:2 * p + 2, :]
                dve.scalar_tensor_tensor(
                    out=w, in0=w, scalar=CLIP_LO, in1=clip_high[:, c:c + 1, k * HALF:(k + 1) * HALF].broadcast_to(
                        [P, 2, HALF]), op0=ALU.max, op1=ALU.min).then_inc(wt_made, 1)

            def reciprocals(b):
                dve.wait_ge(pv_done, nth(b, UN, UN))
                dve.reciprocal(rec, sums[:]).then_inc(rec_made, 1)
                dve.wait_ge(rec_made, nth(b, 1, 1))
                dve.tensor_copy(rec_hi[:], rec).then_inc(rec_hi_made, 1)
                dve.wait_ge(rec_hi_made, nth(b, 1, 1))
                dve.tensor_tensor(rec_lo[:], rec, rec_hi[:].bitcast(F32), ALU.subtract).then_inc(rec_split, 1)

            def do_job(job, number, b, s):
                kind, k = job
                if kind in ("q", "k"):
                    j = k + (2 if kind == "k" else 0)
                    dve.wait_ge(hi_made, nth(b + 1, 4, j + 1))
                    cols = slice(k * HALF, (k + 1) * HALF)
                    dve.scalar_tensor_tensor(out=lo[:, cols], in0=work[:], scalar=(bias_q if kind == "q" else bias_k)[:],
                                             in1=hi[:, cols].bitcast(F32), op0=ALU.add,
                                             op1=ALU.subtract).then_inc(work_used, 1)
                elif kind == "v":
                    dve.wait_ge(work_full, number)
                    dve.tensor_tensor(vn[:, 1 - s, 4 * k:4 * k + 4, :], work[:].rearrange("p (t f) -> p t f", f=F),
                                      rows_in[:, 0:1, :].broadcast_to([P, 4, F]), ALU.add).then_inc(work_used, 1)
                elif kind == "R":
                    dve.wait_ge(work_full, number)
                    dve.wait_ge(ctx_out, nth(b - 1, UN, k + 1))
                    dst = total if k < 2 else part
                    if k >= 4:
                        dve.wait_ge(added, nth(b - 1, UN - 2, k - 3))
                    dve.tensor_tensor(dst[:, k % 2, :], work[:], ctxu[:, k, :], ALU.mult).then_inc(work_used, 1)
                elif kind == "O":
                    dve.wait_ge(work_full, number)
                    if k == 0:
                        dve.wait_ge(z_biased, nth(b - 1, 1, 1))
                    zs = z[:, 4 * k:4 * k + 4, :]
                    dve.tensor_tensor(zs, work[:].rearrange("p (t f) -> p t f", f=F), zs, ALU.add).then_inc(work_used, 1)

            def finish_graph(b, number):
                dve.wait_ge(work_used, number)
                for t in range(NT):
                    dve.bn_stats(z_stats[:, t, :], z[:, t, :]).then_inc(z_stats_made, 1)
                ph.wait_apart(dve, z_stats_made, nth(b, NT, NT))
                for t in range(NT):
                    dve.bn_aggr(z_mv[:, t, :], z_stats[:, t, :]).then_inc(z_mv_made, 1)
                dve.wait_ge(z_mv_made, nth(b, NT, NT))
                dve.tensor_scalar(z_eps[:], z_mv[:, :, 1], LN_EPS, None, ALU.add).then_inc(z_eps_added, 1)
                dve.wait_ge(z_rstd_made, nth(b, 1, 1))
                for t in range(NT):
                    dve.tensor_scalar(z[:, t, :], z[:, t, :], z_mv[:, t, 0:1], z_rstd[:, t:t + 1], ALU.subtract,
                                      ALU.mult).then_inc(z_normed, 1)
                dve.wait_ge(z_normed, nth(b, NT, NT))
                dve.tensor_tensor(z[:], z[:], rows_in[:, 2:3, :].broadcast_to([P, NT, F]), ALU.mult).then_inc(z_scaled, 1)
                dve.wait_ge(z_scaled, nth(b, 1, 1))
                dve.wait_ge(xe_biased, nth(b, 1, 1))
                dve.tensor_tensor(xe[:], xe[:], z[:], ALU.add).then_inc(out_made, 1)

            dve.wait_ge(w_here, 16 * WEIGHT_DMAS)
            norm(0, None)
            for u in range(16):
                for j in jobs.at(u, True, False):
                    do_job(j, jobs.number(-1, j, True, False), -1, 1)
            clip(0, 0, 0)
            clip(0, 0, 1)

            def slot(b, s, prep, finish, attend):
                for u in range(UN):
                    if attend and u + 1 < UN:
                        clip(b, u + 1, 0)
                        clip(b, u + 1, 1)
                    elif attend and prep:
                        clip(b + 1, 0, 0)
                        clip(b + 1, 0, 1)
                    if u == 0 and finish:
                        reciprocals(b - 1)
                    if u == 1 and prep:
                        norm(b + 1, jobs.base(b))
                    for j in jobs.at(u, prep, finish):
                        do_job(j, jobs.number(b, j, prep, finish), b, s)
                if finish:
                    finish_graph(b - 1, jobs.number(b, ("O", 1), prep, finish))

            slots(dve, slot)

        @block.scalar
        def _(act):
            def exps(b, u, p):
                act.wait_ge(qk_done, nth(b, 2 * UN, 2 * u + p + 1))
                if not isinstance(b, int) or b > 0 or u >= 2:
                    act.wait_ge(pv_done, nth(b, UN, u - 1))
                act.activation(wt[:, u % 2, 2 * p:2 * p + 2, :], scores[:, 2 * p:2 * p + 2, :], ACT.Exp,
                               scale=SCALE).then_inc(exp_made, 1)

            def take_ctx(b, u):
                act.wait_ge(pv_done, nth(b, UN, u + 1))
                if not isinstance(b, int) or b > 0:
                    act.wait_ge(work_used, number_R(b, u))
                act.activation(ctxu[:, u, :], ctx_ps[:, u % 2, :], ACT.Copy).then_inc(ctx_out, 1)

            def number_R(b, u):
                return jobs.number(b, ("R", u), True, True) if not isinstance(b, int) or b < B - 1 else jobs.number(
                    b, ("R", u), False, True)

            def do_job(job, number, b, s):
                kind, k = job
                cols = slice(k * HALF, (k + 1) * HALF)
                if kind == "turn":
                    act.wait_ge(work_full, number)
                    act.activation(hT[:, cols], work[:], ACT.Copy).then_inc(work_used, 1)
                elif kind in ("q", "k"):
                    act.wait_ge(work_full, number)
                    n = 16 * 4 * heads
                    if kind == "k":
                        act.wait_ge(q_stacked, nth(b + 1, n, n))
                    elif not isinstance(b, int) or b >= 0:
                        act.wait_ge(k_stacked, nth(b + 1, n, 0))
                    act.activation(hi[:, cols], work[:], ACT.Identity,
                                   bias=(bias_q if kind == "q" else bias_k)[:]).then_inc(hi_made, 1)

            act.wait_ge(w_here, 16 * WEIGHT_DMAS)
            for u in range(16):
                for j in jobs.at(u, True, False):
                    do_job(j, jobs.number(-1, j, True, False), -1, 1)
            act.wait_ge(pick_rounded, 1)
            exps(0, 0, 0)
            exps(0, 0, 1)

            def slot(b, s, prep, finish, attend):
                for u in range(UN):
                    if attend and u + 1 < UN:
                        exps(b, u + 1, 0)
                        exps(b, u + 1, 1)
                    elif attend and prep:
                        exps(b + 1, 0, 0)
                        exps(b + 1, 0, 1)
                    for j in jobs.at(u, prep, finish):
                        do_job(j, jobs.number(b, j, prep, finish), b, s)
                    if u >= 1 and attend:
                        take_ctx(b, u - 1)
                if attend:
                    take_ctx(b, UN - 1)

            slots(act, slot)

        @block.tensor
        def _(pe):
            pe.wait_ge(w_here, 16 * WEIGHT_DMAS)
            for i in range(4):
                last = pe.transpose(work[:, i * F:(i + 1) * F], w_in[:, i, :], ident[:])
            last.then_inc(w_turned, 1)
            pe.wait_ge(wT_made, 1)

            def scores_of(b, s, u):
                c, k = u // 2, u % 2
                if u == 0:
                    n = 16 * 4 * heads
                    pe.wait_ge(q_stacked, nth(b, n, n))
                    pe.wait_ge(k_stacked, nth(b, n, n))
                for p in range(2):
                    if not isinstance(b, int) or b > 0 or u > 0:
                        pe.wait_ge(exp_made, nth(b, 2 * UN, 2 * u + p - 1))
                    for h in (2 * p, 2 * p + 1):
                        last = pe.matmul(scores[:, h, :], ks[:, s, h, c * P:(c + 1) * P],
                                         qs[:, s, h, k * HALF:(k + 1) * HALF], start=True, stop=True)
                    last.then_inc(qk_done, 1)

            def context(b, s, u):
                c = u // 2
                pe.wait_ge(wt_made, nth(b, 2 * UN, 2 * u + 2))
                if not isinstance(b, int) or b > 0 or u >= 2:
                    pe.wait_ge(ctx_out, nth(b, UN, u - 1))
                if u == 0 and (not isinstance(b, int) or b > 0):
                    pe.wait_ge(rec_made, nth(b, 1, 0))
                for h in range(heads):
                    pe.matmul(ctx_ps[h * D:(h + 1) * D, u % 2, :], vn[:, s, c, h * D:(h + 1) * D], wt[:, u % 2, h, :],
                              start=True, stop=True, tile_position=(0, h * D))
                for h in range(heads):
                    last = pe.matmul(sums[h * D:(h + 1) * D, :], hot[:, u, :], wt[:, u % 2, h, :], start=(u == 0),
                                     stop=(u == UN - 1), tile_position=(0, h * D))
                last.then_inc(pv_done, 1)

            def do_job(job, number, b, s):
                kind, k = job
                cols = slice(k * HALF, (k + 1) * HALF)
                if not isinstance(number, int) or number > 1:
                    pe.wait_ge(work_used, number - 1)
                if kind == "turn":
                    if k == 0:
                        pe.wait_ge(h_made, nth(b + 1, 1, 1))
                    for t in range(4):
                        last = pe.transpose(work[:, t * P:(t + 1) * P], ln.y[:, 4 * k + t, :], ident[:])
                elif kind in ("q", "k"):
                    last = pe.matmul(work[:], wT[:, 0 if kind == "q" else 1, :], hT[:, cols], start=True, stop=True)
                elif kind == "v":
                    for t in range(4):
                        last = pe.matmul(work[:, t * P:(t + 1) * P], hT[:, (4 * k + t) * P:(4 * k + t + 1) * P],
                                         wT[:, 2, :], start=True, stop=True)
                elif kind == "R":
                    if k == 0:
                        pe.wait_ge(rec_split, nth(b - 1, 1, 1))
                    pe.matmul(work[:], pick[:, k, :], rec_hi[:], start=True, stop=False)
                    last = pe.matmul(work[:], pick[:, k, :], rec_lo[:], start=False, stop=True)
                else:
                    if k == 0:
                        pe.wait_ge(added, nth(b - 1, UN - 2, UN - 2))
                    tt = total[:].rearrange("p a n -> p (a n)")
                    for t in range(4):
                        last = pe.matmul(work[:, t * P:(t + 1) * P], tt[:, (4 * k + t) * P:(4 * k + t + 1) * P],
                                         wT[:, 3, :], start=True, stop=True)
                last.then_inc(work_full, 1)

            for u in range(16):
                for j in jobs.at(u, True, False):
                    do_job(j, jobs.number(-1, j, True, False), -1, 1)
            pe.wait_ge(hot_made, UN)
            pe.wait_ge(pick_rounded, 1)
            scores_of(0, 0, 0)

            def slot(b, s, prep, finish, attend):
                for u in range(UN):
                    if attend and u + 1 < UN:
                        scores_of(b, s, u + 1)
                    elif attend and prep:
                        scores_of(b + 1, 1 - s, 0)
                    if attend:
                        context(b, s, u)
                    for j in jobs.at(u, prep, finish):
                        do_job(j, jobs.number(b, j, prep, finish), b, s)

            slots(pe, slot)




def program(nc, x, adj, L0, L1, L2, L3, out):
    B, N, F = x.shape
    NT = N // P
    x1 = nc.dram_tensor("x1", (B, N, F), F32).ap()
    x2 = nc.dram_tensor("x2", (B, N, F), F32).ap()
    x3 = nc.dram_tensor("x3", (B, N, F), F32).ap()
    h0 = nc.dram_tensor("h0", (B, N, F), F32).ap()
    o2 = nc.dram_tensor("o2", (B, N, F), F32).ap()
    o2T = nc.dram_tensor("o2T", (B, F, N), F32).ap()
    mlp1_w, mlp1_b, mlp2_w, mlp2_b, W_fc, a_fc, W_hand, a_hand = L3
    with ExitStack() as ctx:
        ident = ctx.enter_context(nc.sbuf_tensor("ident", [P, P], F32))
        with ExitStack() as first:
            clip_high = first.enter_context(nc.sbuf_tensor("clip_high", [P, NT, N], F32))
            masks_phase(nc, adj, clip_high, None, ident, NT, N)
            attention_phase(nc, "att", B, N, F, HEADS, clip_high, ident, *L0, x, h0, x1)
        edge_bias = ctx.enter_context(nc.sbuf_tensor("edge_bias", [P, NT, N], BF16))
        masks_phase(nc, adj, None, edge_bias, ident, NT, N)
        gat_phase(nc, "gat1", B, N, F, edge_bias, ident, *L1, x1, x2, "elu")
        gat_phase(nc, "gat2", B, N, F, edge_bias, ident, *L2, x2, x3, "plain")
        fc_phase(nc, "fc", B, N, F, ident, mlp1_w, mlp1_b, W_fc, a_fc, mlp2_w, mlp2_b, x3, o2T, o2)
        gat_phase(nc, "hand", B, N, F, edge_bias, ident, W_hand, a_hand, x3, out, "hand", o2, o2T)


HEADS = 4
_L0 = ["Wq", "bq", "Wk", "bk", "Wv", "bv", "Wo", "bo", "gamma", "beta"]
_L3 = ["mlp1_w", "mlp1_b", "mlp2_w", "mlp2_b", "W_fc", "a_fc", "W_hand", "a_hand"]
_INS = (["x", "adj"] + ["L0_gnn_" + n for n in _L0] + ["L1_gnn_W", "L1_gnn_a", "L2_gnn_W", "L2_gnn_a"]
        + ["L3_gnn_" + n for n in _L3])


def kernel(**inputs):
    import numpy as np
    import concourse.bacc as bacc
    from concourse.bass_utils import run_bass_kernel_spmd

    nc = bacc.Bacc("TRN2", target_bir_lowering=False, num_devices=1)
    arrays, args = {}, {}
    for name in _INS:
        a = np.ascontiguousarray(inputs[name])
        arrays["in_" + name] = a
        args[name] = nc.dram_tensor("in_" + name, a.shape, mybir.dt.from_np(a.dtype), kind="ExternalInput").ap()
    out = nc.dram_tensor("out_x", inputs["x"].shape, F32, kind="ExternalOutput").ap()
    program(nc, args["x"], args["adj"], [args["L0_gnn_" + n] for n in _L0],
            [args["L1_gnn_W"], args["L1_gnn_a"]], [args["L2_gnn_W"], args["L2_gnn_a"]],
            [args["L3_gnn_" + n] for n in _L3], out)
    r = run_bass_kernel_spmd(nc, [arrays], core_ids=[0])
    return r.results[0]["out_x"]
```

```python
import math
from contextlib import ExitStack

import concourse.bass as bass
from concourse import mybir

F32 = mybir.dt.float32
F32R = mybir.dt.float32r
BF16 = mybir.dt.bfloat16
I32 = mybir.dt.int32
ALU = mybir.AluOpType
ACT = mybir.ActivationFunctionType
AX_X = mybir.AxisListType.X

P = 128
LN_EPS = 1e-5
SLOPE = 0.2
FAR = -1.0e30
CLIP_LO, CLIP_HI = math.exp(-10.0), math.exp(10.0)


def nth(b, per, k):
    return b * per + k


class Phase:

    def __init__(self, nc, ctx, tag):
        self.nc, self.ctx, self.tag = nc, ctx, tag
        self.sems = []
        self.passed = self.sem("passed")
        ctx.callback(self.clear)

    def clear(self):
        self.nc.clear_and_free_semaphores(self.sems)
        self.nc.all_engine_barrier()

    def wait_apart(self, eng, sem, value):
        eng.wait_ge(sem, value)
        eng.sem_inc(self.passed, 1)

    def sb(self, name, shape, dt=F32):
        return self.ctx.enter_context(self.nc.sbuf_tensor(f"{self.tag}_{name}", shape, dt))

    def ps(self, name, shape, dt=F32):
        return self.ctx.enter_context(self.nc.psum_tensor(f"{self.tag}_{name}", shape, dt))

    def sem(self, name):
        self.sems.append(self.nc.alloc_semaphore(f"{self.tag}_{name}"))
        return self.sems[-1]


def pipelined(eng, batches, step, lead):
    looped = batches - lead
    assert looped % 2 == 0 and looped >= 2
    with eng.Fori(0, looped // 2) as pair:
        for s in (0, 1):
            step(pair * 2 + s, s, pair, lead)
    for b in range(looped, batches):
        step(b, b % 2, b // 2, batches - 1 - b)




def masks_phase(nc, adj, clip_high, edge_bias, ident, NT, N):
    with ExitStack() as ctx:
        ph = Phase(nc, ctx, "high" if clip_high is not None else "bias")
        adj_in = ph.sb("adj_in", [P, NT, N], I32)
        adj_here = ph.sem("adj_here")
        bias_made = ph.sem("bias_made")
        if clip_high is not None:
            edge = ph.sb("edge", [P, NT, N], BF16)
            identb = ph.sb("identb", [P, P], BF16)
            turned = ph.ps("turned", [P, 2, 2 * N], BF16)
            zeroed = ph.sem("zeroed")
            ident_made = ph.sem("ident_made")
            edge_made = ph.sem("edge_made")
            turn_done = ph.sem("turn_done")
            high_made = ph.sem("high_made")
        block = ctx.enter_context(nc.Block())

        @block.sync
        def _(sp):
            for t in range(NT):
                sp.dma_start(adj_in[:, t, :], adj[t * P:(t + 1) * P, :]).then_inc(adj_here, 16)

        if clip_high is not None:
            @block.gpsimd
            def _(pool):
                pool.memset(ident[:], 0.0).then_inc(zeroed, 1)
                pool.memset(identb[:], 0.0).then_inc(zeroed, 1)
                pool.wait_ge(zeroed, 2)
                for m in (ident, identb):
                    pool.affine_select(out=m[:], in_=m[:], compare_op=ALU.not_equal, fill=1.0, base=0,
                                       pattern=[[-1, P]], channel_multiplier=1).then_inc(ident_made, 1)

            @block.tensor
            def _(pe):
                pe.wait_ge(ident_made, 2)
                pe.wait_ge(edge_made, NT)
                for c in range(NT):
                    if c >= 2:
                        pe.wait_ge(high_made, c - 1)
                    for t in range(NT):
                        last = pe.transpose(turned[:, c % 2, t * P:(t + 1) * P],
                                            edge[:, t, c * P:(c + 1) * P], identb[:])
                    last.then_inc(turn_done, 1)

        @block.vector
        def _(dve):
            dve.wait_ge(adj_here, 16 * NT)
            for t in range(NT):
                if clip_high is None:
                    dve.tensor_scalar(edge_bias[:, t, :], adj_in[:, t, :], 0, FAR, ALU.is_le,
                                      ALU.mult).then_inc(bias_made, 1)
                else:
                    dve.tensor_scalar(edge[:, t, :], adj_in[:, t, :], 0, None, ALU.is_gt).then_inc(edge_made, 1)
            if clip_high is not None:
                for c in range(NT):
                    dve.wait_ge(turn_done, c + 1)
                    dve.tensor_scalar(clip_high[:, c, :], turned[:, c % 2, 0:N], CLIP_HI - CLIP_LO, CLIP_LO, ALU.mult,
                                      ALU.add).then_inc(high_made, 1)






class Norm:

    def __init__(self, ph, NT, F, buffers=2):
        self.ph, self.NT, self.F = ph, NT, F
        self.x = ph.sb("ln_x", [P, buffers, NT, F])
        self.stats = ph.sb("ln_stats", [P, NT, 6])
        self.mv = ph.sb("ln_mean_var", [P, NT, 2])
        self.var_eps = ph.sb("ln_var_eps", [P, NT])
        self.rstd = ph.sb("ln_rstd", [P, NT])
        self.minus_half = ph.sb("ln_minus_half", [P, NT])
        self.nmr = ph.sb("ln_minus_mean_rstd", [P, NT])
        self.y = ph.sb("ln_y", [P, NT, F])
        self.x_here = [ph.sem(f"x_here{i}") for i in range(buffers)]
        self.stats_made = ph.sem("ln_stats_made")
        self.mv_made = ph.sem("ln_mv_made")
        self.eps_added = ph.sem("ln_eps_added")
        self.rstd_made = ph.sem("ln_rstd_made")
        self.const_made = ph.sem("ln_const_made")
        self.nmr_made = ph.sem("ln_nmr_made")
        self.y_made = ph.sem("ln_y_made")

    def vector(self, dve, b, s, turn):
        self.statistics(dve, b, s, turn)
        self.scale(dve, b, s)

    def statistics(self, dve, b, s, turn):
        NT = self.NT
        dve.wait_ge(self.x_here[s], nth(turn, 16, 16))
        for t in range(NT):
            dve.bn_stats(self.stats[:, t, :], self.x[:, s, t, :]).then_inc(self.stats_made, 1)
        self.ph.wait_apart(dve, self.stats_made, nth(b, NT, NT))
        for t in range(NT):
            dve.bn_aggr(self.mv[:, t, :], self.stats[:, t, :]).then_inc(self.mv_made, 1)
        dve.wait_ge(self.mv_made, nth(b, NT, NT))
        dve.tensor_scalar(self.var_eps[:], self.mv[:, :, 1], LN_EPS, None, ALU.add).then_inc(self.eps_added, 1)

    def scale(self, dve, b, s):
        NT = self.NT
        dve.wait_ge(self.rstd_made, nth(b, 1, 1))
        for t in range(NT):
            dve.tensor_scalar(self.y[:, t, :], self.x[:, s, t, :], self.mv[:, t, 0:1], self.rstd[:, t:t + 1],
                              ALU.subtract, ALU.mult).then_inc(self.y_made, 1)

    def minus_mean(self, dve, b):
        dve.wait_ge(self.rstd_made, nth(b, 1, 1))
        dve.scalar_tensor_tensor(out=self.nmr[:], in0=self.mv[:, :, 0], scalar=-1.0, in1=self.rstd[:],
                                 op0=ALU.mult, op1=ALU.mult).then_inc(self.nmr_made, 1)

    def gpsimd_consts(self, pool):
        pool.memset(self.minus_half[:], -0.5).then_inc(self.const_made, 1)
        pool.wait_ge(self.const_made, 1)

    def gpsimd(self, pool, b):
        pool.wait_ge(self.eps_added, nth(b, 1, 1))
        pool.tensor_tensor(self.rstd[:], self.var_eps[:], self.minus_half[:], ALU.pow).then_inc(self.rstd_made, 1)




def gat_phase(nc, tag, B, N, F, edge_bias, ident, W, a, x_in, x_out, kind, resid=None, hT_in=None):
    NT = N // P
    HB = NT // 2
    FE = F + 1
    normed = kind != "hand"
    TB = NT
    with ExitStack() as ctx:
        ph = Phase(nc, ctx, tag)
        wa = ph.sb("wa", [P, FE + P])
        w_in = ph.sb("w_in", [P, F])
        wT = ph.sb("wT", [P, F])
        a_in = ph.sb("a_in", [F, 2])
        wa2 = ph.sb("wa2", [P, 1])
        ln = Norm(ph, NT, F, buffers=1)
        x = ph.sb("x", [P, 2, NT, F])
        x_here = [ph.sem("x_again0"), ph.sem("x_again1")]
        if not normed:
            rs = ph.sb("rs", [P, 2, NT, F])
            rs_here = [ph.sem("rs_here0"), ph.sem("rs_here1")]
            hT_here = ph.sem("hT_here")
        hT = ph.sb("hT", [P, N])
        H = ph.sb("H", [P, 2, NT, FE])
        s2row = ph.sb("s2row", [P, N])
        s2row4 = ph.sb("s2row4", [P, N])
        y = ph.sb("y", [P, NT, N])
        u = ph.sb("u", [P, NT])
        s1m4 = ph.sb("s1m4", [P, NT])
        z = ph.sb("z", [P, NT])
        mx = ph.sb("mx", [P, NT])
        shift = ph.sb("shift", [P, NT])
        t_buf = ph.sb("t_buf", [P, TB, N])
        pr = ph.sb("pr", [P, NT, N])
        den = ph.sb("den", [P, 2, NT])
        rden = ph.sb("rden", [P, NT])
        prT = ph.sb("prT", [P, 2, NT, P])
        v = ph.sb("v", [P, 2, HB, F])
        vneg = ph.sb("vneg", [P, 2, HB, F])
        vexp = ph.sb("vexp", [P, 2, HB, F])
        res = ph.sb("res", [P, 2, HB, F])
        minus1 = ph.sb("minus1", [P, 1])
        minus1_made = ph.sem("minus1_made")
        work = ph.ps("work", [P, 2, 512])
        turned = ph.ps("turned", [P, 2, N])
        acc = ph.ps("acc", [P, 2, HB, F])

        w_here = ph.sem("w_here")
        w_turned = ph.sem("w_turned")
        wT_made = ph.sem("wT_made")
        wa_done = ph.sem("wa_done")
        wa_copied = ph.sem("wa_copied")
        wext_made = ph.sem("wext_made")
        work_full = ph.sem("work_full")
        hT_made = ph.sem("hT_made")
        s2_made = ph.sem("s2_made")
        H_made = ph.sem("H_made")
        y_max = ph.sem("y_max")
        s1m4_made = ph.sem("s1m4_made")
        z_made = ph.sem("z_made")
        mx_made = ph.sem("mx_made")
        shift_made = ph.sem("shift_made")
        t_made = ph.sem("t_made")
        pr_made = ph.sem("pr_made")
        turn_done = ph.sem("turn_done")
        prT_made = ph.sem("prT_made")
        weighed = ph.sem("weighed")
        rden_made = ph.sem("rden_made")
        v_made = ph.sem("v_made")
        vneg_made = ph.sem("vneg_made")
        vexp_made = ph.sem("vexp_made")
        vexp2_made = ph.sem("vexp2_made")
        sum_made = ph.sem("sum_made")
        sum2_made = ph.sem("sum2_made")
        res_made = ph.sem("res_made")
        stored = [ph.sem("stored0"), ph.sem("stored1")]
        block = ctx.enter_context(nc.Block())
        JOBS = 5 if normed else 4
        H_JOBS = [(0, 3), (3, 3), (6, 2)]
        NPOST = {"plain": 0, "elu": 1, "hand": 1}[kind]

        def rows(dram, b):
            return dram[b].rearrange("(t p) f -> p t f", p=P)

        ORDER = "e2 x0 x1 e3 h x2 e4 s x3 v0 e5 x4 x5 e6 x6 e7 x7 H n0 n1 v1"

        @block.sync
        def _(sp):
            sp.dma_start(w_in[:], W).then_inc(w_here, 16)
            for k in range(2):
                sp.dma_start(a_in[:, k:k + 1], a[k * F:(k + 1) * F, :]).then_inc(w_here, 16)

            def load(b, s):
                sp.dma_start(x[:, s, :, :], rows(x_in, b)).then_inc(x_here[s], 16)
                if not normed:
                    sp.dma_start(rs[:, s, :, :], rows(resid, b)).then_inc(rs_here[s], 16)

            def load_input(b):
                first = isinstance(b, int) and b == 0
                if normed:
                    if not first:
                        ph.wait_apart(sp, ln.y_made, nth(b, NT, 0))
                    sp.dma_start(ln.x[:, 0, :, :], rows(x_in, b)).then_inc(ln.x_here[0], 16)
                else:
                    if not first:
                        ph.wait_apart(sp, work_full, nth(b, JOBS, 0))
                    sp.dma_start(hT[:], hT_in[b]).then_inc(hT_here, 16)

            load_input(0)
            load(0, 0)
            load_input(1)
            load(1, 1)
            load_input(2)

            def step(b, s, pair, left):
                for k in range(2):
                    ph.wait_apart(sp, res_made, nth(b, 2, k + 1))
                    sp.dma_start(rows(x_out, b)[:, k * HB:(k + 1) * HB, :], res[:, k, :, :]).then_inc(stored[k], 16)
                    if k == 0 and left >= 3:
                        load_input(b + 3)
                if left >= 2:
                    load(b + 2, s)

            pipelined(sp, B, step, 4)
            for k in range(2):
                sp.wait_ge(stored[k], 16 * B + 16)

        @block.gpsimd
        def _(pool):
            pool.sem_inc(weighed, 2)
            pool.sem_inc(prT_made, 2)
            pool.sem_inc(v_made, NT)
            pool.sem_inc(rden_made, 1)
            for k in range(2):
                pool.sem_inc(stored[k], 16)
            if kind == "hand":
                pool.memset(minus1[:], -1.0).then_inc(minus1_made, 1)
            if normed:
                ln.gpsimd_consts(pool)
                ln.gpsimd(pool, 0)
                ln.gpsimd(pool, 1)

                def step(b, s, pair, left):
                    if left >= 2:
                        ln.gpsimd(pool, b + 2)

                pipelined(pool, B, step, 2)

        @block.vector
        def _(dve):
            dve.wait_ge(w_here, 48)
            dve.wait_ge(w_turned, 1)
            dve.tensor_copy(wT[:], work[:, 0, 0:F]).then_inc(wT_made, 1)
            dve.tensor_copy(wa[:, 0:F], w_in[:]).then_inc(wext_made, 1)
            dve.wait_ge(wa_done, 1)
            dve.tensor_copy(wa2[:], work[:, 1, 1:2]).then_inc(wa_copied, 1)
            dve.tensor_copy(wa[:, F:FE], work[:, 1, 0:1]).then_inc(wext_made, 1)
            dve.wait_ge(wa_copied, 1)
            dve.tensor_copy(wa[:, FE:FE + P], wa2[:].broadcast_to([P, P])).then_inc(wext_made, 1)

            def maxima(b, t0, t1):
                if t0 == 0 and (not isinstance(b, int) or b > 0):
                    dve.wait_ge(t_made, nth(b, NT, 0))
                if t0 == 0:
                    ph.wait_apart(dve, s2_made, nth(b, 2, 2))
                for t in range(t0, t1):
                    dve.tensor_tensor_reduce(y[:, t, :], s2row[:], edge_bias[:, t, :], 1.0, -3.0e38, ALU.add,
                                             ALU.max, u[:, t:t + 1]).then_inc(y_max, 1)

            def shifts(b, s):
                dve.wait_ge(H_made, nth(b, 3, 3))
                if not isinstance(b, int) or b > 0:
                    dve.wait_ge(t_made, nth(b, NT, 0))
                s1 = H[:, s, :, F]
                dve.tensor_scalar(s1m4[:], s1, -4.0, None, ALU.mult).then_inc(s1m4_made, 1)
                dve.wait_ge(y_max, nth(b, NT, NT))
                dve.tensor_tensor(z[:], s1, u[:], ALU.add).then_inc(z_made, 1)
                dve.wait_ge(z_made, nth(b, 1, 1))
                dve.scalar_tensor_tensor(out=mx[:], in0=z[:], scalar=SLOPE, in1=z[:], op0=ALU.mult,
                                         op1=ALU.max).then_inc(mx_made, 1)
                dve.wait_ge(mx_made, nth(b, 1, 1))
                if not isinstance(b, int) or b > 0:
                    dve.wait_ge(pr_made, nth(b, NT, 0))
                dve.tensor_tensor(shift[:], s1, mx[:], ALU.subtract).then_inc(shift_made, 1)
                dve.wait_ge(s1m4_made, nth(b, 1, 1))

            def t_tile(b, t):
                if not isinstance(b, int) or b > 0 or t >= TB:
                    dve.wait_ge(pr_made, nth(b, NT, t + 1 - TB))
                dve.scalar_tensor_tensor(out=t_buf[:, t % TB, :], in0=s2row4[:], scalar=s1m4[:, t:t + 1],
                                         in1=y[:, t, :], op0=ALU.max, op1=ALU.add).then_inc(t_made, 1)

            def divide(b, s, k):
                if k == 0:
                    dve.wait_ge(pr_made, nth(b, NT, NT))
                    dve.reciprocal(rden[:], den[:, s, :]).then_inc(rden_made, 1)
                    dve.wait_ge(rden_made, nth(b, 1, 1) + 1)
                dve.wait_ge(weighed, nth(b, NT, (k + 1) * HB) + 2)
                dve.wait_ge(stored[k], nth(b, 16, 16))
                for q in range(HB):
                    t = k * HB + q
                    dve.tensor_scalar(v[:, k, q, :], acc[:, k, q, :], rden[:, t:t + 1], None,
                                      ALU.mult).then_inc(v_made, 1)
                dve.wait_ge(v_made, nth(b, NT, (k + 1) * HB) + NT)
                if kind != "plain":
                    dve.tensor_scalar(vneg[:, k, :, :], v[:, k, :, :], 0.0, None, ALU.min).then_inc(vneg_made, 1)

            def post(b, s, half, k):
                xs = x[:, s, k * HB:(k + 1) * HB, :]
                if k == 0:
                    dve.wait_ge(x_here[s], nth(half, 16, 16))
                if kind == "plain":
                    dve.tensor_tensor(res[:, k, :, :], v[:, k, :, :], xs, ALU.add).then_inc(res_made, 1)
                    return
                dve.wait_ge(vexp_made, nth(b, 2, k + 1))
                dve.scalar_tensor_tensor(out=v[:, k, :, :], in0=v[:, k, :, :], scalar=0.0, in1=vexp[:, k, :, :],
                                         op0=ALU.max, op1=ALU.add).then_inc(sum_made, 1)
                dve.wait_ge(sum_made, nth(b, 2, k + 1))
                if kind == "elu":
                    dve.scalar_tensor_tensor(out=res[:, k, :, :], in0=v[:, k, :, :], scalar=-1.0, in1=xs,
                                             op0=ALU.add, op1=ALU.add).then_inc(res_made, 1)
                    return
                if k == 0:
                    dve.wait_ge(rs_here[s], nth(half, 16, 16))
                dve.scalar_tensor_tensor(out=vneg[:, k, :, :], in0=v[:, k, :, :], scalar=-1.0,
                                         in1=rs[:, s, k * HB:(k + 1) * HB, :], op0=ALU.add,
                                         op1=ALU.add).then_inc(sum2_made, 1)
                dve.wait_ge(sum2_made, nth(b, 2, k + 1))
                dve.scalar_tensor_tensor(out=res[:, k, :, :], in0=vneg[:, k, :, :], scalar=0.0, in1=xs,
                                         op0=ALU.max, op1=ALU.add).then_inc(res_made, 1)

            def norm(b):
                if not isinstance(b, int) or b > 0:
                    dve.wait_ge(work_full, nth(b, JOBS, 1 - JOBS))
                ln.scale(dve, b, 0)

            if normed:
                ln.statistics(dve, 0, 0, 0)
                norm(0)
                ln.statistics(dve, 1, 0, 1)
                norm(1)
            maxima(0, 0, NT)
            shifts(0, 0)
            for t in range(NT):
                t_tile(0, t)
            maxima(1, 0, NT)
            shifts(1, 1)
            t_tile(1, 0)

            def step(b, s, pair, left):
                if left >= 2 and normed:
                    ln.statistics(dve, b + 2, 0, b + 2)
                if left >= 1:
                    for t in range(1, 3):
                        t_tile(b + 1, t)
                if left >= 2 and normed:
                    norm(b + 2)
                if left >= 1:
                    for t in range(3, NT):
                        t_tile(b + 1, t)
                divide(b, s, 0)
                if left >= 2:
                    maxima(b + 2, 0, 3)
                post(b, s, pair, 0)
                if left >= 2:
                    maxima(b + 2, 3, NT)
                    shifts(b + 2, s)
                    t_tile(b + 2, 0)
                divide(b, s, 1)
                post(b, s, pair, 1)

            pipelined(dve, B, step, 2)

        @block.scalar
        def _(act):
            whole = work[:].rearrange("p a n -> p (a n)")

            def take_hT(b):
                if normed:
                    act.wait_ge(work_full, nth(b, JOBS, 1))
                    act.activation(hT[:], whole, ACT.Relu).then_inc(hT_made, 1)

            def take_s2(b):
                act.wait_ge(work_full, nth(b, JOBS, JOBS - 3))
                if not isinstance(b, int) or b > 0:
                    act.wait_ge(t_made, nth(b, NT, 0))
                act.activation(s2row[:], whole, ACT.Copy).then_inc(s2_made, 1)
                act.activation(s2row4[:], whole, ACT.Copy, scale=4.0).then_inc(s2_made, 1)

            def take_H(b, s):
                for i, (t0, n) in enumerate(H_JOBS):
                    act.wait_ge(work_full, nth(b, JOBS, JOBS - 2 + i))
                    act.activation(H[:, s, t0:t0 + n, :],
                                   work[:, i % 2, 0:n * FE].rearrange("p (t f) -> p t f", t=n),
                                   ACT.Copy).then_inc(H_made, 1)

            def exps(b, s, t):
                act.wait_ge(t_made, nth(b, NT, t + 1))
                if t == 0:
                    act.wait_ge(shift_made, nth(b, 1, 1))
                    if not isinstance(b, int) or b > 0:
                        act.wait_ge(rden_made, nth(b, 1, 0))
                if not isinstance(b, int) or b > 0:
                    act.wait_ge(turn_done, nth(b, NT, t + 1 - NT))
                act.activation(pr[:, t, :], t_buf[:, t % TB, :], ACT.Exp, bias=shift[:, t:t + 1], scale=SLOPE,
                               accum_out=den[:, s, t:t + 1]).then_inc(pr_made, 1)

            def evac(b, t):
                act.wait_ge(turn_done, nth(b, NT, t + 1))
                act.wait_ge(weighed, nth(b, NT, t + 1))
                act.activation(prT[:, t % 2, :, :].rearrange("p a n -> p (a n)"), turned[:, t % 2, :],
                               ACT.Copy).then_inc(prT_made, 1)

            def vexp_half(b, k):
                if kind == "plain":
                    return
                act.wait_ge(vneg_made, nth(b, 2, k + 1))
                act.activation(vexp[:, k, :, :], vneg[:, k, :, :], ACT.Exp).then_inc(
                    vexp_made if kind == "elu" else vexp2_made, 1)
                if kind == "hand":
                    act.wait_ge(vexp2_made, nth(b, 2, k + 1))
                    act.activation(vexp[:, k, :, :], vexp[:, k, :, :], ACT.Exp, bias=minus1[:]).then_inc(vexp_made, 1)

            act.wait_ge(wext_made, 3)
            if kind == "hand":
                act.wait_ge(minus1_made, 1)
            take_hT(0)
            take_s2(0)
            take_H(0, 0)
            for t in range(NT):
                exps(0, 0, t)
            take_hT(1)
            take_s2(1)
            take_H(1, 1)
            evac(0, 0)
            evac(0, 1)

            def step(b, s, pair, left):
                for what in ORDER.split():
                    n = int(what[1:] or 0)
                    if what[0] == "e":
                        evac(b, n)
                    elif what[0] == "n" and left >= 1:
                        evac(b + 1, n)
                    elif what[0] == "v":
                        vexp_half(b, n)
                    elif what[0] == "x" and left >= 1:
                        exps(b + 1, 1 - s, n)
                    elif what == "h" and left >= 2:
                        take_hT(b + 2)
                    elif what == "s" and left >= 2:
                        take_s2(b + 2)
                    elif what == "H" and left >= 2:
                        take_H(b + 2, s)

            pipelined(act, B, step, 2)

        @block.tensor
        def _(pe):
            pe.wait_ge(w_here, 48)
            pe.transpose(work[:, 0, 0:P], w_in[:], ident[:]).then_inc(w_turned, 1)
            pe.wait_ge(wT_made, 1)
            pe.matmul(work[:, 1, 0:2], wT[:], a_in[:], start=True, stop=True).then_inc(wa_done, 1)
            pe.wait_ge(wext_made, 3)

            def turn_y(b):
                if normed:
                    pe.wait_ge(ln.y_made, nth(b, NT, NT))
                    if not isinstance(b, int) or b > 0:
                        pe.wait_ge(H_made, nth(b, 3, 0))
                    for t in range(NT):
                        last = pe.transpose(work[:, t // 4, (t % 4) * P:(t % 4 + 1) * P], ln.y[:, t, :], ident[:])
                    last.then_inc(work_full, 1)

            def s2_product(b):
                if normed:
                    pe.wait_ge(hT_made, nth(b, 1, 1))
                else:
                    pe.wait_ge(hT_here, nth(b, 16, 16))
                    if not isinstance(b, int) or b > 0:
                        pe.wait_ge(H_made, nth(b, 3, 0))
                for k in range(2):
                    last = pe.matmul(work[:, k, :], wa[:, FE:FE + P], hT[:, k * 512:(k + 1) * 512], start=True,
                                     stop=True)
                last.then_inc(work_full, 1)

            def H_products(b):
                for i, (t0, n) in enumerate(H_JOBS):
                    if i == 0:
                        pe.wait_ge(s2_made, nth(b, 2, 2))
                    if i == 2:
                        pe.wait_ge(H_made, nth(b, 3, 1))
                    for t in range(t0, t0 + n):
                        last = pe.matmul(work[:, i % 2, (t - t0) * FE:(t - t0 + 1) * FE], hT[:, t * P:(t + 1) * P],
                                         wa[:, 0:FE], start=True, stop=True)
                    last.then_inc(work_full, 1)

            def turn(b, t):
                pe.wait_ge(pr_made, nth(b, NT, t + 1))
                pe.wait_ge(prT_made, nth(b, NT, t + 1))
                for j in range(NT):
                    last = pe.transpose(turned[:, t % 2, j * P:(j + 1) * P], pr[:, t, j * P:(j + 1) * P], ident[:])
                last.then_inc(turn_done, 1)

            def weigh(b, s, t):
                k, q = t // HB, t % HB
                pe.wait_ge(prT_made, nth(b, NT, t + 1) + 2)
                if q == 0:
                    pe.wait_ge(v_made, nth(b, NT, (k + 1) * HB))
                for j in range(NT):
                    last = pe.matmul(acc[:, k, q, :], prT[:, t % 2, j, :], H[:, s, j, 0:F], start=(j == 0),
                                     stop=(j == NT - 1))
                last.then_inc(weighed, 1)

            for b in range(2):
                turn_y(b)
                s2_product(b)
                H_products(b)

            def step(b, s, pair, left):
                turn(b, 0)
                for t in range(NT):
                    if t + 1 < NT:
                        turn(b, t + 1)
                    if left >= 2 and t == 3:
                        turn_y(b + 2)
                    if left >= 2 and t == 4:
                        s2_product(b + 2)
                    weigh(b, s, t)
                if left >= 2:
                    H_products(b + 2)

            pipelined(pe, B, step, 2)




def fc_phase(nc, tag, B, N, F, ident, mlp1_w, mlp1_b, W, a, mlp2_w, mlp2_b, x_in, hT_out, h_out):
    NT = N // P
    HB = NT // 2
    W2 = 2 * F
    with ExitStack() as ctx:
        ph = Phase(nc, ctx, tag)
        ln = Norm(ph, NT, F)
        w1 = ph.sb("w1", [P, W2])
        b1 = ph.sb("b1", [P, 2])
        w_in = ph.sb("w_in", [P, 2, W2])
        wT = ph.sb("wT", [P, 2, W2])
        a_in = ph.sb("a_in", [P, 2, 2])
        wx = ph.sb("wx", [P, 2, W2 + 1])
        wa1 = ph.sb("wa1", [P, 2, 1])
        wa1_wide = ph.sb("wa1_wide", [P, 2, P])
        w2 = ph.sb("w2", [P, 2, F])
        b2 = ph.sb("b2", [P, 1])
        minus1 = ph.sb("minus1", [P, 1])
        hT = ph.sb("hT", [P, N])
        o1T = ph.sb("o1T", [P, 2, 2, N])
        H = ph.sb("H", [P, 2, NT, W2 + 2])
        f2max = ph.sb("f2max", [P, 1])
        G = ph.sb("G", [P, 1])
        mG8 = ph.sb("mG8", [P, 1])
        mG2 = ph.sb("mG2", [P, 1])
        E = ph.sb("E", [P, NT])
        D = ph.sb("D", [P, NT])
        F_raw = ph.sb("F_raw", [P, N])
        F_row = ph.sb("F_row", [P, N])
        prT = ph.sb("prT", [P, 2, NT, N])
        rden = ph.sb("rden", [P, NT])
        v = ph.sb("v", [P, 2, HB, W2])
        vexp = ph.sb("vexp", [P, 2, HB, W2])
        g = ph.sb("g", [P, 2, HB, W2])
        g2T = ph.sb("g2T", [P, 2, N])
        o2T = ph.sb("o2T", [P, 2, 512])
        o2 = ph.sb("o2", [P, 2, HB, F])
        work = ph.ps("work", [P, 2, 512])
        acc = ph.ps("acc", [P, 2, 512])
        gT_ps = ph.ps("gT_ps", [P, 2, 512])
        m2_ps = ph.ps("m2_ps", [P, 512])
        nat_ps = ph.ps("nat_ps", [P, HB, F])

        w_here = ph.sem("w_here")
        w_turned = ph.sem("w_turned")
        wT_made = ph.sem("wT_made")
        wa_done = ph.sem("wa_done")
        wa_copied = ph.sem("wa_copied")
        wext_made = ph.sem("wext_made")
        ones_made = ph.sem("ones_made")
        work_full = ph.sem("work_full")
        hT_made = ph.sem("hT_made")
        o1_made = ph.sem("o1_made")
        H_made = ph.sem("H_made")
        f2max_made = ph.sem("f2max_made")
        G_made = ph.sem("G_made")
        mG_made = ph.sem("mG_made")
        ED_made = ph.sem("ED_made")
        F_made = ph.sem("F_made")
        F_cut = ph.sem("F_cut")
        prT_made = ph.sem("prT_made")
        acc_done = ph.sem("acc_done")
        rden_made = ph.sem("rden_made")
        v_made = ph.sem("v_made")
        vneg_made = ph.sem("vneg_made")
        exp1_made = ph.sem("exp1_made")
        exp2_made = ph.sem("exp2_made")
        g_made = ph.sem("g_made")
        gT_done = ph.sem("gT_done")
        g2T_made = ph.sem("g2T_made")
        m2_done = ph.sem("m2_done")
        o2T_made = ph.sem("o2T_made")
        nat_done = ph.sem("nat_done")
        o2_made = ph.sem("o2_made")
        o2T_stored = [ph.sem("o2T_stored0"), ph.sem("o2T_stored1")]
        o2_stored = [ph.sem("o2_stored0"), ph.sem("o2_stored1")]
        block = ctx.enter_context(nc.Block())
        JOBS = 8

        def rows(dram, b):
            return dram[b].rearrange("(t p) f -> p t f", p=P)

        @block.sync
        def _(sp):
            def load(b, s):
                sp.dma_start(ln.x[:, s, :, :], rows(x_in, b)).then_inc(ln.x_here[s], 16)

            load(0, 0)
            sp.dma_start(w_in[:], W.rearrange("(c p) n -> p c n", p=P)).then_inc(w_here, 16)
            for k in range(2):
                for c in range(2):
                    sp.dma_start(a_in[:, c, k:k + 1], a[k * W2 + c * P:k * W2 + (c + 1) * P, :]).then_inc(w_here, 16)
            sp.dma_start(w1[:], mlp1_w).then_inc(w_here, 16)
            for c in range(2):
                sp.dma_start(b1[:, c:c + 1], mlp1_b[c * P:(c + 1) * P].rearrange("(p o) -> p o", o=1)).then_inc(w_here, 16)
            sp.dma_start(w2[:], mlp2_w.rearrange("(c p) n -> p c n", p=P)).then_inc(w_here, 16)
            sp.dma_start(b2[:], mlp2_b.rearrange("(p o) -> p o", o=1)).then_inc(w_here, 16)
            load(1, 1)

            def step(b, s, pair, left):
                if left >= 2:
                    ph.wait_apart(sp, ln.y_made, nth(b, NT, NT))
                    load(b + 2, s)
                for k in range(2):
                    ph.wait_apart(sp, o2T_made, nth(b, 2, k + 1) + 1)
                    sp.dma_start(hT_out[b][:, k * 512:(k + 1) * 512], o2T[:, k, :]).then_inc(o2T_stored[k], 16)
                    ph.wait_apart(sp, o2_made, nth(b, 2, k + 1) + 1)
                    sp.dma_start(rows(h_out, b)[:, k * HB:(k + 1) * HB, :], o2[:, k, :, :]).then_inc(o2_stored[k], 16)

            pipelined(sp, B, step, 2)
            for k in range(2):
                sp.wait_ge(o2T_stored[k], 16 * B + 16)
                sp.wait_ge(o2_stored[k], 16 * B + 16)

        @block.gpsimd
        def _(pool):
            for s_, n in ((g2T_made, 2), (v_made, 2), (gT_done, 2), (m2_done, 2), (o2T_made, 1), (nat_done, 2),
                          (o2_made, 1), (o2T_stored[0], 16), (o2T_stored[1], 16), (o2_stored[0], 16),
                          (o2_stored[1], 16)):
                pool.sem_inc(s_, n)
            pool.memset(minus1[:], -1.0).then_inc(ones_made, 1)
            for s_ in range(2):
                pool.memset(H[:, s_, :, W2 + 1:W2 + 2], 1.0).then_inc(ones_made, 1)
            ln.gpsimd_consts(pool)

            def reduce_G(b):
                ph.wait_apart(pool, f2max_made, nth(b, 1, 1))
                pool.partition_all_reduce(G[:], f2max[:], P, bass.bass_isa.ReduceOp.max).then_inc(G_made, 1)

            ln.gpsimd(pool, 0)
            ln.gpsimd(pool, 1)
            reduce_G(0)

            def step(b, s, pair, left):
                if left >= 1:
                    reduce_G(b + 1)
                if left >= 2:
                    ln.gpsimd(pool, b + 2)

            pipelined(pool, B, step, 2)

        @block.vector
        def _(dve):
            dve.wait_ge(w_here, 16 * 10)
            dve.wait_ge(w_turned, 1)
            dve.tensor_copy(wT[:].rearrange("p c (e m) -> p c e m", e=2),
                            work[:, 0, :].rearrange("p (c e m) -> p c e m", c=2, e=2)).then_inc(wT_made, 1)
            dve.tensor_copy(wx[:, :, 1:W2 + 1], w_in[:]).then_inc(wext_made, 1)
            dve.wait_ge(wa_done, 1)
            for c in range(2):
                dve.tensor_copy(wa1[:, c, :], work[:, 1, 2 * c:2 * c + 1]).then_inc(wa_copied, 1)
                dve.tensor_copy(wx[:, c, 0:1], work[:, 1, 2 * c + 1:2 * c + 2]).then_inc(wext_made, 1)
            dve.wait_ge(wa_copied, 2)
            for c in range(2):
                dve.tensor_copy(wa1_wide[:, c, :], wa1[:, c, :].broadcast_to([P, P])).then_inc(wext_made, 1)

            def norm(b, s, half):
                if not isinstance(b, int) or b > 0:
                    dve.wait_ge(work_full, nth(b, JOBS, 1 - JOBS))
                ln.vector(dve, b, s, half)

            def top_f2(b, s):
                dve.wait_ge(H_made, nth(b, 4, 4))
                if not isinstance(b, int) or b > 0:
                    dve.wait_ge(G_made, nth(b, 1, 0))
                dve.tensor_reduce(f2max[:], H[:, s, :, 0], AX_X, ALU.max).then_inc(f2max_made, 1)

            def minus_G(b):
                dve.wait_ge(G_made, nth(b, 1, 1))
                if not isinstance(b, int) or b > 0:
                    dve.wait_ge(F_made, nth(b, 1, 0))
                dve.tensor_scalar(mG8[:], G[:], -(1.0 - SLOPE), None, ALU.mult).then_inc(mG_made, 1)
                dve.tensor_scalar(mG2[:], G[:], -SLOPE, None, ALU.mult).then_inc(mG_made, 1)

            def cut_F(b):
                dve.wait_ge(F_made, nth(b, 1, 1))
                if not isinstance(b, int) or b > 0:
                    dve.wait_ge(prT_made, nth(b, NT, 0))
                dve.tensor_scalar(F_row[:], F_raw[:], 1.0, None, ALU.min).then_inc(F_cut, 1)
                dve.wait_ge(F_cut, nth(b, 1, 1))
                dve.wait_ge(ED_made, nth(b, 2, 2))

            def probs(b, s, j0, j1):
                for j in range(j0, j1):
                    dve.tensor_scalar(prT[:, s, j, :], F_row[:], E[:, j:j + 1], D[:, j:j + 1], ALU.max,
                                      ALU.mult).then_inc(prT_made, 1)

            def divide(b, t):
                dve.wait_ge(acc_done, nth(b, NT, t + 1))
                dve.reciprocal(rden[:, t:t + 1], acc[:, t % 2, W2:W2 + 1]).then_inc(rden_made, 1)
                dve.wait_ge(rden_made, nth(b, NT, t + 1))
                dve.tensor_scalar(v[:, t // HB, t % HB, :], acc[:, t % 2, 0:W2], rden[:, t:t + 1], None,
                                  ALU.mult).then_inc(v_made, 1)

            def negative(b, k):
                dve.wait_ge(v_made, nth(b, NT, (k + 1) * HB) + 2)
                dve.tensor_scalar(vexp[:, k, :, :], v[:, k, :, :], 0.0, None, ALU.min).then_inc(vneg_made, 1)

            def positive(b, k):
                dve.wait_ge(exp2_made, nth(b, 2, k + 1))
                dve.wait_ge(gT_done, nth(b, 2, k + 1))
                dve.scalar_tensor_tensor(out=g[:, k, :, :], in0=v[:, k, :, :], scalar=0.0, in1=vexp[:, k, :, :],
                                         op0=ALU.max, op1=ALU.add).then_inc(g_made, 1)

            def add_o1(b, s, k):
                dve.wait_ge(gT_done, nth(b, 2, k + 1) + 2)
                dve.wait_ge(m2_done, nth(b, 2, k + 1))
                dve.scalar_tensor_tensor(out=g2T[:, :, k * 512:(k + 1) * 512], in0=gT_ps[:], scalar=-1.0,
                                         in1=o1T[:, s, :, k * 512:(k + 1) * 512], op0=ALU.add,
                                         op1=ALU.add).then_inc(g2T_made, 1)

            norm(0, 0, 0)
            norm(1, 1, 0)
            top_f2(0, 0)
            minus_G(0)
            cut_F(0)
            probs(0, 0, 0, NT)

            def step(b, s, pair, left):
                more = left >= 1
                for t in range(HB):
                    divide(b, t)
                negative(b, 0)
                divide(b, 4)
                positive(b, 0)
                divide(b, 5)
                if more:
                    top_f2(b + 1, 1 - s)
                divide(b, 6)
                add_o1(b, s, 0)
                if more:
                    minus_G(b + 1)
                divide(b, 7)
                negative(b, 1)
                if more:
                    cut_F(b + 1)
                    probs(b + 1, 1 - s, 0, HB)
                positive(b, 1)
                if more:
                    probs(b + 1, 1 - s, HB, NT)
                add_o1(b, s, 1)
                if left >= 2:
                    norm(b + 2, s, pair + 1)

            pipelined(dve, B, step, 2)

        @block.scalar
        def _(act):
            two = lambda ap: ap.rearrange("p a n -> p (a n)")

            def take_hT(b):
                act.wait_ge(work_full, nth(b, JOBS, 1))
                act.activation(hT[:], two(work[:]), ACT.Relu).then_inc(hT_made, 1)

            def take_o1(b, s, c):
                act.wait_ge(work_full, nth(b, JOBS, 2 + c))
                if c == 0 and (not isinstance(b, int) or b > 0):
                    act.wait_ge(g2T_made, nth(b, 2, 0))
                act.activation(o1T[:, s, c, :], two(work[:]), ACT.Relu, bias=b1[:, c:c + 1]).then_inc(o1_made, 1)

            def take_H(b, s, i):
                act.wait_ge(work_full, nth(b, JOBS, 4 + i))
                act.activation(H[:, s, 2 * i:2 * i + 2, 0:W2 + 1], work[:, :, 0:W2 + 1], ACT.Copy).then_inc(H_made, 1)

            def exp_f2(b, s):
                act.wait_ge(mG_made, nth(b, 2, 2))
                if not isinstance(b, int) or b > 0:
                    act.wait_ge(prT_made, nth(b, NT, 0))
                act.activation(E[:], H[:, s, :, 0], ACT.Exp, bias=mG8[:], scale=1.0 - SLOPE).then_inc(ED_made, 1)
                act.activation(D[:], H[:, s, :, 0], ACT.Exp, bias=mG2[:], scale=SLOPE).then_inc(ED_made, 1)

            def exp_f1(b):
                act.wait_ge(work_full, nth(b, JOBS, 8))
                if not isinstance(b, int) or b > 0:
                    act.wait_ge(F_cut, nth(b, 1, 0))
                act.activation(F_raw[:], two(work[:]), ACT.Exp, bias=mG8[:], scale=-(1.0 - SLOPE)).then_inc(F_made, 1)

            def elu_exps(b, k):
                act.wait_ge(vneg_made, nth(b, 2, k + 1))
                act.activation(vexp[:, k, :, :], vexp[:, k, :, :], ACT.Exp).then_inc(exp1_made, 1)
                act.wait_ge(exp1_made, nth(b, 2, k + 1))
                act.activation(vexp[:, k, :, :], vexp[:, k, :, :], ACT.Exp, bias=minus1[:]).then_inc(exp2_made, 1)

            def take_o2T(b, k):
                act.wait_ge(m2_done, nth(b, 2, k + 1) + 2)
                act.wait_ge(o2T_stored[k], nth(b, 16, 16))
                act.wait_ge(nat_done, nth(b, 2, k + 1))
                act.activation(o2T[:, k, :], m2_ps[:], ACT.Relu, bias=b2[:]).then_inc(o2T_made, 1)

            def take_o2(b, k):
                act.wait_ge(nat_done, nth(b, 2, k + 1) + 2)
                act.wait_ge(o2_stored[k], nth(b, 16, 16))
                act.activation(o2[:, k, :, :], nat_ps[:], ACT.Copy).then_inc(o2_made, 1)

            act.wait_ge(w_here, 16 * 10)
            act.wait_ge(ones_made, 3)
            take_hT(0)
            take_o1(0, 0, 0)
            take_o1(0, 0, 1)
            for i in range(4):
                take_H(0, 0, i)
            exp_f2(0, 0)
            exp_f1(0)

            def step(b, s, pair, left):
                more, n, o = left >= 1, b + 1, 1 - s
                if more:
                    take_hT(n)
                    take_o1(n, o, 0)
                    take_o1(n, o, 1)
                    take_H(n, o, 0)
                    take_H(n, o, 1)
                elu_exps(b, 0)
                if more:
                    take_H(n, o, 2)
                    take_H(n, o, 3)
                    exp_f2(n, o)
                take_o2T(b, 0)
                if more:
                    exp_f1(n)
                take_o2(b, 0)
                elu_exps(b, 1)
                take_o2T(b, 1)
                take_o2(b, 1)

            pipelined(act, B, step, 2)

        @block.tensor
        def _(pe):
            pe.wait_ge(w_here, 16 * 10)
            for e in range(2):
                for c in range(2):
                    last = pe.transpose(work[:, 0, (2 * e + c) * P:(2 * e + c + 1) * P], w_in[:, c, e * P:(e + 1) * P],
                                        ident[:])
            last.then_inc(w_turned, 1)
            pe.wait_ge(wT_made, 1)
            for c in range(2):
                for e in range(2):
                    last = pe.matmul(work[:, 1, 2 * c:2 * c + 2], wT[:, e, c * P:(c + 1) * P], a_in[:, e, :],
                                     start=(e == 0), stop=(e == 1))
            last.then_inc(wa_done, 1)
            pe.wait_ge(wext_made, 5)
            pe.wait_ge(ones_made, 3)

            def job(b, s, n):
                if n == 0:
                    pe.wait_ge(ln.y_made, nth(b, NT, NT))
                    if not isinstance(b, int) or b > 0:
                        pe.wait_ge(F_made, nth(b, 1, 0))
                    for t in range(NT):
                        last = pe.transpose(work[:, t // 4, (t % 4) * P:(t % 4 + 1) * P], ln.y[:, t, :], ident[:])
                elif n in (1, 2):
                    pe.wait_ge(hT_made, nth(b, 1, 1))
                    if n == 2:
                        pe.wait_ge(o1_made, nth(b, 2, 1))
                    c = n - 1
                    for k in range(2):
                        last = pe.matmul(work[:, k, :], w1[:, c * P:(c + 1) * P], hT[:, k * 512:(k + 1) * 512],
                                         start=True, stop=True)
                elif n < 7:
                    i = n - 3
                    if i == 0:
                        pe.wait_ge(o1_made, nth(b, 2, 2))
                    else:
                        pe.wait_ge(H_made, nth(b, 4, i))
                    for q in range(2):
                        t = 2 * i + q
                        for c in range(2):
                            last = pe.matmul(work[:, q, 0:W2 + 1], o1T[:, s, c, t * P:(t + 1) * P], wx[:, c, :],
                                             start=(c == 0), stop=(c == 1))
                else:
                    pe.wait_ge(H_made, nth(b, 4, 4))
                    for k in range(2):
                        for c in range(2):
                            last = pe.matmul(work[:, k, :], wa1_wide[:, c, :], o1T[:, s, c, k * 512:(k + 1) * 512],
                                             start=(c == 0), stop=(c == 1))
                last.then_inc(work_full, 1)

            def weigh(b, s, t):
                if t == 0:
                    pe.wait_ge(prT_made, nth(b, NT, NT))
                pe.wait_ge(v_made, nth(b, NT, t + 1))
                for j in range(NT):
                    last = pe.matmul(acc[:, t % 2, 0:W2 + 1], prT[:, s, j, t * P:(t + 1) * P],
                                     H[:, s, j, 1:W2 + 2], start=(j == 0), stop=(j == NT - 1))
                last.then_inc(acc_done, 1)

            def turn_g(b, k):
                pe.wait_ge(g_made, nth(b, 2, k + 1))
                pe.wait_ge(g2T_made, nth(b, 2, k) + 2)
                for q in range(HB):
                    for c in range(2):
                        last = pe.transpose(gT_ps[:, c, q * P:(q + 1) * P], g[:, k, q, c * P:(c + 1) * P], ident[:])
                last.then_inc(gT_done, 1)

            def mlp2(b, k):
                pe.wait_ge(g2T_made, nth(b, 2, k + 1) + 2)
                pe.wait_ge(o2T_made, nth(b, 2, k) + 1)
                for c in range(2):
                    last = pe.matmul(m2_ps[:], w2[:, c, :], g2T[:, c, k * 512:(k + 1) * 512], start=(c == 0),
                                     stop=(c == 1))
                last.then_inc(m2_done, 1)

            def turn_o2(b, k):
                pe.wait_ge(o2T_made, nth(b, 2, k + 1) + 1)
                pe.wait_ge(o2_made, nth(b, 2, k) + 1)
                for q in range(HB):
                    last = pe.transpose(nat_ps[:, q, :], o2T[:, k, q * P:(q + 1) * P], ident[:])
                last.then_inc(nat_done, 1)

            for n in range(JOBS):
                job(0, 0, n)

            def step(b, s, pair, left):
                more = left >= 1
                if more:
                    job(b + 1, 1 - s, 0)
                for t in range(NT):
                    weigh(b, s, t)
                    if more and t + 1 < JOBS:
                        job(b + 1, 1 - s, t + 1)
                    if t == 5:
                        turn_g(b, 0)
                    if t == 6:
                        mlp2(b, 0)
                turn_o2(b, 0)
                turn_g(b, 1)
                mlp2(b, 1)
                turn_o2(b, 1)

            pipelined(pe, B, step, 2)




class Jobs:

    PREP = {3: [("turn", 0)], 4: [("turn", 1)], 5: [("q", 0)], 6: [("q", 1)], 7: [("v", 0)], 8: [("v", 1)],
            10: [("k", 0)], 11: [("k", 1)]}
    FINISH = {3: [("R", 3), ("R", 0)], **{u: [("R", u)] for u in (2, *range(4, 16))}}
    FINISH_TAIL = {1: [("R", 1)]}
    LATE_TAIL = {0: [("O", 0), ("O", 1)]}
    R_ORDER = [1, 2, 3, 0] + list(range(4, 16))

    def __init__(self, B):
        self.B = B

    def does(self, b):
        if not isinstance(b, int):
            return True, True, True
        return b + 1 < self.B, 1 <= b <= self.B, b >= 2

    def at(self, b, u):
        prep, finish, _ = self.does(b)
        return (self.PREP.get(u, []) if prep else []) + (self.FINISH.get(u, []) if finish else [])

    def tail(self, b, u):
        _, finish, late = self.does(b)
        return (self.LATE_TAIL.get(u, []) if late else []) + (self.FINISH_TAIL.get(u, []) if finish else [])

    def order(self, b):
        return [j for u in range(16) for j in self.at(b, u) + self.tail(b, u)]

    def half_before(self, b):
        if isinstance(b, int) and (b <= 2 or b >= self.B - 1):
            return sum(len(self.order(i)) for i in range(-1, b)) // 2
        full = len(self.order(2)) // 2
        return (b - 2) * full + self.half_before(2)

    def index(self, b, job):
        return self.order(b).index(job)

    def bank(self, b, job):
        return self.index(b, job) % 2

    def count(self, b, job):
        return self.half_before(b) * 2 + (self.index(b, job) + 1)

    def uses(self, b, job):
        return self.half_before(b) + (self.index(b, job) // 2 + 1)


def attention_phase(nc, tag, B, N, F, heads, clip_high, ident, Wq, bq, Wk, bk, Wv, bv, Wo, bo, gamma, beta, x_in,
                    h_scratch, x_out):
    NT = N // P
    D = F // heads
    HALF = 512
    UN = 2 * NT
    SCALE = 1.0 / math.sqrt(D)
    jobs = Jobs(B)
    with ExitStack() as ctx:
        ph = Phase(nc, ctx, tag)
        ln = Norm(ph, NT, F, buffers=1)
        wT = ph.sb("wT", [P, 4, F])
        bias_q = ph.sb("bias_q", [P, 1])
        bias_k = ph.sb("bias_k", [P, 1])
        rows_in = ph.sb("rows_in", [P, 4, F])
        hot = ph.sb("hot", [P, 3 * UN])
        pick = ph.sb("pick", [P, UN, P], F32R)
        hT = ph.sb("hT", [P, N])
        hi = ph.sb("hi", [P, N], F32R)
        lo = ph.sb("lo", [P, N], F32R)
        qs = ph.sb("qs", [P, 2, heads, N], F32R)
        ks = ph.sb("ks", [P, 2, heads, N], F32R)
        vn = ph.sb("vn", [P, 2, NT, F])
        wt = ph.sb("wt", [P, 2, heads, HALF])
        ctxu = ph.sb("ctxu", [P, UN + 1, HALF])
        rec_hi = ph.sb("rec_hi", [P, HALF], F32R)
        rec_lo = ph.sb("rec_lo", [P, HALF], F32R)
        part = ph.sb("part", [P, 2, HALF])
        rec = hT[:, 0:HALF]
        total = ph.sb("total", [P, 2, HALF])
        z = ph.sb("z", [P, NT, F])
        w_in = z[:, 0:4, :]
        z_stats = ph.sb("z_stats", [P, NT, 6])
        z_mv = ph.sb("z_mv", [P, NT, 2])
        z_eps = ph.sb("z_eps", [P, NT])
        z_rstd = ph.sb("z_rstd", [P, NT])
        z_nmr = ph.sb("z_nmr", [P, NT])
        xe = ph.sb("xe", [P, NT, F])
        scores = ph.ps("scores", [P, heads, HALF])
        ctx_ps = ph.ps("ctx_ps", [P, HALF])
        sums = ph.ps("sums", [P, HALF])
        work = ph.ps("work", [P, 2, HALF])

        w_here = ph.sem("w_here")
        w_turned = ph.sem("w_turned")
        wT_made = ph.sem("wT_made")
        consts_zeroed = ph.sem("consts_zeroed")
        hot_made = ph.sem("hot_made")
        pick_made = ph.sem("pick_made")
        pick_rounded = ph.sem("pick_rounded")
        h_stored = ph.sem("h_stored")
        work_full = ph.sem("work_full")
        work_used = [ph.sem("work_used0"), ph.sem("work_used1")]
        hi_made = ph.sem("hi_made")
        q_stacked = ph.sem("q_stacked")
        k_stacked = ph.sem("k_stacked")
        qk_done = ph.sem("qk_done")
        exp_made = ph.sem("exp_made")
        wt_made = ph.sem("wt_made")
        pv_done = ph.sem("pv_done")
        ctx_out = ph.sem("ctx_out")
        sums_out = ph.sem("sums_out")
        rec_made = ph.sem("rec_made")
        rec_hi_made = ph.sem("rec_hi_made")
        rec_split = ph.sem("rec_split")
        added = ph.sem("added")
        z_here = ph.sem("z_here")
        xe_here = ph.sem("xe_here")
        z_biased = ph.sem("z_biased")
        xe_biased = ph.sem("xe_biased")
        z_stats_made = ph.sem("z_stats_made")
        z_mv_made = ph.sem("z_mv_made")
        z_eps_added = ph.sem("z_eps_added")
        z_rstd_made = ph.sem("z_rstd_made")
        z_nmr_made = ph.sem("z_nmr_made")
        z_normed = ph.sem("z_normed")
        z_scaled = ph.sem("z_scaled")
        out_made = ph.sem("out_made")
        stored = ph.sem("stored")
        block = ctx.enter_context(nc.Block())
        WEIGHT_DMAS = 10

        def rows(dram, b):
            return dram[b].rearrange("(t p) f -> p t f", p=P)

        def hot_of(u):
            return hot[:, UN - 1 - u:UN - 1 - u + D]

        def unit(s, u):
            return ctxu[:, u if u > 0 else UN * s, :]

        def run_slots(eng, slot):
            for b in range(2):
                slot(b, b % 2, *jobs.does(b))
            with eng.Fori(0, (B - 4) // 2) as pair:
                for s in range(2):
                    slot(pair * 2 + (2 + s), s, True, True, True)
            for b in range(B - 2, B + 2):
                slot(b, b % 2, *jobs.does(b))

        def ahead(b):
            return not isinstance(b, int) or b + 2 < B

        def later(b, least=1):
            return not isinstance(b, int) or b >= least

        @block.sync
        def _(sp):
            def load(b):
                sp.dma_start(ln.x[:, 0, :, :], rows(x_in, b)).then_inc(ln.x_here[0], 16)

            def store_h(b):
                ph.wait_apart(sp, ln.y_made, nth(b, NT, NT))
                sp.dma_start(rows(h_scratch, b), ln.y[:]).then_inc(h_stored, 16)

            def stack(slot_b, s, kind):
                dst, sem, groups = ((qs, q_stacked, (hi, lo, hi, lo)) if kind == "q" else
                                    (ks, k_stacked, (hi, hi, lo, lo)))
                for k in range(2):
                    ph.wait_apart(sp, work_used[jobs.bank(slot_b, (kind, k))], jobs.uses(slot_b, (kind, k)))
                for g, src in enumerate(groups):
                    for h in range(heads):
                        sp.dma_start(dst[g * D:(g + 1) * D, s, h, :].bitcast(F32),
                                     src[h * D:(h + 1) * D, :].bitcast(F32)).then_inc(sem, 16)

            load(0)
            for i, w in enumerate((Wq, Wk, Wv, Wo)):
                sp.dma_start(w_in[:, i, :], w).then_inc(w_here, 16)
            for t, w in ((bias_q, bq), (bias_k, bk)):
                sp.dma_start(t[:], w.rearrange("(p o) -> p o", o=1)).then_inc(w_here, 16)
            for i, w in enumerate((bv, bo, gamma, beta)):
                sp.dma_start(rows_in[:, i, :], w.rearrange("(o f) -> o f", o=1).broadcast_to([P, F])).then_inc(w_here, 16)
            store_h(0)
            load(1)
            stack(-1, 0, "q")
            stack(-1, 0, "k")

            def slot(b, s, prep, finish, late):
                if prep:
                    store_h(b + 1)
                    if ahead(b):
                        load(b + 2)
                    stack(b, 1 - s, "q")
                if late:
                    ph.wait_apart(sp, out_made, nth(b - 1, 1, 0))
                    sp.dma_start(rows(x_out, b - 2), xe[:]).then_inc(stored, 16)
                if finish:
                    if late:
                        ph.wait_apart(sp, stored, nth(b - 1, 16, 0))
                    ph.wait_apart(sp, h_stored, nth(b, 16, 0))
                    sp.dma_start(z[:], rows(h_scratch, b - 1)).then_inc(z_here, 16)
                    sp.dma_start(xe[:], rows(x_in, b - 1)).then_inc(xe_here, 16)
                if prep:
                    stack(b, 1 - s, "k")

            run_slots(sp, slot)
            sp.wait_ge(stored, 16 * B)

        @block.gpsimd
        def _(pool):
            pool.memset(hot[:], 0.0).then_inc(consts_zeroed, 1)
            pick_f = ctxu[:, 0:UN * P // HALF, :].rearrange("p a (b m) -> p (a b) m", m=P)
            pool.memset(ctxu[:, 0:UN * P // HALF, :], 0.0).then_inc(consts_zeroed, 1)
            pool.wait_ge(consts_zeroed, 2)
            pool.memset(hot[:, UN - 1:2 * UN:UN], 1.0).then_inc(hot_made, 1)
            sel = pick_f.rearrange("p u (h d) -> p u h d", h=heads)
            pool.affine_select(out=sel, in_=sel, compare_op=ALU.not_equal, fill=1.0, base=0,
                               pattern=[[-1, UN], [-D, heads], [0, D]], channel_multiplier=1).then_inc(pick_made, 1)
            ln.gpsimd_consts(pool)
            ln.gpsimd(pool, 0)
            ln.gpsimd(pool, 1)
            pool.wait_ge(w_here, 16 * WEIGHT_DMAS)

            def add(b, n):
                u = jobs.R_ORDER[n + 2]
                pool.wait_ge(work_used[jobs.bank(b, ("R", u))], jobs.uses(b, ("R", u)))
                if later(b, 2) or n > 0:
                    pool.wait_ge(added, nth(b - 1, UN - 2, n))
                pool.tensor_tensor(total[:, u % 2, :], total[:, u % 2, :], part[:, n % 2, :],
                                   ALU.add).then_inc(added, 1)

            def slot(b, s, prep, finish, late):
                if late:
                    pool.wait_ge(z_eps_added, nth(b - 2, 1, 1))
                    pool.tensor_tensor(z_rstd[:], z_eps[:], ln.minus_half[:], ALU.pow).then_inc(z_rstd_made, 1)
                for n in range(UN - 2):
                    if finish:
                        add(b, n)
                    if late and n == 3:
                        pool.wait_ge(z_normed, nth(b - 2, NT, NT))
                        pool.tensor_tensor(z[:], z[:], rows_in[:, 2:3, :].broadcast_to([P, NT, F]),
                                           ALU.mult).then_inc(z_scaled, 1)
                    if late and n == 4:
                        pool.wait_ge(z_scaled, nth(b - 2, 1, 1))
                        pool.wait_ge(xe_biased, nth(b - 2, 1, 1))
                        pool.tensor_tensor(xe[:], xe[:], z[:], ALU.add).then_inc(out_made, 1)
                    if finish and n == UN - 5:
                        pool.wait_ge(z_here, nth(b - 1, 16, 16))
                        pool.tensor_tensor(z[:], z[:], rows_in[:, 1:2, :].broadcast_to([P, NT, F]),
                                           ALU.add).then_inc(z_biased, 1)
                if ahead(b):
                    ln.gpsimd(pool, b + 2)
                if finish:
                    pool.wait_ge(xe_here, nth(b - 1, 16, 16))
                    pool.tensor_tensor(xe[:], xe[:], rows_in[:, 3:4, :].broadcast_to([P, NT, F]),
                                       ALU.add).then_inc(xe_biased, 1)

            run_slots(pool, slot)

        @block.vector
        def _(dve):
            dve.wait_ge(pick_made, 1)
            pick_f = ctxu[:, 0:UN * P // HALF, :].rearrange("p a (b m) -> p (a b) m", m=P)
            dve.tensor_copy(pick[:], pick_f).then_inc(pick_rounded, 1)
            dve.wait_ge(w_turned, 1)
            dve.tensor_copy(wT[:], work[:, 0, :].rearrange("p (i f) -> p i f", i=4)).then_inc(wT_made, 1)

            def clip(b, u, p):
                dve.wait_ge(exp_made, nth(b, 2 * UN, 2 * u + p + 1))
                c, k = u // 2, u % 2
                w = wt[:, u % 2, 2 * p:2 * p + 2, :]
                dve.scalar_tensor_tensor(
                    out=w, in0=w, scalar=CLIP_LO, in1=clip_high[:, c:c + 1, k * HALF:(k + 1) * HALF].broadcast_to(
                        [P, 2, HALF]), op0=ALU.max, op1=ALU.min).then_inc(wt_made, 1)

            def reciprocals(b, k):
                cols = slice(k * HALF // 2, (k + 1) * HALF // 2)
                if k == 0:
                    dve.wait_ge(sums_out, nth(b, 1, 1))
                dve.reciprocal(rec[:, cols], rec[:, cols]).then_inc(rec_made, 1)
                if k == 1:
                    dve.wait_ge(rec_made, nth(b, 2, 2))
                    dve.tensor_copy(rec_hi[:], rec).then_inc(rec_hi_made, 1)
                    dve.wait_ge(rec_hi_made, nth(b, 1, 1))
                    dve.tensor_tensor(rec_lo[:], rec, rec_hi[:].bitcast(F32), ALU.subtract).then_inc(rec_split, 1)

            def do_job(job, b, s):
                kind, k = job
                if kind == "turn":
                    return
                bank = jobs.bank(b, job)
                res, used = work[:, bank, :], work_used[bank]
                if kind in ("q", "k"):
                    j = k + (2 if kind == "k" else 0)
                    dve.wait_ge(hi_made, nth(b + 1, 4, j + 1))
                    cols = slice(k * HALF, (k + 1) * HALF)
                    dve.scalar_tensor_tensor(out=lo[:, cols], in0=res, scalar=(bias_q if kind == "q" else bias_k)[:],
                                             in1=hi[:, cols].bitcast(F32), op0=ALU.add,
                                             op1=ALU.subtract).then_inc(used, 1)
                    return
                dve.wait_ge(work_full, jobs.count(b, job))
                if kind == "v":
                    dve.tensor_tensor(vn[:, 1 - s, 4 * k:4 * k + 4, :], res.rearrange("p (t f) -> p t f", f=F),
                                      rows_in[:, 0:1, :].broadcast_to([P, 4, F]), ALU.add).then_inc(used, 1)
                elif kind == "R":
                    dve.wait_ge(ctx_out, nth(b - 1, UN, k + 1))
                    n = jobs.R_ORDER.index(k) - 2
                    dst = total[:, k % 2, :] if n < 0 else part[:, n % 2, :]
                    if n >= 2:
                        dve.wait_ge(added, nth(b - 1, UN - 2, n - 1))
                    dve.tensor_tensor(dst, res, unit(1 - s, k), ALU.mult).then_inc(used, 1)
                else:
                    if k == 0:
                        dve.wait_ge(z_biased, nth(b - 2, 1, 1))
                    zs = z[:, 4 * k:4 * k + 4, :]
                    dve.tensor_tensor(zs, res.rearrange("p (t f) -> p t f", f=F), zs, ALU.add).then_inc(used, 1)

            def z_statistics(slot_b):
                for k in range(2):
                    dve.wait_ge(work_used[jobs.bank(slot_b, ("O", k))], jobs.uses(slot_b, ("O", k)))
                for t in range(NT):
                    dve.bn_stats(z_stats[:, t, :], z[:, t, :]).then_inc(z_stats_made, 1)
                ph.wait_apart(dve, z_stats_made, nth(slot_b - 2, NT, NT))
                for t in range(NT):
                    dve.bn_aggr(z_mv[:, t, :], z_stats[:, t, :]).then_inc(z_mv_made, 1)
                dve.wait_ge(z_mv_made, nth(slot_b - 2, NT, NT))
                dve.tensor_scalar(z_eps[:], z_mv[:, :, 1], LN_EPS, None, ALU.add).then_inc(z_eps_added, 1)

            def z_minus_mean(b):
                dve.wait_ge(z_rstd_made, nth(b, 1, 1))
                dve.scalar_tensor_tensor(out=z_nmr[:], in0=z_mv[:, :, 0], scalar=-1.0, in1=z_rstd[:], op0=ALU.mult,
                                         op1=ALU.mult).then_inc(z_nmr_made, 1)

            dve.wait_ge(w_here, 16 * WEIGHT_DMAS)
            ln.statistics(dve, 0, 0, 0)
            ln.minus_mean(dve, 0)
            for u in range(16):
                for j in jobs.at(-1, u):
                    do_job(j, -1, 1)
            ln.statistics(dve, 1, 0, 1)
            clip(0, 0, 0)
            clip(0, 0, 1)
            ln.minus_mean(dve, 1)

            def slot(b, s, prep, finish, late):
                for u in range(UN):
                    if u <= 1 and finish:
                        reciprocals(b - 1, u)
                    if u == 4 and late:
                        z_minus_mean(b - 2)
                    for j in jobs.at(b, u):
                        do_job(j, b, s)
                    if isinstance(b, int) and b >= B:
                        pass
                    elif u + 1 < UN:
                        clip(b, u + 1, 0)
                        clip(b, u + 1, 1)
                    elif prep:
                        clip(b + 1, 0, 0)
                        clip(b + 1, 0, 1)
                    for j in jobs.tail(b, u):
                        do_job(j, b, s)
                    if u == 13 and ahead(b):
                        ln.statistics(dve, b + 2, 0, b + 2)
                    if u == 15 and ahead(b):
                        ln.minus_mean(dve, b + 2)
                    if u == 2 and late:
                        z_statistics(b)

            run_slots(dve, slot)

        @block.scalar
        def _(act):
            def exps(b, u, p):
                act.wait_ge(qk_done, nth(b, 2 * UN, 2 * u + p + 1))
                if not isinstance(b, int) or b > 0 or u >= 2:
                    act.wait_ge(pv_done, nth(b, UN, u - 1))
                act.activation(wt[:, u % 2, 2 * p:2 * p + 2, :], scores[:, 2 * p:2 * p + 2, :], ACT.Exp,
                               scale=SCALE).then_inc(exp_made, 1)

            def take_ctx(b, s, u, slot_b):
                act.wait_ge(pv_done, nth(b, UN, u + 1))
                if u > 0 and jobs.does(b)[1]:
                    act.wait_ge(work_used[jobs.bank(b, ("R", u))], jobs.uses(b, ("R", u)))
                elif u == 0 and later(b, 2):
                    act.wait_ge(added, nth(b - 1, UN - 2, 0))
                act.activation(unit(s, u), ctx_ps[:], ACT.Copy).then_inc(ctx_out, 1)

            def normalise(b):
                act.wait_ge(ln.nmr_made, nth(b, 1, 1))
                if later(b):
                    act.wait_ge(work_full, jobs.count(b - 2, ("turn", 1)))
                    act.wait_ge(h_stored, nth(b, 16, 0))
                for t in range(NT):
                    act.activation(ln.y[:, t, :], ln.x[:, 0, t, :], ACT.Relu, bias=ln.nmr[:, t:t + 1],
                                   scale=ln.rstd[:, t:t + 1]).then_inc(ln.y_made, 1)

            def normalise_z(b):
                act.wait_ge(z_nmr_made, nth(b, 1, 1))
                for t in range(NT):
                    act.activation(z[:, t, :], z[:, t, :], ACT.Identity, bias=z_nmr[:, t:t + 1],
                                   scale=z_rstd[:, t:t + 1]).then_inc(z_normed, 1)

            def do_job(job, b):
                kind, k = job
                if kind not in ("turn", "q", "k"):
                    return
                cols = slice(k * HALF, (k + 1) * HALF)
                bank = jobs.bank(b, job)
                act.wait_ge(work_full, jobs.count(b, job))
                if kind == "turn":
                    if k == 0 and later(b):
                        act.wait_ge(rec_split, nth(b, 1, 0))
                    act.activation(hT[:, cols], work[:, bank, :], ACT.Copy).then_inc(work_used[bank], 1)
                else:
                    n = 16 * 4 * heads
                    if kind == "k":
                        act.wait_ge(q_stacked, nth(b + 1, n, n))
                    elif not isinstance(b, int) or b >= 0:
                        act.wait_ge(k_stacked, nth(b + 1, n, 0))
                    act.activation(hi[:, cols], work[:, bank, :], ACT.Identity,
                                   bias=(bias_q if kind == "q" else bias_k)[:]).then_inc(hi_made, 1)

            act.wait_ge(w_here, 16 * WEIGHT_DMAS)
            normalise(0)
            for u in range(16):
                for j in jobs.at(-1, u):
                    do_job(j, -1)
            act.wait_ge(pick_rounded, 1)
            exps(0, 0, 0)
            exps(0, 0, 1)

            def slot(b, s, prep, finish, late):
                attend = not isinstance(b, int) or b < B
                for u in range(UN):
                    if attend and u >= 1:
                        take_ctx(b, s, u - 1, b)
                    if u == 0 and finish:
                        take_ctx(b - 1, 1 - s, UN - 1, b)
                        act.activation(rec, sums[:], ACT.Copy).then_inc(sums_out, 1)
                    for j in jobs.at(b, u):
                        do_job(j, b)
                    if attend and u + 1 < UN:
                        exps(b, u + 1, 0)
                        exps(b, u + 1, 1)
                    elif attend and prep:
                        exps(b + 1, 0, 0)
                        exps(b + 1, 0, 1)
                    if u == 0 and prep:
                        normalise(b + 1)
                    if u == 5 and late:
                        normalise_z(b - 2)

            run_slots(act, slot)

        @block.tensor
        def _(pe):
            pe.wait_ge(w_here, 16 * WEIGHT_DMAS)
            for i in range(4):
                last = pe.transpose(work[:, 0, i * F:(i + 1) * F], w_in[:, i, :], ident[:])
            last.then_inc(w_turned, 1)
            pe.wait_ge(wT_made, 1)

            def scores_of(b, s, u):
                c, k = u // 2, u % 2
                if u == 0:
                    n = 16 * 4 * heads
                    pe.wait_ge(q_stacked, nth(b, n, n))
                    pe.wait_ge(k_stacked, nth(b, n, n))
                for p in range(2):
                    if not isinstance(b, int) or b > 0 or u > 0:
                        pe.wait_ge(exp_made, nth(b, 2 * UN, 2 * u + p - 1))
                    for h in (2 * p, 2 * p + 1):
                        last = pe.matmul(scores[:, h, :], ks[:, s, h, c * P:(c + 1) * P],
                                         qs[:, s, h, k * HALF:(k + 1) * HALF], start=True, stop=True)
                    last.then_inc(qk_done, 1)

            def context(b, s, u):
                c = u // 2
                pe.wait_ge(wt_made, nth(b, 2 * UN, 2 * u + 2))
                if later(b) or u > 0:
                    pe.wait_ge(ctx_out, nth(b, UN, u))
                if u == 0 and later(b):
                    pe.wait_ge(sums_out, nth(b, 1, 0))
                for h in range(heads):
                    pe.matmul(ctx_ps[h * D:(h + 1) * D, :], vn[:, s, c, h * D:(h + 1) * D], wt[:, u % 2, h, :],
                              start=True, stop=True, tile_position=(0, h * D))
                for h in range(heads):
                    last = pe.matmul(sums[h * D:(h + 1) * D, :], hot_of(u), wt[:, u % 2, h, :], start=(u == 0),
                                     stop=(u == UN - 1), tile_position=(0, h * D))
                last.then_inc(pv_done, 1)

            def do_job(job, b):
                kind, k = job
                cols = slice(k * HALF, (k + 1) * HALF)
                i, bank = jobs.index(b, job), jobs.bank(b, job)
                dst = work[:, bank, :]
                if i >= 2 or later(b, 0):
                    pe.wait_ge(work_used[bank], jobs.half_before(b) + i // 2)
                if kind == "turn":
                    if k == 0:
                        pe.wait_ge(ln.y_made, nth(b + 1, NT, NT))
                    for t in range(4):
                        last = pe.transpose(dst[:, t * P:(t + 1) * P], ln.y[:, 4 * k + t, :], ident[:])
                elif kind == "q" or kind == "k":
                    pe.wait_ge(work_used[jobs.bank(b, ("turn", k))], jobs.uses(b, ("turn", k)))
                    last = pe.matmul(dst, wT[:, 0 if kind == "q" else 1, :], hT[:, cols], start=True, stop=True)
                elif kind == "v":
                    for t in range(4):
                        last = pe.matmul(dst[:, t * P:(t + 1) * P], hT[:, (4 * k + t) * P:(4 * k + t + 1) * P],
                                         wT[:, 2, :], start=True, stop=True)
                elif kind == "R":
                    if k == jobs.R_ORDER[0]:
                        pe.wait_ge(rec_split, nth(b - 1, 1, 1))
                    pe.matmul(dst, pick[:, k, :], rec_hi[:], start=True, stop=False)
                    last = pe.matmul(dst, pick[:, k, :], rec_lo[:], start=False, stop=True)
                else:
                    if k == 0:
                        pe.wait_ge(added, nth(b - 2, UN - 2, UN - 2))
                    tt = total[:].rearrange("p a n -> p (a n)")
                    for t in range(4):
                        last = pe.matmul(dst[:, t * P:(t + 1) * P], tt[:, (4 * k + t) * P:(4 * k + t + 1) * P],
                                         wT[:, 3, :], start=True, stop=True)
                last.then_inc(work_full, 1)

            for u in range(16):
                for j in jobs.at(-1, u):
                    do_job(j, -1)
            pe.wait_ge(hot_made, 1)
            pe.wait_ge(pick_rounded, 1)
            scores_of(0, 0, 0)

            def slot(b, s, prep, finish, late):
                attend = not isinstance(b, int) or b < B
                for u in range(UN):
                    for j in jobs.at(b, u):
                        do_job(j, b)
                    if attend and u + 1 < UN:
                        scores_of(b, s, u + 1)
                    elif attend and prep:
                        scores_of(b + 1, 1 - s, 0)
                    if attend:
                        context(b, s, u)
                    for j in jobs.tail(b, u):
                        do_job(j, b)

            run_slots(pe, slot)




def program(nc, x, adj, L0, L1, L2, L3, out):
    B, N, F = x.shape
    NT = N // P
    x1 = nc.dram_tensor("x1", (B, N, F), F32).ap()
    x2 = nc.dram_tensor("x2", (B, N, F), F32).ap()
    x3 = nc.dram_tensor("x3", (B, N, F), F32).ap()
    h0 = nc.dram_tensor("h0", (B, N, F), F32).ap()
    o2 = nc.dram_tensor("o2", (B, N, F), F32).ap()
    o2T = nc.dram_tensor("o2T", (B, F, N), F32).ap()
    mlp1_w, mlp1_b, mlp2_w, mlp2_b, W_fc, a_fc, W_hand, a_hand = L3
    with ExitStack() as ctx:
        ident = ctx.enter_context(nc.sbuf_tensor("ident", [P, P], F32))
        with ExitStack() as first:
            clip_high = first.enter_context(nc.sbuf_tensor("clip_high", [P, NT, N], F32))
            masks_phase(nc, adj, clip_high, None, ident, NT, N)
            attention_phase(nc, "att", B, N, F, HEADS, clip_high, ident, *L0, x, h0, x1)
        edge_bias = ctx.enter_context(nc.sbuf_tensor("edge_bias", [P, NT, N], BF16))
        masks_phase(nc, adj, None, edge_bias, ident, NT, N)
        gat_phase(nc, "gat1", B, N, F, edge_bias, ident, *L1, x1, x2, "elu")
        gat_phase(nc, "gat2", B, N, F, edge_bias, ident, *L2, x2, x3, "plain")
        fc_phase(nc, "fc", B, N, F, ident, mlp1_w, mlp1_b, W_fc, a_fc, mlp2_w, mlp2_b, x3, o2T, o2)
        gat_phase(nc, "hand", B, N, F, edge_bias, ident, W_hand, a_hand, x3, out, "hand", o2, o2T)


HEADS = 4
_L0 = ["Wq", "bq", "Wk", "bk", "Wv", "bv", "Wo", "bo", "gamma", "beta"]
_L3 = ["mlp1_w", "mlp1_b", "mlp2_w", "mlp2_b", "W_fc", "a_fc", "W_hand", "a_hand"]
_INS = (["x", "adj"] + ["L0_gnn_" + n for n in _L0] + ["L1_gnn_W", "L1_gnn_a", "L2_gnn_W", "L2_gnn_a"]
        + ["L3_gnn_" + n for n in _L3])


def kernel(**inputs):
    import numpy as np
    import concourse.bacc as bacc
    from concourse.bass_utils import run_bass_kernel_spmd

    nc = bacc.Bacc("TRN2", target_bir_lowering=False, num_devices=1)
    arrays, args = {}, {}
    for name in _INS:
        a = np.ascontiguousarray(inputs[name])
        arrays["in_" + name] = a
        args[name] = nc.dram_tensor("in_" + name, a.shape, mybir.dt.from_np(a.dtype), kind="ExternalInput").ap()
    out = nc.dram_tensor("out_x", inputs["x"].shape, F32, kind="ExternalOutput").ap()
    program(nc, args["x"], args["adj"], [args["L0_gnn_" + n] for n in _L0],
            [args["L1_gnn_W"], args["L1_gnn_a"]], [args["L2_gnn_W"], args["L2_gnn_a"]],
            [args["L3_gnn_" + n] for n in _L3], out)
    r = run_bass_kernel_spmd(nc, [arrays], core_ids=[0])
    return r.results[0]["out_x"]
```

```python
import math
from contextlib import ExitStack

import concourse.bass as bass
from concourse import mybir

F32 = mybir.dt.float32
F32R = mybir.dt.float32r
BF16 = mybir.dt.bfloat16
I32 = mybir.dt.int32
ALU = mybir.AluOpType
ACT = mybir.ActivationFunctionType
AX_X = mybir.AxisListType.X

P = 128
LN_EPS = 1e-5
SLOPE = 0.2
FAR = -2.0 ** 100
CLIP_LO, CLIP_HI = math.exp(-10.0), math.exp(10.0)


def nth(b, per, k):
    return b * per + k


def later(b, least=1):
    return not isinstance(b, int) or b >= least


class Phase:

    def __init__(self, nc, ctx, tag):
        self.nc, self.ctx, self.tag = nc, ctx, tag
        self.sems = []
        self.passed = self.sem("passed")
        ctx.callback(self.clear)

    def clear(self):
        self.nc.clear_and_free_semaphores(self.sems)
        self.nc.all_engine_barrier()

    def wait_apart(self, eng, sem, value):
        eng.wait_ge(sem, value)
        eng.sem_inc(self.passed, 1)

    def sb(self, name, shape, dt=F32):
        return self.ctx.enter_context(self.nc.sbuf_tensor(f"{self.tag}_{name}", shape, dt))

    def ps(self, name, shape, dt=F32):
        return self.ctx.enter_context(self.nc.psum_tensor(f"{self.tag}_{name}", shape, dt))

    def sem(self, name):
        self.sems.append(self.nc.alloc_semaphore(f"{self.tag}_{name}"))
        return self.sems[-1]


def pipelined(eng, batches, step, lead):
    looped = batches - lead
    assert looped % 2 == 0 and looped >= 2
    with eng.Fori(0, looped // 2) as pair:
        for s in (0, 1):
            step(pair * 2 + s, s, pair, lead)
    for b in range(looped, batches):
        step(b, b % 2, b // 2, batches - 1 - b)




def masks_phase(nc, adj, clip_high, bias_out, ident, NT, N):
    with ExitStack() as ctx:
        ph = Phase(nc, ctx, "masks")
        adj_in = ph.sb("adj_in", [P, NT, N], I32)
        edge = ph.sb("edge", [P, NT, N], BF16)
        bias = ph.sb("bias", [P, NT, N], BF16)
        identb = ph.sb("identb", [P, P], BF16)
        offset = ph.sb("offset", [P, 2])
        turned = ph.ps("turned", [P, NT, N], BF16)
        adj_here = [ph.sem(f"adj_here{t}") for t in range(NT)]
        zeroed = ph.sem("zeroed")
        offset_made = ph.sem("offset_made")
        ident_made = ph.sem("ident_made")
        edge_made = ph.sem("edge_made")
        bias_made = ph.sem("bias_made")
        bias_stored = ph.sem("bias_stored")
        turn_done = ph.sem("turn_done")
        high_made = ph.sem("high_made")
        block = ctx.enter_context(nc.Block())
        SCALAR_CHUNKS = (5, 7)

        @block.sync
        def _(sp):
            for t in range(NT):
                sp.dma_start(adj_in[:, t, :], adj[t * P:(t + 1) * P, :]).then_inc(adj_here[t], 16)
            for h in range(2):
                half = slice(h * NT // 2, (h + 1) * NT // 2)
                sp.wait_ge(bias_made, (h + 1) * NT // 2)
                sp.dma_start(bias_out[:, half, :], bias[:, half, :]).then_inc(bias_stored, 16)
            sp.wait_ge(bias_stored, 32)

        @block.gpsimd
        def _(pool):
            pool.memset(offset[:, 0:1], FAR).then_inc(offset_made, 1)
            pool.memset(offset[:, 1:2], CLIP_LO).then_inc(offset_made, 1)
            pool.memset(ident[:], 0.0).then_inc(zeroed, 1)
            pool.memset(identb[:], 0.0).then_inc(zeroed, 1)
            pool.wait_ge(zeroed, 2)
            for m in (ident, identb):
                pool.affine_select(out=m[:], in_=m[:], compare_op=ALU.not_equal, fill=1.0, base=0,
                                   pattern=[[-1, P]], channel_multiplier=1).then_inc(ident_made, 1)

        @block.tensor
        def _(pe):
            pe.wait_ge(ident_made, 2)
            pe.wait_ge(edge_made, NT)
            for c in range(NT):
                for t in range(NT):
                    last = pe.transpose(turned[:, c, t * P:(t + 1) * P], edge[:, t, c * P:(c + 1) * P], identb[:])
                last.then_inc(turn_done, 1)

        @block.vector
        def _(dve):
            for t in range(NT):
                dve.wait_ge(adj_here[t], 16)
                dve.tensor_scalar(edge[:, t, :], adj_in[:, t, :], 0, None, ALU.is_gt).then_inc(edge_made, 1)
            for c in range(NT):
                if c not in SCALAR_CHUNKS:
                    dve.wait_ge(turn_done, c + 1)
                    dve.tensor_scalar(clip_high[:, c, :], turned[:, c, :], CLIP_HI - CLIP_LO, CLIP_LO, ALU.mult,
                                      ALU.add).then_inc(high_made, 1)

        @block.scalar
        def _(act):
            act.wait_ge(offset_made, 2)
            for t in range(NT):
                act.wait_ge(edge_made, t + 1)
                act.activation(bias[:, t, :], edge[:, t, :], ACT.Identity, bias=offset[:, 0:1],
                               scale=-FAR).then_inc(bias_made, 1)
            for c in SCALAR_CHUNKS:
                act.wait_ge(turn_done, c + 1)
                act.activation(clip_high[:, c, :], turned[:, c, :], ACT.Identity, bias=offset[:, 1:2],
                               scale=CLIP_HI - CLIP_LO).then_inc(high_made, 1)




class Norm:

    def __init__(self, ph, NT, F, buffers=2):
        self.ph, self.NT, self.F = ph, NT, F
        self.x = ph.sb("ln_x", [P, buffers, NT, F])
        self.stats = ph.sb("ln_stats", [P, NT, 6])
        self.mv = ph.sb("ln_mean_var", [P, NT, 2])
        self.var_eps = ph.sb("ln_var_eps", [P, NT])
        self.rstd = ph.sb("ln_rstd", [P, NT])
        self.minus_half = ph.sb("ln_minus_half", [P, NT])
        self.nmr = ph.sb("ln_minus_mean_rstd", [P, NT])
        self.y = ph.sb("ln_y", [P, NT, F])
        self.x_here = [ph.sem(f"x_here{i}") for i in range(buffers)]
        self.stats_made = ph.sem("ln_stats_made")
        self.mv_made = ph.sem("ln_mv_made")
        self.eps_added = ph.sem("ln_eps_added")
        self.rstd_made = ph.sem("ln_rstd_made")
        self.const_made = ph.sem("ln_const_made")
        self.nmr_made = ph.sem("ln_nmr_made")
        self.y_made = ph.sem("ln_y_made")

    def statistics(self, dve, b, s, turn):
        NT = self.NT
        dve.wait_ge(self.x_here[s], nth(turn, 16, 16))
        for t in range(NT):
            dve.bn_stats(self.stats[:, t, :], self.x[:, s, t, :]).then_inc(self.stats_made, 1)
        self.ph.wait_apart(dve, self.stats_made, nth(b, NT, NT))
        for t in range(NT):
            dve.bn_aggr(self.mv[:, t, :], self.stats[:, t, :]).then_inc(self.mv_made, 1)
        dve.wait_ge(self.mv_made, nth(b, NT, NT))
        dve.tensor_scalar(self.var_eps[:], self.mv[:, :, 1], LN_EPS, None, ALU.add).then_inc(self.eps_added, 1)

    def scale(self, dve, b, s):
        NT = self.NT
        dve.wait_ge(self.rstd_made, nth(b, 1, 1))
        for t in range(NT):
            dve.tensor_scalar(self.y[:, t, :], self.x[:, s, t, :], self.mv[:, t, 0:1], self.rstd[:, t:t + 1],
                              ALU.subtract, ALU.mult).then_inc(self.y_made, 1)

    def minus_mean(self, dve, b):
        dve.wait_ge(self.rstd_made, nth(b, 1, 1))
        dve.scalar_tensor_tensor(out=self.nmr[:], in0=self.mv[:, :, 0], scalar=-1.0, in1=self.rstd[:],
                                 op0=ALU.mult, op1=ALU.mult).then_inc(self.nmr_made, 1)

    def relu(self, act, b, s):
        act.wait_ge(self.nmr_made, nth(b, 1, 1))
        for t in range(self.NT):
            act.activation(self.y[:, t, :], self.x[:, s, t, :], ACT.Relu, bias=self.nmr[:, t:t + 1],
                           scale=self.rstd[:, t:t + 1]).then_inc(self.y_made, 1)

    def gpsimd_consts(self, pool):
        pool.memset(self.minus_half[:], -0.5).then_inc(self.const_made, 1)
        pool.wait_ge(self.const_made, 1)

    def gpsimd(self, pool, b):
        pool.wait_ge(self.eps_added, nth(b, 1, 1))
        pool.tensor_tensor(self.rstd[:], self.var_eps[:], self.minus_half[:], ALU.pow).then_inc(self.rstd_made, 1)




def gat_phase(nc, tag, B, N, F, edge_bias, ident, W, a, x_in, x_out, kind, resid=None, hT_in=None):
    NT = N // P
    HB = NT // 2
    FE = F + 1
    normed = kind != "hand"
    TB = NT
    with ExitStack() as ctx:
        ph = Phase(nc, ctx, tag)
        wa = ph.sb("wa", [P, FE + P])
        w_in = ph.sb("w_in", [P, F])
        wT = ph.sb("wT", [P, F])
        a_in = ph.sb("a_in", [F, 2])
        wa2 = ph.sb("wa2", [P, 1])
        ln = Norm(ph, NT, F, buffers=1)
        x = ph.sb("x", [P, 2, NT, F])
        x_here = [ph.sem("x_again0"), ph.sem("x_again1")]
        if not normed:
            rs = ph.sb("rs", [P, 2, NT, F])
            rs_here = [ph.sem("rs_here0"), ph.sem("rs_here1")]
            hT_here = ph.sem("hT_here")
        hT = ph.sb("hT", [P, N])
        H = ph.sb("H", [P, 2, NT, FE])
        s2row = ph.sb("s2row", [P, 2, N])
        s2row4 = ph.sb("s2row4", [P, 2, N])
        y = ph.sb("y", [P, NT, N])
        u = ph.sb("u", [P, NT])
        s1m4 = ph.sb("s1m4", [P, NT])
        z = ph.sb("z", [P, NT])
        mx = ph.sb("mx", [P, NT])
        shift = ph.sb("shift", [P, NT])
        t_buf = ph.sb("t_buf", [P, TB, N])
        pr = ph.sb("pr", [P, NT, N])
        den = ph.sb("den", [P, 2, NT])
        rden = ph.sb("rden", [P, NT])
        prT = ph.sb("prT", [P, 2, NT, P])
        v = ph.sb("v", [P, 2, HB, F])
        vneg = ph.sb("vneg", [P, 2, HB, F])
        vexp = ph.sb("vexp", [P, 2, HB, F])
        res = ph.sb("res", [P, 2, HB, F])
        minus1 = ph.sb("minus1", [P, 1])
        minus1_made = ph.sem("minus1_made")
        work = ph.ps("work", [P, 2, 512])
        turned = ph.ps("turned", [P, 2, N])
        acc = ph.ps("acc", [P, 2, HB, F])

        w_here = ph.sem("w_here")
        w_turned = ph.sem("w_turned")
        wT_made = ph.sem("wT_made")
        wa_done = ph.sem("wa_done")
        wa_copied = ph.sem("wa_copied")
        wext_made = ph.sem("wext_made")
        work_full = ph.sem("work_full")
        hT_made = ph.sem("hT_made")
        s2_made = ph.sem("s2_made")
        H_made = ph.sem("H_made")
        y_max = ph.sem("y_max")
        s1m4_made = ph.sem("s1m4_made")
        z_made = ph.sem("z_made")
        mx_made = ph.sem("mx_made")
        shift_made = ph.sem("shift_made")
        t_made = ph.sem("t_made")
        pr_made = ph.sem("pr_made")
        turn_done = ph.sem("turn_done")
        prT_made = ph.sem("prT_made")
        weighed = ph.sem("weighed")
        rden_made = ph.sem("rden_made")
        v_made = ph.sem("v_made")
        vneg_made = ph.sem("vneg_made")
        vexp_made = ph.sem("vexp_made")
        vexp2_made = ph.sem("vexp2_made")
        sum_made = ph.sem("sum_made")
        sum2_made = ph.sem("sum2_made")
        less_made = ph.sem("less_made")
        relu_made = ph.sem("relu_made")
        res_made = ph.sem("res_made")
        stored = [ph.sem("stored0"), ph.sem("stored1")]
        block = ctx.enter_context(nc.Block())
        JOBS = 5 if normed else 4
        H_JOBS = [(0, 3), (3, 3), (6, 2)]

        def rows(dram, b):
            return dram[b].rearrange("(t p) f -> p t f", p=P)

        if normed:
            ORDER, S2_AT = "y e2 x0 h e3 x1 s e4 x2 x3 v0 e5 x4 x5 e6 x6 e7 x7 H n0 v1 n1", 3
        else:
            ORDER, S2_AT = "e2 x0 x1 e3 s x2 e4 x3 v0 e5 x4 x5 e6 x6 e7 x7 H n0 v1 n1", 2

        @block.sync
        def _(sp):
            def load(b, s):
                sp.dma_start(x[:, s, :, :], rows(x_in, b)).then_inc(x_here[s], 16)
                if not normed:
                    sp.dma_start(rs[:, s, :, :], rows(resid, b)).then_inc(rs_here[s], 16)

            def load_input(b):
                first = isinstance(b, int) and b == 0
                if normed:
                    if not first:
                        ph.wait_apart(sp, ln.y_made, nth(b, NT, 0))
                    sp.dma_start(ln.x[:, 0, :, :], rows(x_in, b)).then_inc(ln.x_here[0], 16)
                else:
                    if not first:
                        ph.wait_apart(sp, work_full, nth(b, JOBS, 0))
                    sp.dma_start(hT[:], hT_in[b]).then_inc(hT_here, 16)

            load_input(0)
            sp.dma_start(w_in[:], W).then_inc(w_here, 16)
            for k in range(2):
                sp.dma_start(a_in[:, k:k + 1], a[k * F:(k + 1) * F, :]).then_inc(w_here, 16)
            load(0, 0)
            load_input(1)
            load(1, 1)
            load_input(2)

            def step(b, s, pair, left):
                if normed and left >= 3:
                    load_input(b + 3)
                for k in range(2):
                    ph.wait_apart(sp, res_made, nth(b, 2, k + 1))
                    sp.dma_start(rows(x_out, b)[:, k * HB:(k + 1) * HB, :], res[:, k, :, :]).then_inc(stored[k], 16)
                    if k == 0 and left >= 3 and not normed:
                        load_input(b + 3)
                if left >= 2:
                    load(b + 2, s)

            pipelined(sp, B, step, 4)
            for k in range(2):
                sp.wait_ge(stored[k], 16 * B + 16)

        @block.gpsimd
        def _(pool):
            pool.sem_inc(weighed, 2)
            pool.sem_inc(prT_made, 2)
            pool.sem_inc(v_made, NT)
            pool.sem_inc(rden_made, 1)
            for k in range(2):
                pool.sem_inc(stored[k], 16)
            if kind == "hand":
                pool.memset(minus1[:], -1.0).then_inc(minus1_made, 1)
            if normed:
                ln.gpsimd_consts(pool)
                for b in range(3):
                    ln.gpsimd(pool, b)

            def less_one(b, s, half):
                if kind != "plain":
                    what, here = (rs, rs_here) if kind == "hand" else (x, x_here)
                    ph.wait_apart(pool, here[s], nth(half, 16, 16))
                    pool.tensor_scalar(what[:, s, :, :], what[:, s, :, :], -1.0, None, ALU.add).then_inc(less_made, 1)

            def finish(b, s, half, k):
                done = v[:, k, :, :]
                if k == 0 and kind != "elu":
                    pool.wait_ge(x_here[s], nth(half, 16, 16))
                if kind != "plain":
                    pool.wait_ge(less_made, nth(b, 1, 1))
                    pool.wait_ge(sum_made, nth(b, 2, k + 1))
                else:
                    pool.wait_ge(v_made, nth(b, NT, (k + 1) * HB) + NT)
                if kind == "hand":
                    pool.tensor_tensor(done, done, rs[:, s, k * HB:(k + 1) * HB, :], ALU.add).then_inc(sum2_made, 1)
                    ph.wait_apart(pool, sum2_made, nth(b, 2, k + 1))
                    pool.tensor_scalar(done, done, 0.0, None, ALU.max).then_inc(relu_made, 1)
                    pool.wait_ge(relu_made, nth(b, 2, k + 1))
                pool.wait_ge(stored[k], nth(b, 16, 16))
                pool.tensor_tensor(res[:, k, :, :], done, x[:, s, k * HB:(k + 1) * HB, :], ALU.add).then_inc(res_made, 1)

            def step(b, s, pair, left):
                less_one(b, s, pair)
                finish(b, s, pair, 0)
                if normed and left >= 3:
                    ln.gpsimd(pool, b + 3)
                finish(b, s, pair, 1)

            pipelined(pool, B, step, 4)

        @block.vector
        def _(dve):
            if normed:
                ln.statistics(dve, 0, 0, 0)
            dve.wait_ge(w_here, 48)
            dve.wait_ge(w_turned, 1)
            dve.tensor_copy(wT[:], work[:, 0, 0:F]).then_inc(wT_made, 1)
            dve.tensor_copy(wa[:, 0:F], w_in[:]).then_inc(wext_made, 1)
            dve.wait_ge(wa_done, 1)
            dve.tensor_copy(wa2[:], work[:, 1, 1:2]).then_inc(wa_copied, 1)
            dve.tensor_copy(wa[:, F:FE], work[:, 1, 0:1]).then_inc(wext_made, 1)
            dve.wait_ge(wa_copied, 1)
            dve.tensor_copy(wa[:, FE:FE + P], wa2[:].broadcast_to([P, P])).then_inc(wext_made, 1)

            def maxima(b, s, t0, t1):
                if t0 == 0 and later(b):
                    dve.wait_ge(t_made, nth(b, NT, 0))
                if t0 == 0:
                    ph.wait_apart(dve, s2_made, nth(b, 2, 2))
                for t in range(t0, t1):
                    dve.tensor_tensor_reduce(y[:, t, :], s2row[:, s, :], edge_bias[:, t, :], 1.0, -3.0e38, ALU.add,
                                             ALU.max, u[:, t:t + 1]).then_inc(y_max, 1)

            def shifts(b, s):
                dve.wait_ge(H_made, nth(b, 3, 3))
                if later(b):
                    dve.wait_ge(t_made, nth(b, NT, 0))
                s1 = H[:, s, :, F]
                dve.tensor_scalar(s1m4[:], s1, -4.0, None, ALU.mult).then_inc(s1m4_made, 1)
                dve.wait_ge(y_max, nth(b, NT, NT))
                dve.tensor_tensor(z[:], s1, u[:], ALU.add).then_inc(z_made, 1)
                dve.wait_ge(z_made, nth(b, 1, 1))
                dve.scalar_tensor_tensor(out=mx[:], in0=z[:], scalar=SLOPE, in1=z[:], op0=ALU.mult,
                                         op1=ALU.max).then_inc(mx_made, 1)
                dve.wait_ge(mx_made, nth(b, 1, 1))
                if later(b):
                    dve.wait_ge(pr_made, nth(b, NT, 0))
                dve.tensor_tensor(shift[:], s1, mx[:], ALU.subtract).then_inc(shift_made, 1)
                dve.wait_ge(s1m4_made, nth(b, 1, 1))

            def t_tile(b, s, t):
                if later(b) or t >= TB:
                    dve.wait_ge(pr_made, nth(b, NT, t + 1 - TB))
                dve.scalar_tensor_tensor(out=t_buf[:, t % TB, :], in0=s2row4[:, s, :], scalar=s1m4[:, t:t + 1],
                                         in1=y[:, t, :], op0=ALU.max, op1=ALU.add).then_inc(t_made, 1)

            def divide(b, s, k):
                if k == 0:
                    dve.wait_ge(pr_made, nth(b, NT, NT))
                    dve.reciprocal(rden[:], den[:, s, :]).then_inc(rden_made, 1)
                    dve.wait_ge(rden_made, nth(b, 1, 1) + 1)
                dve.wait_ge(weighed, nth(b, NT, (k + 1) * HB) + 2)
                dve.wait_ge(stored[k], nth(b, 16, 16))
                for q in range(HB):
                    t = k * HB + q
                    dve.tensor_scalar(v[:, k, q, :], acc[:, k, q, :], rden[:, t:t + 1], None,
                                      ALU.mult).then_inc(v_made, 1)
                dve.wait_ge(v_made, nth(b, NT, (k + 1) * HB) + NT)
                if kind != "plain":
                    dve.tensor_scalar(vneg[:, k, :, :], v[:, k, :, :], 0.0, None, ALU.min).then_inc(vneg_made, 1)

            def add_parts(b, k):
                if kind != "plain":
                    dve.wait_ge(vexp_made, nth(b, 2, k + 1))
                    dve.scalar_tensor_tensor(out=v[:, k, :, :], in0=v[:, k, :, :], scalar=0.0, in1=vexp[:, k, :, :],
                                             op0=ALU.max, op1=ALU.add).then_inc(sum_made, 1)

            if normed:
                ln.minus_mean(dve, 0)
                ln.statistics(dve, 1, 0, 1)
                ln.minus_mean(dve, 1)
            maxima(0, 0, 0, NT)
            shifts(0, 0)
            for t in range(NT):
                t_tile(0, 0, t)
            if normed:
                ln.statistics(dve, 2, 0, 2)
                ln.minus_mean(dve, 2)
            maxima(1, 1, 0, NT)
            shifts(1, 1)
            t_tile(1, 1, 0)

            def step(b, s, pair, left):
                if left >= 1:
                    for t in range(1, NT):
                        t_tile(b + 1, 1 - s, t)
                divide(b, s, 0)
                if left >= 2:
                    maxima(b + 2, s, 0, 3)
                add_parts(b, 0)
                if left >= 3 and normed:
                    ln.statistics(dve, b + 3, 0, b + 3)
                if left >= 2:
                    maxima(b + 2, s, 3, NT)
                if left >= 3 and normed:
                    ln.minus_mean(dve, b + 3)
                divide(b, s, 1)
                if left >= 2:
                    shifts(b + 2, s)
                    t_tile(b + 2, s, 0)
                add_parts(b, 1)

            pipelined(dve, B, step, 4)

        @block.scalar
        def _(act):
            whole = work[:].rearrange("p a n -> p (a n)")

            def normalise(b):
                if normed:
                    if later(b):
                        act.wait_ge(work_full, nth(b, JOBS, 1 - JOBS))
                    ln.relu(act, b, 0)

            def take_hT(b):
                if normed:
                    act.wait_ge(work_full, nth(b, JOBS, 1))
                    act.activation(hT[:], whole, ACT.Copy).then_inc(hT_made, 1)

            def take_s2(b, s):
                act.wait_ge(work_full, nth(b, JOBS, JOBS - 3))
                if later(b, 2):
                    act.wait_ge(t_made, nth(b, NT, -NT))
                act.activation(s2row[:, s, :], whole, ACT.Copy).then_inc(s2_made, 1)
                act.activation(s2row4[:, s, :], whole, ACT.Copy, scale=4.0).then_inc(s2_made, 1)

            def take_H(b, s):
                for i, (t0, n) in enumerate(H_JOBS):
                    act.wait_ge(work_full, nth(b, JOBS, JOBS - 2 + i))
                    act.activation(H[:, s, t0:t0 + n, :],
                                   work[:, i % 2, 0:n * FE].rearrange("p (t f) -> p t f", t=n),
                                   ACT.Copy).then_inc(H_made, 1)

            def exps(b, s, t):
                act.wait_ge(t_made, nth(b, NT, t + 1))
                if t == 0:
                    act.wait_ge(shift_made, nth(b, 1, 1))
                    if later(b):
                        act.wait_ge(rden_made, nth(b, 1, 0))
                if later(b):
                    act.wait_ge(turn_done, nth(b, NT, t + 1 - NT))
                act.activation(pr[:, t, :], t_buf[:, t % TB, :], ACT.Exp, bias=shift[:, t:t + 1], scale=SLOPE,
                               accum_out=den[:, s, t:t + 1]).then_inc(pr_made, 1)

            def evac(b, t):
                act.wait_ge(turn_done, nth(b, NT, t + 1))
                act.wait_ge(weighed, nth(b, NT, t + 1))
                act.activation(prT[:, t % 2, :, :].rearrange("p a n -> p (a n)"), turned[:, t % 2, :],
                               ACT.Copy).then_inc(prT_made, 1)

            def vexp_half(b, k):
                if kind == "plain":
                    return
                act.wait_ge(vneg_made, nth(b, 2, k + 1))
                act.activation(vexp[:, k, :, :], vneg[:, k, :, :], ACT.Exp).then_inc(
                    vexp_made if kind == "elu" else vexp2_made, 1)
                if kind == "hand":
                    act.wait_ge(vexp2_made, nth(b, 2, k + 1))
                    act.activation(vexp[:, k, :, :], vexp[:, k, :, :], ACT.Exp, bias=minus1[:]).then_inc(vexp_made, 1)

            act.wait_ge(wext_made, 3)
            if kind == "hand":
                act.wait_ge(minus1_made, 1)
            normalise(0)
            take_hT(0)
            take_s2(0, 0)
            take_H(0, 0)
            normalise(1)
            take_hT(1)
            for t in range(NT):
                exps(0, 0, t)
            take_s2(1, 1)
            take_H(1, 1)
            evac(0, 0)
            evac(0, 1)

            def step(b, s, pair, left):
                for what in ORDER.split():
                    n = int(what[1:] or 0)
                    if what[0] == "e":
                        evac(b, n)
                    elif what[0] == "n" and left >= 1:
                        evac(b + 1, n)
                    elif what[0] == "v":
                        vexp_half(b, n)
                    elif what[0] == "x" and left >= 1:
                        exps(b + 1, 1 - s, n)
                    elif what == "y" and left >= 2:
                        normalise(b + 2)
                    elif what == "h" and left >= 2:
                        take_hT(b + 2)
                    elif what == "s" and left >= 2:
                        take_s2(b + 2, s)
                    elif what == "H" and left >= 2:
                        take_H(b + 2, s)

            pipelined(act, B, step, 2)

        @block.tensor
        def _(pe):
            pe.wait_ge(w_here, 48)
            pe.transpose(work[:, 0, 0:P], w_in[:], ident[:]).then_inc(w_turned, 1)
            pe.wait_ge(wT_made, 1)
            pe.matmul(work[:, 1, 0:2], wT[:], a_in[:], start=True, stop=True).then_inc(wa_done, 1)
            pe.wait_ge(wext_made, 3)

            def turn_y(b):
                if normed:
                    pe.wait_ge(ln.y_made, nth(b, NT, NT))
                    if later(b):
                        pe.wait_ge(H_made, nth(b, 3, 0))
                    for t in range(NT):
                        last = pe.transpose(work[:, t // 4, (t % 4) * P:(t % 4 + 1) * P], ln.y[:, t, :], ident[:])
                    last.then_inc(work_full, 1)

            def s2_product(b):
                if normed:
                    pe.wait_ge(hT_made, nth(b, 1, 1))
                else:
                    pe.wait_ge(hT_here, nth(b, 16, 16))
                    if later(b):
                        pe.wait_ge(H_made, nth(b, 3, 0))
                for k in range(2):
                    last = pe.matmul(work[:, k, :], wa[:, FE:FE + P], hT[:, k * 512:(k + 1) * 512], start=True,
                                     stop=True)
                last.then_inc(work_full, 1)

            def H_products(b):
                for i, (t0, n) in enumerate(H_JOBS):
                    if i == 0:
                        pe.wait_ge(s2_made, nth(b, 2, 2))
                    if i == 2:
                        pe.wait_ge(H_made, nth(b, 3, 1))
                    for t in range(t0, t0 + n):
                        last = pe.matmul(work[:, i % 2, (t - t0) * FE:(t - t0 + 1) * FE], hT[:, t * P:(t + 1) * P],
                                         wa[:, 0:FE], start=True, stop=True)
                    last.then_inc(work_full, 1)

            def turn(b, t):
                pe.wait_ge(pr_made, nth(b, NT, t + 1))
                pe.wait_ge(prT_made, nth(b, NT, t + 1))
                for j in range(NT):
                    last = pe.transpose(turned[:, t % 2, j * P:(j + 1) * P], pr[:, t, j * P:(j + 1) * P], ident[:])
                last.then_inc(turn_done, 1)

            def weigh(b, s, t):
                k, q = t // HB, t % HB
                pe.wait_ge(prT_made, nth(b, NT, t + 1) + 2)
                if q == 0:
                    pe.wait_ge(v_made, nth(b, NT, (k + 1) * HB))
                for j in range(NT):
                    last = pe.matmul(acc[:, k, q, :], prT[:, t % 2, j, :], H[:, s, j, 0:F], start=(j == 0),
                                     stop=(j == NT - 1))
                last.then_inc(weighed, 1)

            for b in range(2):
                turn_y(b)
                s2_product(b)
                H_products(b)

            def step(b, s, pair, left):
                turn(b, 0)
                for t in range(NT):
                    if t + 1 < NT:
                        turn(b, t + 1)
                    if left >= 2 and t == S2_AT - 1:
                        turn_y(b + 2)
                    if left >= 2 and t == S2_AT:
                        s2_product(b + 2)
                    weigh(b, s, t)
                if left >= 2:
                    H_products(b + 2)

            pipelined(pe, B, step, 2)




def fc_phase(nc, tag, B, N, F, ident, mlp1_w, mlp1_b, W, a, mlp2_w, mlp2_b, x_in, hT_out, h_out):
    NT = N // P
    HB = NT // 2
    W2 = 2 * F
    with ExitStack() as ctx:
        ph = Phase(nc, ctx, tag)
        ln = Norm(ph, NT, F)
        w1 = ph.sb("w1", [P, W2])
        b1 = ph.sb("b1", [P, 2])
        w_in = ph.sb("w_in", [P, 2, W2])
        wT = ph.sb("wT", [P, 2, W2])
        a_in = ph.sb("a_in", [P, 2, 2])
        wx = ph.sb("wx", [P, 2, W2 + 1])
        wa1 = ph.sb("wa1", [P, 2, 1])
        wa1_wide = ph.sb("wa1_wide", [P, 2, P])
        w2 = ph.sb("w2", [P, 2, F])
        b2 = ph.sb("b2", [P, 1])
        minus1 = ph.sb("minus1", [P, 1])
        hT = ph.sb("hT", [P, N])
        o1T = ph.sb("o1T", [P, 2, 2, N])
        H = ph.sb("H", [P, 2, NT, W2 + 2])
        f2max = ph.sb("f2max", [P, 1])
        G = ph.sb("G", [P, 1])
        mG8 = ph.sb("mG8", [P, 1])
        mG2 = ph.sb("mG2", [P, 1])
        E = ph.sb("E", [P, NT])
        D = ph.sb("D", [P, NT])
        F_raw = ph.sb("F_raw", [P, N])
        F_row = ph.sb("F_row", [P, N])
        prT = ph.sb("prT", [P, 2, NT, N])
        rden = ph.sb("rden", [P, NT])
        v = ph.sb("v", [P, 2, HB, W2])
        vexp = ph.sb("vexp", [P, 2, HB, W2])
        g = ph.sb("g", [P, 2, HB, W2])
        g2T = ph.sb("g2T", [P, 2, N])
        o2T = ph.sb("o2T", [P, 2, 512])
        o2 = ph.sb("o2", [P, 2, HB, F])
        work = ph.ps("work", [P, 2, 512])
        acc = ph.ps("acc", [P, 2, 512])
        gT_ps = ph.ps("gT_ps", [P, 2, 512])
        m2_ps = ph.ps("m2_ps", [P, 512])
        nat_ps = ph.ps("nat_ps", [P, HB, F])

        w_here = ph.sem("w_here")
        w_turned = ph.sem("w_turned")
        wT_made = ph.sem("wT_made")
        wa_done = ph.sem("wa_done")
        wa_copied = ph.sem("wa_copied")
        wext_made = ph.sem("wext_made")
        ones_made = ph.sem("ones_made")
        work_full = ph.sem("work_full")
        hT_made = ph.sem("hT_made")
        o1_made = ph.sem("o1_made")
        H_made = ph.sem("H_made")
        f2max_made = ph.sem("f2max_made")
        G_made = ph.sem("G_made")
        mG_made = ph.sem("mG_made")
        ED_made = ph.sem("ED_made")
        F_made = ph.sem("F_made")
        F_cut = ph.sem("F_cut")
        prT_made = ph.sem("prT_made")
        acc_done = ph.sem("acc_done")
        rden_made = ph.sem("rden_made")
        v_made = ph.sem("v_made")
        vneg_made = ph.sem("vneg_made")
        exp1_made = ph.sem("exp1_made")
        exp2_made = ph.sem("exp2_made")
        g_made = ph.sem("g_made")
        gT_done = ph.sem("gT_done")
        g2T_made = ph.sem("g2T_made")
        m2_done = ph.sem("m2_done")
        o2T_made = ph.sem("o2T_made")
        nat_done = ph.sem("nat_done")
        o2_made = ph.sem("o2_made")
        o2T_stored = [ph.sem("o2T_stored0"), ph.sem("o2T_stored1")]
        o2_stored = [ph.sem("o2_stored0"), ph.sem("o2_stored1")]
        block = ctx.enter_context(nc.Block())
        JOBS = 8
        TURN_AT = 7

        def rows(dram, b):
            return dram[b].rearrange("(t p) f -> p t f", p=P)

        @block.sync
        def _(sp):
            def load(b, s):
                sp.dma_start(ln.x[:, s, :, :], rows(x_in, b)).then_inc(ln.x_here[s], 16)

            load(0, 0)
            sp.dma_start(w_in[:], W.rearrange("(c p) n -> p c n", p=P)).then_inc(w_here, 16)
            for k in range(2):
                for c in range(2):
                    sp.dma_start(a_in[:, c, k:k + 1], a[k * W2 + c * P:k * W2 + (c + 1) * P, :]).then_inc(w_here, 16)
            sp.dma_start(w1[:], mlp1_w).then_inc(w_here, 16)
            for c in range(2):
                sp.dma_start(b1[:, c:c + 1], mlp1_b[c * P:(c + 1) * P].rearrange("(p o) -> p o", o=1)).then_inc(w_here, 16)
            sp.dma_start(w2[:], mlp2_w.rearrange("(c p) n -> p c n", p=P)).then_inc(w_here, 16)
            sp.dma_start(b2[:], mlp2_b.rearrange("(p o) -> p o", o=1)).then_inc(w_here, 16)
            load(1, 1)
            sp.wait_ge(ln.y_made, nth(0, NT, NT))
            load(2, 0)

            def step(b, s, pair, left):
                if left >= 3:
                    ph.wait_apart(sp, ln.y_made, nth(b + 1, NT, NT))
                    load(b + 3, 1 - s)
                for k in range(2):
                    ph.wait_apart(sp, o2T_made, nth(b, 2, k + 1) + 1)
                    sp.dma_start(hT_out[b][:, k * 512:(k + 1) * 512], o2T[:, k, :]).then_inc(o2T_stored[k], 16)
                    ph.wait_apart(sp, o2_made, nth(b, 2, k + 1) + 1)
                    sp.dma_start(rows(h_out, b)[:, k * HB:(k + 1) * HB, :], o2[:, k, :, :]).then_inc(o2_stored[k], 16)

            pipelined(sp, B, step, 4)
            for k in range(2):
                sp.wait_ge(o2T_stored[k], 16 * B + 16)
                sp.wait_ge(o2_stored[k], 16 * B + 16)

        @block.gpsimd
        def _(pool):
            for s_, n in ((g2T_made, 2), (v_made, 2), (gT_done, 2), (m2_done, 2), (o2T_made, 1), (nat_done, 2),
                          (o2_made, 1), (o2T_stored[0], 16), (o2T_stored[1], 16), (o2_stored[0], 16),
                          (o2_stored[1], 16)):
                pool.sem_inc(s_, n)
            pool.memset(minus1[:], -1.0).then_inc(ones_made, 1)
            for s_ in range(2):
                pool.memset(H[:, s_, :, W2 + 1:W2 + 2], 1.0).then_inc(ones_made, 1)
            ln.gpsimd_consts(pool)

            def reduce_G(b):
                ph.wait_apart(pool, f2max_made, nth(b, 1, 1))
                pool.partition_all_reduce(G[:], f2max[:], P, bass.bass_isa.ReduceOp.max).then_inc(G_made, 1)

            ln.gpsimd(pool, 0)
            ln.gpsimd(pool, 1)
            reduce_G(0)

            def step(b, s, pair, left):
                if left >= 2:
                    ln.gpsimd(pool, b + 2)
                if left >= 1:
                    reduce_G(b + 1)

            pipelined(pool, B, step, 2)

        @block.vector
        def _(dve):
            ln.statistics(dve, 0, 0, 0)
            dve.wait_ge(w_here, 16 * 10)
            dve.wait_ge(w_turned, 1)
            dve.tensor_copy(wT[:].rearrange("p c (e m) -> p c e m", e=2),
                            gT_ps[:, 0, :].rearrange("p (c e m) -> p c e m", c=2, e=2)).then_inc(wT_made, 1)
            ln.scale(dve, 0, 0)
            dve.tensor_copy(wx[:, :, 1:W2 + 1], w_in[:]).then_inc(wext_made, 1)
            dve.wait_ge(wa_done, 1)
            for c in range(2):
                dve.tensor_copy(wa1[:, c, :], gT_ps[:, 1, 2 * c:2 * c + 1]).then_inc(wa_copied, 1)
                dve.tensor_copy(wx[:, c, 0:1], gT_ps[:, 1, 2 * c + 1:2 * c + 2]).then_inc(wext_made, 1)
            dve.wait_ge(wa_copied, 2)
            for c in range(2):
                dve.tensor_copy(wa1_wide[:, c, :], wa1[:, c, :].broadcast_to([P, P])).then_inc(wext_made, 1)

            def norm(b, s):
                if later(b):
                    dve.wait_ge(work_full, nth(b, JOBS, 1 - JOBS))
                ln.scale(dve, b, s)

            def top_f2(b, s):
                dve.wait_ge(H_made, nth(b, 4, 4))
                if later(b):
                    dve.wait_ge(G_made, nth(b, 1, 0))
                dve.tensor_reduce(f2max[:], H[:, s, :, 0], AX_X, ALU.max).then_inc(f2max_made, 1)

            def minus_G(b):
                dve.wait_ge(G_made, nth(b, 1, 1))
                if later(b):
                    dve.wait_ge(F_made, nth(b, 1, 0))
                dve.tensor_scalar(mG8[:], G[:], -(1.0 - SLOPE), None, ALU.mult).then_inc(mG_made, 1)
                dve.tensor_scalar(mG2[:], G[:], -SLOPE, None, ALU.mult).then_inc(mG_made, 1)

            def cut_F(b):
                dve.wait_ge(F_made, nth(b, 1, 1))
                if later(b):
                    dve.wait_ge(prT_made, nth(b, NT, 0))
                dve.tensor_scalar(F_row[:], F_raw[:], 1.0, None, ALU.min).then_inc(F_cut, 1)
                dve.wait_ge(F_cut, nth(b, 1, 1))
                dve.wait_ge(ED_made, nth(b, 2, 2))

            def probs(b, s, j0, j1):
                for j in range(j0, j1):
                    dve.tensor_scalar(prT[:, s, j, :], F_row[:], E[:, j:j + 1], D[:, j:j + 1], ALU.max,
                                      ALU.mult).then_inc(prT_made, 1)

            def divide(b, t):
                dve.wait_ge(acc_done, nth(b, NT, t + 1))
                dve.reciprocal(rden[:, t:t + 1], acc[:, t % 2, W2:W2 + 1]).then_inc(rden_made, 1)
                dve.wait_ge(rden_made, nth(b, NT, t + 1))
                dve.tensor_scalar(v[:, t // HB, t % HB, :], acc[:, t % 2, 0:W2], rden[:, t:t + 1], None,
                                  ALU.mult).then_inc(v_made, 1)

            def negative(b, k):
                dve.wait_ge(v_made, nth(b, NT, (k + 1) * HB) + 2)
                dve.tensor_scalar(vexp[:, k, :, :], v[:, k, :, :], 0.0, None, ALU.min).then_inc(vneg_made, 1)

            def positive(b, k):
                dve.wait_ge(exp2_made, nth(b, 2, k + 1))
                dve.wait_ge(gT_done, nth(b, 2, k + 1))
                dve.scalar_tensor_tensor(out=g[:, k, :, :], in0=v[:, k, :, :], scalar=0.0, in1=vexp[:, k, :, :],
                                         op0=ALU.max, op1=ALU.add).then_inc(g_made, 1)

            def add_o1(b, s, k):
                dve.wait_ge(gT_done, nth(b, 2, k + 1) + 2)
                dve.wait_ge(m2_done, nth(b, 2, k + 1))
                dve.scalar_tensor_tensor(out=g2T[:, :, k * 512:(k + 1) * 512], in0=gT_ps[:], scalar=-1.0,
                                         in1=o1T[:, s, :, k * 512:(k + 1) * 512], op0=ALU.add,
                                         op1=ALU.add).then_inc(g2T_made, 1)

            ln.statistics(dve, 1, 1, 0)
            norm(1, 1)
            top_f2(0, 0)
            minus_G(0)
            cut_F(0)
            probs(0, 0, 0, NT)
            divide(0, 0)
            divide(0, 1)

            def step(b, s, pair, left):
                more, n, o = left >= 1, b + 1, 1 - s
                divide(b, 2)
                if left >= 2:
                    ln.statistics(dve, b + 2, s, pair + 1)
                divide(b, 3)
                negative(b, 0)
                if left >= 2:
                    norm(b + 2, s)
                divide(b, 4)
                positive(b, 0)
                if more:
                    top_f2(n, o)
                divide(b, 5)
                add_o1(b, s, 0)
                if more:
                    minus_G(n)
                    cut_F(n)
                    probs(n, o, 0, HB)
                divide(b, 6)
                if more:
                    probs(n, o, HB, NT)
                divide(b, 7)
                negative(b, 1)
                if more:
                    divide(n, 0)
                positive(b, 1)
                add_o1(b, s, 1)
                if more:
                    divide(n, 1)

            pipelined(dve, B, step, 2)

        @block.scalar
        def _(act):
            two = lambda ap: ap.rearrange("p a n -> p (a n)")

            def take_hT(b):
                act.wait_ge(work_full, nth(b, JOBS, 1))
                act.activation(hT[:], two(work[:]), ACT.Relu).then_inc(hT_made, 1)

            def take_o1(b, s, c):
                act.wait_ge(work_full, nth(b, JOBS, 2 + c))
                if c == 0 and later(b):
                    act.wait_ge(g2T_made, nth(b, 2, 0))
                act.activation(o1T[:, s, c, :], two(work[:]), ACT.Relu, bias=b1[:, c:c + 1]).then_inc(o1_made, 1)

            def take_H(b, s, i):
                act.wait_ge(work_full, nth(b, JOBS, 4 + i))
                act.activation(H[:, s, 2 * i:2 * i + 2, 0:W2 + 1], work[:, :, 0:W2 + 1], ACT.Copy).then_inc(H_made, 1)

            def exp_f2(b, s):
                act.wait_ge(mG_made, nth(b, 2, 2))
                if later(b):
                    act.wait_ge(prT_made, nth(b, NT, 0))
                act.activation(E[:], H[:, s, :, 0], ACT.Exp, bias=mG8[:], scale=1.0 - SLOPE).then_inc(ED_made, 1)
                act.activation(D[:], H[:, s, :, 0], ACT.Exp, bias=mG2[:], scale=SLOPE).then_inc(ED_made, 1)

            def exp_f1(b):
                act.wait_ge(work_full, nth(b, JOBS, 8))
                if later(b):
                    act.wait_ge(F_cut, nth(b, 1, 0))
                act.activation(F_raw[:], two(work[:]), ACT.Exp, bias=mG8[:], scale=-(1.0 - SLOPE)).then_inc(F_made, 1)

            def elu_exps(b, k):
                act.wait_ge(vneg_made, nth(b, 2, k + 1))
                act.activation(vexp[:, k, :, :], vexp[:, k, :, :], ACT.Exp).then_inc(exp1_made, 1)
                act.wait_ge(exp1_made, nth(b, 2, k + 1))
                act.activation(vexp[:, k, :, :], vexp[:, k, :, :], ACT.Exp, bias=minus1[:]).then_inc(exp2_made, 1)

            def take_o2T(b, k):
                act.wait_ge(m2_done, nth(b, 2, k + 1) + 2)
                act.wait_ge(o2T_stored[k], nth(b, 16, 16))
                act.wait_ge(nat_done, nth(b, 2, k + 1))
                act.activation(o2T[:, k, :], m2_ps[:], ACT.Relu, bias=b2[:]).then_inc(o2T_made, 1)

            def take_o2(b, k):
                act.wait_ge(nat_done, nth(b, 2, k + 1) + 2)
                act.wait_ge(o2_stored[k], nth(b, 16, 16))
                act.activation(o2[:, k, :, :], nat_ps[:], ACT.Copy).then_inc(o2_made, 1)

            act.wait_ge(w_here, 16 * 10)
            act.wait_ge(ones_made, 3)
            take_hT(0)
            take_o1(0, 0, 0)
            take_o1(0, 0, 1)
            for i in range(4):
                take_H(0, 0, i)
            exp_f2(0, 0)
            exp_f1(0)
            take_hT(1)
            take_o1(1, 1, 0)

            def step(b, s, pair, left):
                more, n, o = left >= 1, b + 1, 1 - s
                if more:
                    take_o1(n, o, 1)
                    take_H(n, o, 0)
                    take_H(n, o, 1)
                    take_H(n, o, 2)
                elu_exps(b, 0)
                if more:
                    take_H(n, o, 3)
                    exp_f2(n, o)
                    exp_f1(n)
                take_o2T(b, 0)
                take_o2(b, 0)
                elu_exps(b, 1)
                take_o2T(b, 1)
                if left >= 2:
                    take_hT(b + 2)
                take_o2(b, 1)
                if left >= 2:
                    take_o1(b + 2, s, 0)

            pipelined(act, B, step, 2)

        @block.tensor
        def _(pe):
            pe.wait_ge(w_here, 16 * 10)
            for e in range(2):
                for c in range(2):
                    last = pe.transpose(gT_ps[:, 0, (2 * e + c) * P:(2 * e + c + 1) * P], w_in[:, c, e * P:(e + 1) * P],
                                        ident[:])
            last.then_inc(w_turned, 1)

            def job(b, s, n):
                if n == 0:
                    pe.wait_ge(ln.y_made, nth(b, NT, NT))
                    if later(b):
                        pe.wait_ge(F_made, nth(b, 1, 0))
                    for t in range(NT):
                        last = pe.transpose(work[:, t // 4, (t % 4) * P:(t % 4 + 1) * P], ln.y[:, t, :], ident[:])
                elif n in (1, 2):
                    pe.wait_ge(hT_made, nth(b, 1, 1))
                    if n == 2:
                        pe.wait_ge(o1_made, nth(b, 2, 1))
                    c = n - 1
                    for k in range(2):
                        last = pe.matmul(work[:, k, :], w1[:, c * P:(c + 1) * P], hT[:, k * 512:(k + 1) * 512],
                                         start=True, stop=True)
                elif n < 7:
                    i = n - 3
                    if i == 0:
                        pe.wait_ge(o1_made, nth(b, 2, 2))
                    else:
                        pe.wait_ge(H_made, nth(b, 4, i))
                    for q in range(2):
                        t = 2 * i + q
                        for c in range(2):
                            last = pe.matmul(work[:, q, 0:W2 + 1], o1T[:, s, c, t * P:(t + 1) * P], wx[:, c, :],
                                             start=(c == 0), stop=(c == 1))
                else:
                    pe.wait_ge(H_made, nth(b, 4, 4))
                    for k in range(2):
                        for c in range(2):
                            last = pe.matmul(work[:, k, :], wa1_wide[:, c, :], o1T[:, s, c, k * 512:(k + 1) * 512],
                                             start=(c == 0), stop=(c == 1))
                last.then_inc(work_full, 1)

            def weigh(b, s, t, half):
                if half == 0:
                    pe.wait_ge(v_made, nth(b, NT, t + 1))
                for j in range(half * HB, (half + 1) * HB):
                    if t == 0:
                        pe.wait_ge(prT_made, nth(b, NT, j + 1))
                    last = pe.matmul(acc[:, t % 2, 0:W2 + 1], prT[:, s, j, t * P:(t + 1) * P],
                                     H[:, s, j, 1:W2 + 2], start=(j == 0), stop=(j == NT - 1))
                if half == 1:
                    last.then_inc(acc_done, 1)

            def turn_g(b, k):
                pe.wait_ge(g_made, nth(b, 2, k + 1))
                pe.wait_ge(g2T_made, nth(b, 2, k) + 2)
                for q in range(HB):
                    for c in range(2):
                        last = pe.transpose(gT_ps[:, c, q * P:(q + 1) * P], g[:, k, q, c * P:(c + 1) * P], ident[:])
                last.then_inc(gT_done, 1)

            def mlp2(b, k):
                pe.wait_ge(g2T_made, nth(b, 2, k + 1) + 2)
                pe.wait_ge(o2T_made, nth(b, 2, k) + 1)
                for c in range(2):
                    last = pe.matmul(m2_ps[:], w2[:, c, :], g2T[:, c, k * 512:(k + 1) * 512], start=(c == 0),
                                     stop=(c == 1))
                last.then_inc(m2_done, 1)

            def turn_o2(b, k):
                pe.wait_ge(o2T_made, nth(b, 2, k + 1) + 1)
                pe.wait_ge(o2_made, nth(b, 2, k) + 1)
                for q in range(HB):
                    last = pe.transpose(nat_ps[:, q, :], o2T[:, k, q * P:(q + 1) * P], ident[:])
                last.then_inc(nat_done, 1)

            job(0, 0, 0)
            pe.wait_ge(wT_made, 1)
            for c in range(2):
                for e in range(2):
                    last = pe.matmul(gT_ps[:, 1, 2 * c:2 * c + 2], wT[:, e, c * P:(c + 1) * P], a_in[:, e, :],
                                     start=(e == 0), stop=(e == 1))
            last.then_inc(wa_done, 1)
            for n in (1, 2):
                job(0, 0, n)
            pe.wait_ge(wext_made, 5)
            pe.wait_ge(ones_made, 3)
            for n in range(3, JOBS):
                job(0, 0, n)
            for t in range(2):
                for half in range(2):
                    weigh(0, 0, t, half)
            job(1, 1, 0)
            job(1, 1, 1)

            def step(b, s, pair, left):
                more = left >= 1
                for i in range(2 * (NT - 2)):
                    weigh(b, s, 2 + i // 2, i % 2)
                    if more and i + 2 < JOBS:
                        job(b + 1, 1 - s, i + 2)
                    if i == TURN_AT:
                        turn_g(b, 0)
                    if i == TURN_AT + 3:
                        mlp2(b, 0)
                turn_o2(b, 0)
                if more:
                    weigh(b + 1, 1 - s, 0, 0)
                    weigh(b + 1, 1 - s, 0, 1)
                turn_g(b, 1)
                if more:
                    weigh(b + 1, 1 - s, 1, 0)
                mlp2(b, 1)
                if more:
                    weigh(b + 1, 1 - s, 1, 1)
                if left >= 2:
                    job(b + 2, s, 0)
                turn_o2(b, 1)
                if left >= 2:
                    job(b + 2, s, 1)

            pipelined(pe, B, step, 2)




class Jobs:

    PREP = {3: [("turn", 0), ("turn", 1)], 4: [("q", 0)], 5: [("q", 1)], 7: [("v", 0)], 8: [("v", 1)],
            10: [("k", 0)], 11: [("k", 1)]}
    FINISH = {3: [("R", 3), ("R", 0)], **{u: [("R", u)] for u in (2, *range(4, 16))}}
    FINISH_TAIL = {1: [("R", 1)]}
    LATE_TAIL = {0: [("O", 0), ("O", 1)]}
    R_ORDER = [1, 2, 3, 0] + list(range(4, 16))

    def __init__(self, B):
        self.B = B

    def does(self, b):
        if not isinstance(b, int):
            return True, True, True
        return b + 1 < self.B, 1 <= b <= self.B, b >= 2

    def at(self, b, u):
        prep, finish, _ = self.does(b)
        return (self.PREP.get(u, []) if prep else []) + (self.FINISH.get(u, []) if finish else [])

    def tail(self, b, u):
        _, finish, late = self.does(b)
        return (self.LATE_TAIL.get(u, []) if late else []) + (self.FINISH_TAIL.get(u, []) if finish else [])

    def order(self, b):
        return [j for u in range(16) for j in self.at(b, u) + self.tail(b, u)]

    def half_before(self, b):
        if isinstance(b, int) and (b <= 2 or b >= self.B - 1):
            return sum(len(self.order(i)) for i in range(-1, b)) // 2
        full = len(self.order(2)) // 2
        return (b - 2) * full + self.half_before(2)

    def index(self, b, job):
        return self.order(b).index(job)

    def bank(self, b, job):
        return self.index(b, job) % 2

    def count(self, b, job):
        return self.half_before(b) * 2 + (self.index(b, job) + 1)

    def uses(self, b, job):
        return self.half_before(b) + (self.index(b, job) // 2 + 1)


def attention_phase(nc, tag, B, N, F, heads, clip_high, ident, Wq, bq, Wk, bk, Wv, bv, Wo, bo, gamma, beta, x_in,
                    h_scratch, x_out, bias_dram, edge_bias):
    NT = N // P
    D = F // heads
    HALF = 512
    UN = 2 * NT
    SCALE = 1.0 / math.sqrt(D)
    jobs = Jobs(B)
    with ExitStack() as ctx:
        ph = Phase(nc, ctx, tag)
        ln = Norm(ph, NT, F, buffers=1)
        wT = ph.sb("wT", [P, 4, F])
        bias_q = ph.sb("bias_q", [P, 1])
        bias_k = ph.sb("bias_k", [P, 1])
        rows_in = ph.sb("rows_in", [P, 4, F])
        hot = ph.sb("hot", [P, 3 * UN])
        pick = ph.sb("pick", [P, UN, P], F32R)
        hT = ph.sb("hT", [P, N])
        hi = ph.sb("hi", [P, N], F32R)
        lo = ph.sb("lo", [P, N], F32R)
        qs = ph.sb("qs", [P, 2, heads, N], F32R)
        ks = ph.sb("ks", [P, 2, heads, N], F32R)
        vn = ph.sb("vn", [P, 2, NT, F])
        wt = ph.sb("wt", [P, 2, heads, HALF])
        ctxu = ph.sb("ctxu", [P, UN + 1, HALF])
        rec_hi = ph.sb("rec_hi", [P, HALF], F32R)
        rec_lo = ph.sb("rec_lo", [P, HALF], F32R)
        part = ph.sb("part", [P, 2, HALF])
        rec = hT[:, 0:HALF]
        total = ph.sb("total", [P, 2, HALF])
        z = ph.sb("z", [P, NT, F])
        w_in = z[:, 0:4, :]
        z_stats = ph.sb("z_stats", [P, NT, 6])
        z_mv = ph.sb("z_mv", [P, NT, 2])
        z_eps = ph.sb("z_eps", [P, NT])
        z_rstd = ph.sb("z_rstd", [P, NT])
        z_nmr = ph.sb("z_nmr", [P, NT])
        xe = ph.sb("xe", [P, NT, F])
        scores = ph.ps("scores", [P, heads, HALF])
        ctx_ps = ph.ps("ctx_ps", [P, HALF])
        sums = ph.ps("sums", [P, HALF])
        work = ph.ps("work", [P, 2, HALF])

        w_here = ph.sem("w_here")
        w_turned = ph.sem("w_turned")
        wT_made = ph.sem("wT_made")
        consts_zeroed = ph.sem("consts_zeroed")
        hot_made = ph.sem("hot_made")
        pick_made = ph.sem("pick_made")
        pick_rounded = ph.sem("pick_rounded")
        h_stored = ph.sem("h_stored")
        work_full = ph.sem("work_full")
        work_used = [ph.sem("work_used0"), ph.sem("work_used1")]
        hi_made = ph.sem("hi_made")
        q_stacked = ph.sem("q_stacked")
        k_stacked = ph.sem("k_stacked")
        qk_done = ph.sem("qk_done")
        exp_made = ph.sem("exp_made")
        wt_made = ph.sem("wt_made")
        pv_done = ph.sem("pv_done")
        ctx_out = ph.sem("ctx_out")
        sums_out = ph.sem("sums_out")
        rec_made = ph.sem("rec_made")
        rec_hi_made = ph.sem("rec_hi_made")
        rec_split = ph.sem("rec_split")
        added = ph.sem("added")
        z_here = ph.sem("z_here")
        xe_here = ph.sem("xe_here")
        z_biased = ph.sem("z_biased")
        xe_biased = ph.sem("xe_biased")
        z_stats_made = ph.sem("z_stats_made")
        z_mv_made = ph.sem("z_mv_made")
        z_eps_added = ph.sem("z_eps_added")
        z_rstd_made = ph.sem("z_rstd_made")
        z_nmr_made = ph.sem("z_nmr_made")
        z_normed = ph.sem("z_normed")
        z_scaled = ph.sem("z_scaled")
        out_made = ph.sem("out_made")
        stored = ph.sem("stored")
        bias_here = ph.sem("bias_here")
        block = ctx.enter_context(nc.Block())
        WEIGHT_DMAS = 10

        def rows(dram, b):
            return dram[b].rearrange("(t p) f -> p t f", p=P)

        def parts(kind, b):
            if kind == "k" and isinstance(b, int) and b == 0:
                return [w[:].rearrange("p a n -> p (a n)").bitcast(F32R) for w in (total, part)]
            return hi[:], lo[:]

        def hot_of(u):
            return hot[:, UN - 1 - u:UN - 1 - u + D]

        def unit(s, u):
            return ctxu[:, u if u > 0 else UN * s, :]

        def run_slots(eng, slot):
            for b in range(2):
                slot(b, b % 2, *jobs.does(b))
            with eng.Fori(0, (B - 4) // 2) as pair:
                for s in range(2):
                    slot(pair * 2 + (2 + s), s, True, True, True)
            for b in range(B - 2, B + 2):
                slot(b, b % 2, *jobs.does(b))

        def ahead(b):
            return not isinstance(b, int) or b + 2 < B

        @block.sync
        def _(sp):
            def load(b):
                sp.dma_start(ln.x[:, 0, :, :], rows(x_in, b)).then_inc(ln.x_here[0], 16)

            def store_h(b):
                ph.wait_apart(sp, ln.y_made, nth(b, NT, NT))
                sp.dma_start(rows(h_scratch, b), ln.y[:]).then_inc(h_stored, 16)

            def stack(slot_b, s, kind):
                h, l = parts(kind, slot_b + 1)
                dst, sem, groups = (qs, q_stacked, (h, l, h, l)) if kind == "q" else (ks, k_stacked, (h, h, l, l))
                for k in range(2):
                    ph.wait_apart(sp, work_used[jobs.bank(slot_b, (kind, k))], jobs.uses(slot_b, (kind, k)))
                for g, src in enumerate(groups):
                    for head in range(heads):
                        sp.dma_start(dst[g * D:(g + 1) * D, s, head, :].bitcast(F32),
                                     src[head * D:(head + 1) * D, :].bitcast(F32)).then_inc(sem, 16)

            load(0)
            for i, w in enumerate((Wq, Wk, Wv, Wo)):
                sp.dma_start(w_in[:, i, :], w).then_inc(w_here, 16)
            for t, w in ((bias_q, bq), (bias_k, bk)):
                sp.dma_start(t[:], w.rearrange("(p o) -> p o", o=1)).then_inc(w_here, 16)
            for i, w in enumerate((bv, bo, gamma, beta)):
                sp.dma_start(rows_in[:, i, :], w.rearrange("(o f) -> o f", o=1).broadcast_to([P, F])).then_inc(w_here, 16)
            store_h(0)
            load(1)
            stack(-1, 0, "q")
            stack(-1, 0, "k")

            def slot(b, s, prep, finish, late):
                if prep:
                    store_h(b + 1)
                    if ahead(b):
                        load(b + 2)
                    stack(b, 1 - s, "q")
                if isinstance(b, int) and b == B:
                    sp.wait_ge(wt_made, nth(B, 2 * UN, 0))
                    sp.dma_start(edge_bias, bias_dram).then_inc(bias_here, 16)
                if late:
                    ph.wait_apart(sp, out_made, nth(b - 1, 1, 0))
                    sp.dma_start(rows(x_out, b - 2), xe[:]).then_inc(stored, 16)
                if finish:
                    if late:
                        ph.wait_apart(sp, stored, nth(b - 1, 16, 0))
                    ph.wait_apart(sp, h_stored, nth(b, 16, 0))
                    sp.dma_start(z[:], rows(h_scratch, b - 1)).then_inc(z_here, 16)
                    sp.dma_start(xe[:], rows(x_in, b - 1)).then_inc(xe_here, 16)
                if prep:
                    stack(b, 1 - s, "k")

            run_slots(sp, slot)
            sp.wait_ge(stored, 16 * B)
            sp.wait_ge(bias_here, 16)

        @block.gpsimd
        def _(pool):
            pool.memset(hot[:], 0.0).then_inc(consts_zeroed, 1)
            pick_f = ctxu[:, 0:UN * P // HALF, :].rearrange("p a (b m) -> p (a b) m", m=P)
            pool.memset(ctxu[:, 0:UN * P // HALF, :], 0.0).then_inc(consts_zeroed, 1)
            pool.wait_ge(consts_zeroed, 2)
            pool.memset(hot[:, UN - 1:2 * UN:UN], 1.0).then_inc(hot_made, 1)
            ln.gpsimd_consts(pool)
            ln.gpsimd(pool, 0)
            sel = pick_f.rearrange("p u (h d) -> p u h d", h=heads)
            pool.affine_select(out=sel, in_=sel, compare_op=ALU.not_equal, fill=1.0, base=0,
                               pattern=[[-1, UN], [-D, heads], [0, D]], channel_multiplier=1).then_inc(pick_made, 1)
            ln.gpsimd(pool, 1)
            pool.wait_ge(w_here, 16 * WEIGHT_DMAS)

            def add(b, n):
                u = jobs.R_ORDER[n + 2]
                pool.wait_ge(work_used[jobs.bank(b, ("R", u))], jobs.uses(b, ("R", u)))
                if later(b, 2) or n > 0:
                    pool.wait_ge(added, nth(b - 1, UN - 2, n))
                pool.tensor_tensor(total[:, u % 2, :], total[:, u % 2, :], part[:, n % 2, :],
                                   ALU.add).then_inc(added, 1)

            def slot(b, s, prep, finish, late):
                if late:
                    pool.wait_ge(z_eps_added, nth(b - 2, 1, 1))
                    pool.tensor_tensor(z_rstd[:], z_eps[:], ln.minus_half[:], ALU.pow).then_inc(z_rstd_made, 1)
                for n in range(UN - 2):
                    if finish:
                        add(b, n)
                    if late and n == 3:
                        pool.wait_ge(z_normed, nth(b - 2, NT, NT))
                        pool.tensor_tensor(z[:], z[:], rows_in[:, 2:3, :].broadcast_to([P, NT, F]),
                                           ALU.mult).then_inc(z_scaled, 1)
                    if late and n == 4:
                        pool.wait_ge(z_scaled, nth(b - 2, 1, 1))
                        pool.wait_ge(xe_biased, nth(b - 2, 1, 1))
                        pool.tensor_tensor(xe[:], xe[:], z[:], ALU.add).then_inc(out_made, 1)
                    if finish and n == UN - 5:
                        pool.wait_ge(z_here, nth(b - 1, 16, 16))
                        pool.tensor_tensor(z[:], z[:], rows_in[:, 1:2, :].broadcast_to([P, NT, F]),
                                           ALU.add).then_inc(z_biased, 1)
                if ahead(b):
                    ln.gpsimd(pool, b + 2)
                if finish:
                    pool.wait_ge(xe_here, nth(b - 1, 16, 16))
                    pool.tensor_tensor(xe[:], xe[:], rows_in[:, 3:4, :].broadcast_to([P, NT, F]),
                                       ALU.add).then_inc(xe_biased, 1)

            run_slots(pool, slot)

        @block.vector
        def _(dve):
            ln.statistics(dve, 0, 0, 0)
            ln.minus_mean(dve, 0)
            dve.wait_ge(w_turned, 1)
            dve.tensor_copy(wT[:], work[:, 0, :].rearrange("p (i f) -> p i f", i=4)).then_inc(wT_made, 1)

            def clip(b, u, p):
                dve.wait_ge(exp_made, nth(b, 2 * UN, 2 * u + p + 1))
                c, k = u // 2, u % 2
                w = wt[:, u % 2, 2 * p:2 * p + 2, :]
                dve.scalar_tensor_tensor(
                    out=w, in0=w, scalar=CLIP_LO, in1=clip_high[:, c:c + 1, k * HALF:(k + 1) * HALF].broadcast_to(
                        [P, 2, HALF]), op0=ALU.max, op1=ALU.min).then_inc(wt_made, 1)

            def reciprocals(b, k):
                cols = slice(k * HALF // 2, (k + 1) * HALF // 2)
                if k == 0:
                    dve.wait_ge(sums_out, nth(b, 1, 1))
                dve.reciprocal(rec[:, cols], rec[:, cols]).then_inc(rec_made, 1)
                if k == 1:
                    dve.wait_ge(rec_made, nth(b, 2, 2))
                    dve.tensor_copy(rec_hi[:], rec).then_inc(rec_hi_made, 1)
                    dve.wait_ge(rec_hi_made, nth(b, 1, 1))
                    dve.tensor_tensor(rec_lo[:], rec, rec_hi[:].bitcast(F32), ALU.subtract).then_inc(rec_split, 1)

            def do_job(job, b, s):
                kind, k = job
                if kind == "turn":
                    return
                bank = jobs.bank(b, job)
                res, used = work[:, bank, :], work_used[bank]
                if kind in ("q", "k"):
                    j = k + (2 if kind == "k" else 0)
                    dve.wait_ge(hi_made, nth(b + 1, 4, j + 1))
                    cols = slice(k * HALF, (k + 1) * HALF)
                    high, low = parts(kind, b + 1)
                    dve.scalar_tensor_tensor(out=low[:, cols], in0=res, scalar=(bias_q if kind == "q" else bias_k)[:],
                                             in1=high[:, cols].bitcast(F32), op0=ALU.add,
                                             op1=ALU.subtract).then_inc(used, 1)
                    return
                dve.wait_ge(work_full, jobs.count(b, job))
                if kind == "v":
                    dve.tensor_tensor(vn[:, 1 - s, 4 * k:4 * k + 4, :], res.rearrange("p (t f) -> p t f", f=F),
                                      rows_in[:, 0:1, :].broadcast_to([P, 4, F]), ALU.add).then_inc(used, 1)
                elif kind == "R":
                    dve.wait_ge(ctx_out, nth(b - 1, UN, k + 1))
                    n = jobs.R_ORDER.index(k) - 2
                    dst = total[:, k % 2, :] if n < 0 else part[:, n % 2, :]
                    if n >= 2:
                        dve.wait_ge(added, nth(b - 1, UN - 2, n - 1))
                    dve.tensor_tensor(dst, res, unit(1 - s, k), ALU.mult).then_inc(used, 1)
                else:
                    if k == 0:
                        dve.wait_ge(z_biased, nth(b - 2, 1, 1))
                    zs = z[:, 4 * k:4 * k + 4, :]
                    dve.tensor_tensor(zs, res.rearrange("p (t f) -> p t f", f=F), zs, ALU.add).then_inc(used, 1)

            def z_statistics(slot_b):
                for k in range(2):
                    dve.wait_ge(work_used[jobs.bank(slot_b, ("O", k))], jobs.uses(slot_b, ("O", k)))
                for t in range(NT):
                    dve.bn_stats(z_stats[:, t, :], z[:, t, :]).then_inc(z_stats_made, 1)
                ph.wait_apart(dve, z_stats_made, nth(slot_b - 2, NT, NT))
                for t in range(NT):
                    dve.bn_aggr(z_mv[:, t, :], z_stats[:, t, :]).then_inc(z_mv_made, 1)
                dve.wait_ge(z_mv_made, nth(slot_b - 2, NT, NT))
                dve.tensor_scalar(z_eps[:], z_mv[:, :, 1], LN_EPS, None, ALU.add).then_inc(z_eps_added, 1)

            def z_minus_mean(b):
                dve.wait_ge(z_rstd_made, nth(b, 1, 1))
                dve.scalar_tensor_tensor(out=z_nmr[:], in0=z_mv[:, :, 0], scalar=-1.0, in1=z_rstd[:], op0=ALU.mult,
                                         op1=ALU.mult).then_inc(z_nmr_made, 1)

            dve.wait_ge(w_here, 16 * WEIGHT_DMAS)
            for u in range(16):
                for j in jobs.at(-1, u):
                    do_job(j, -1, 1)
            pick_f = ctxu[:, 0:UN * P // HALF, :].rearrange("p a (b m) -> p (a b) m", m=P)
            dve.wait_ge(pick_made, 1)
            dve.tensor_copy(pick[:], pick_f).then_inc(pick_rounded, 1)
            ln.statistics(dve, 1, 0, 1)
            clip(0, 0, 0)
            clip(0, 0, 1)
            ln.minus_mean(dve, 1)

            def slot(b, s, prep, finish, late):
                for u in range(UN):
                    if u <= 1 and finish:
                        reciprocals(b - 1, u)
                    if u == 4 and late:
                        z_minus_mean(b - 2)
                    for j in jobs.at(b, u):
                        do_job(j, b, s)
                    if isinstance(b, int) and b >= B:
                        pass
                    elif u + 1 < UN:
                        clip(b, u + 1, 0)
                        clip(b, u + 1, 1)
                    elif prep:
                        clip(b + 1, 0, 0)
                        clip(b + 1, 0, 1)
                    for j in jobs.tail(b, u):
                        do_job(j, b, s)
                    if u == 13 and ahead(b):
                        ln.statistics(dve, b + 2, 0, b + 2)
                    if u == 15 and ahead(b):
                        ln.minus_mean(dve, b + 2)
                    if u == 2 and late:
                        z_statistics(b)

            run_slots(dve, slot)

        @block.scalar
        def _(act):
            def exps(b, u, p):
                act.wait_ge(qk_done, nth(b, 2 * UN, 2 * u + p + 1))
                if later(b) or u >= 2:
                    act.wait_ge(pv_done, nth(b, UN, u - 1))
                act.activation(wt[:, u % 2, 2 * p:2 * p + 2, :], scores[:, 2 * p:2 * p + 2, :], ACT.Exp,
                               scale=SCALE).then_inc(exp_made, 1)

            def take_ctx(b, s, u, slot_b):
                act.wait_ge(pv_done, nth(b, UN, u + 1))
                if u > 0 and jobs.does(b)[1]:
                    act.wait_ge(work_used[jobs.bank(b, ("R", u))], jobs.uses(b, ("R", u)))
                elif u == 0 and later(b, 2):
                    act.wait_ge(added, nth(b - 1, UN - 2, 0))
                act.activation(unit(s, u), ctx_ps[:], ACT.Copy).then_inc(ctx_out, 1)

            def normalise(b):
                if later(b):
                    act.wait_ge(work_full, jobs.count(b - 2, ("turn", 1)))
                    act.wait_ge(h_stored, nth(b, 16, 0))
                ln.relu(act, b, 0)

            def normalise_z(b):
                act.wait_ge(z_nmr_made, nth(b, 1, 1))
                for t in range(NT):
                    act.activation(z[:, t, :], z[:, t, :], ACT.Identity, bias=z_nmr[:, t:t + 1],
                                   scale=z_rstd[:, t:t + 1]).then_inc(z_normed, 1)

            def do_job(job, b):
                kind, k = job
                if kind not in ("turn", "q", "k"):
                    return
                cols = slice(k * HALF, (k + 1) * HALF)
                bank = jobs.bank(b, job)
                act.wait_ge(work_full, jobs.count(b, job))
                if kind == "turn":
                    if k == 0 and later(b):
                        act.wait_ge(rec_split, nth(b, 1, 0))
                    act.activation(hT[:, cols], work[:, bank, :], ACT.Copy).then_inc(work_used[bank], 1)
                else:
                    n = 16 * 4 * heads
                    if later(b, 0):
                        act.wait_ge(*((q_stacked, nth(b + 1, n, n)) if kind == "k" else
                                      (k_stacked, nth(b + 1, n, 0))))
                    act.activation(parts(kind, b + 1)[0][:, cols], work[:, bank, :], ACT.Identity,
                                   bias=(bias_q if kind == "q" else bias_k)[:]).then_inc(hi_made, 1)

            act.wait_ge(w_here, 16 * WEIGHT_DMAS)
            normalise(0)
            for u in range(16):
                for j in jobs.at(-1, u):
                    do_job(j, -1)
            act.wait_ge(pick_rounded, 1)
            exps(0, 0, 0)
            exps(0, 0, 1)

            def slot(b, s, prep, finish, late):
                attend = not isinstance(b, int) or b < B
                for u in range(UN):
                    if attend and u >= 1:
                        take_ctx(b, s, u - 1, b)
                    if u == 0 and finish:
                        take_ctx(b - 1, 1 - s, UN - 1, b)
                        act.activation(rec, sums[:], ACT.Copy).then_inc(sums_out, 1)
                    for j in jobs.at(b, u):
                        do_job(j, b)
                    if attend and u + 1 < UN:
                        exps(b, u + 1, 0)
                        exps(b, u + 1, 1)
                    elif attend and prep:
                        exps(b + 1, 0, 0)
                        exps(b + 1, 0, 1)
                    if u == 0 and prep:
                        normalise(b + 1)
                    if u == 5 and late:
                        normalise_z(b - 2)

            run_slots(act, slot)

        @block.tensor
        def _(pe):
            pe.wait_ge(w_here, 16 * WEIGHT_DMAS)
            for i in range(4):
                last = pe.transpose(work[:, 0, i * F:(i + 1) * F], w_in[:, i, :], ident[:])
            last.then_inc(w_turned, 1)
            pe.wait_ge(wT_made, 1)

            def scores_of(b, s, u):
                c, k = u // 2, u % 2
                if u == 0:
                    n = 16 * 4 * heads
                    pe.wait_ge(q_stacked, nth(b, n, n))
                    pe.wait_ge(k_stacked, nth(b, n, n))
                for p in range(2):
                    if later(b) or u > 0:
                        pe.wait_ge(exp_made, nth(b, 2 * UN, 2 * u + p - 1))
                    for h in (2 * p, 2 * p + 1):
                        last = pe.matmul(scores[:, h, :], ks[:, s, h, c * P:(c + 1) * P],
                                         qs[:, s, h, k * HALF:(k + 1) * HALF], start=True, stop=True)
                    last.then_inc(qk_done, 1)

            def context(b, s, u):
                c = u // 2
                pe.wait_ge(wt_made, nth(b, 2 * UN, 2 * u + 2))
                if later(b) or u > 0:
                    pe.wait_ge(ctx_out, nth(b, UN, u))
                if u == 0 and later(b):
                    pe.wait_ge(sums_out, nth(b, 1, 0))
                for h in range(heads):
                    pe.matmul(ctx_ps[h * D:(h + 1) * D, :], vn[:, s, c, h * D:(h + 1) * D], wt[:, u % 2, h, :],
                              start=True, stop=True, tile_position=(0, h * D))
                for h in range(heads):
                    last = pe.matmul(sums[h * D:(h + 1) * D, :], hot_of(u), wt[:, u % 2, h, :], start=(u == 0),
                                     stop=(u == UN - 1), tile_position=(0, h * D))
                last.then_inc(pv_done, 1)

            def do_job(job, b):
                kind, k = job
                cols = slice(k * HALF, (k + 1) * HALF)
                i, bank = jobs.index(b, job), jobs.bank(b, job)
                dst = work[:, bank, :]
                if i >= 2 or later(b, 0):
                    pe.wait_ge(work_used[bank], jobs.half_before(b) + i // 2)
                if kind == "turn":
                    if k == 0:
                        pe.wait_ge(ln.y_made, nth(b + 1, NT, NT))
                    for t in range(4):
                        last = pe.transpose(dst[:, t * P:(t + 1) * P], ln.y[:, 4 * k + t, :], ident[:])
                elif kind == "q" or kind == "k":
                    pe.wait_ge(work_used[jobs.bank(b, ("turn", k))], jobs.uses(b, ("turn", k)))
                    last = pe.matmul(dst, wT[:, 0 if kind == "q" else 1, :], hT[:, cols], start=True, stop=True)
                elif kind == "v":
                    for t in range(4):
                        last = pe.matmul(dst[:, t * P:(t + 1) * P], hT[:, (4 * k + t) * P:(4 * k + t + 1) * P],
                                         wT[:, 2, :], start=True, stop=True)
                elif kind == "R":
                    if k == jobs.R_ORDER[0]:
                        pe.wait_ge(rec_split, nth(b - 1, 1, 1))
                    pe.matmul(dst, pick[:, k, :], rec_hi[:], start=True, stop=False)
                    last = pe.matmul(dst, pick[:, k, :], rec_lo[:], start=False, stop=True)
                else:
                    if k == 0:
                        pe.wait_ge(added, nth(b - 2, UN - 2, UN - 2))
                    tt = total[:].rearrange("p a n -> p (a n)")
                    for t in range(4):
                        last = pe.matmul(dst[:, t * P:(t + 1) * P], tt[:, (4 * k + t) * P:(4 * k + t + 1) * P],
                                         wT[:, 3, :], start=True, stop=True)
                last.then_inc(work_full, 1)

            for u in range(16):
                for j in jobs.at(-1, u):
                    do_job(j, -1)
            pe.wait_ge(hot_made, 1)
            pe.wait_ge(pick_rounded, 1)
            scores_of(0, 0, 0)

            def slot(b, s, prep, finish, late):
                attend = not isinstance(b, int) or b < B
                for u in range(UN):
                    for j in jobs.at(b, u):
                        do_job(j, b)
                    if attend and u + 1 < UN:
                        scores_of(b, s, u + 1)
                    elif attend and prep:
                        scores_of(b + 1, 1 - s, 0)
                    if attend:
                        context(b, s, u)
                    for j in jobs.tail(b, u):
                        do_job(j, b)

            run_slots(pe, slot)




def program(nc, x, adj, L0, L1, L2, L3, out):
    B, N, F = x.shape
    NT = N // P
    x1 = nc.dram_tensor("x1", (B, N, F), F32).ap()
    x2 = nc.dram_tensor("x2", (B, N, F), F32).ap()
    x3 = nc.dram_tensor("x3", (B, N, F), F32).ap()
    h0 = nc.dram_tensor("h0", (B, N, F), F32).ap()
    o2 = nc.dram_tensor("o2", (B, N, F), F32).ap()
    o2T = nc.dram_tensor("o2T", (B, F, N), F32).ap()
    bias_dram = nc.dram_tensor("edge_bias_dram", (P, NT, N), BF16).ap()
    mlp1_w, mlp1_b, mlp2_w, mlp2_b, W_fc, a_fc, W_hand, a_hand = L3
    with ExitStack() as ctx:
        ident = ctx.enter_context(nc.sbuf_tensor("ident", [P, P], F32))
        clip_high = ctx.enter_context(nc.sbuf_tensor("clip_high", [P, NT, N], F32))
        edge_bias = clip_high[:, 0:NT // 2, :].bitcast(BF16).rearrange("p a (b n) -> p (a b) n", b=2)
        masks_phase(nc, adj, clip_high, bias_dram, ident, NT, N)
        attention_phase(nc, "att", B, N, F, HEADS, clip_high, ident, *L0, x, h0, x1, bias_dram, edge_bias)
        gat_phase(nc, "gat1", B, N, F, edge_bias, ident, *L1, x1, x2, "elu")
        gat_phase(nc, "gat2", B, N, F, edge_bias, ident, *L2, x2, x3, "plain")
        fc_phase(nc, "fc", B, N, F, ident, mlp1_w, mlp1_b, W_fc, a_fc, mlp2_w, mlp2_b, x3, o2T, o2)
        gat_phase(nc, "hand", B, N, F, edge_bias, ident, W_hand, a_hand, x3, out, "hand", o2, o2T)


HEADS = 4
_L0 = ["Wq", "bq", "Wk", "bk", "Wv", "bv", "Wo", "bo", "gamma", "beta"]
_L3 = ["mlp1_w", "mlp1_b", "mlp2_w", "mlp2_b", "W_fc", "a_fc", "W_hand", "a_hand"]
_INS = (["x", "adj"] + ["L0_gnn_" + n for n in _L0] + ["L1_gnn_W", "L1_gnn_a", "L2_gnn_W", "L2_gnn_a"]
        + ["L3_gnn_" + n for n in _L3])


def kernel(**inputs):
    import numpy as np
    import concourse.bacc as bacc
    from concourse.bass_utils import run_bass_kernel_spmd

    nc = bacc.Bacc("TRN2", target_bir_lowering=False, num_devices=1)
    arrays, args = {}, {}
    for name in _INS:
        a = np.ascontiguousarray(inputs[name])
        arrays["in_" + name] = a
        args[name] = nc.dram_tensor("in_" + name, a.shape, mybir.dt.from_np(a.dtype), kind="ExternalInput").ap()
    out = nc.dram_tensor("out_x", inputs["x"].shape, F32, kind="ExternalOutput").ap()
    program(nc, args["x"], args["adj"], [args["L0_gnn_" + n] for n in _L0],
            [args["L1_gnn_W"], args["L1_gnn_a"]], [args["L2_gnn_W"], args["L2_gnn_a"]],
            [args["L3_gnn_" + n] for n in _L3], out)
    r = run_bass_kernel_spmd(nc, [arrays], core_ids=[0])
    return r.results[0]["out_x"]
```
